# Optimizing a Trainium2 kernel written in Bass

```python
import numpy as np
import jax
import jax.numpy as jnp

def _softmax(x, axis=-1):
    return jax.nn.softmax(x, axis=axis)

def _gelu(x):
    return jax.nn.gelu(x, approximate=True)

def _silu(x):
    return jax.nn.silu(x)

def _sigmoid(x):
    return jax.nn.sigmoid(x)

def _layernorm(x, axis=-1, eps=1e-05):
    m = jnp.mean(x, axis=axis, keepdims=True)
    v = jnp.var(x, axis=axis, keepdims=True)
    return (x - m) / jnp.sqrt(v + eps)

def _scatter_add(tgt, idx, src, axis=0):
    return tgt.at[idx].add(src)

def _segment_sum(src, seg, n):
    return jax.ops.segment_sum(src, seg, n)
kernel_name = 'mk_hybrid_d2_jaxref_r8_e94808'

def setup_inputs(seed: int=0):
    np.random.seed(seed)
    _w = jnp.asarray

    def _L0_attn_a_setup():
        import jax, jax.numpy as jnp
        import numpy as np
        import math
        B, S, D = (4, 256, 128)
        H, KV = (16, 4)
        HD = D // H
        GROUPS = H // KV

        def _alibi_slopes(n):
            start = 2.0 ** (-2.0 ** (-(math.log2(n) - 3)))
            return np.array([start * start ** i for i in range(n)], dtype=np.float32)
        key = jax.random.key(seed)
        ks = jax.random.split(key, 5)
        sc = 0.02
        return {'x': jax.random.normal(ks[0], (B, S, D), jnp.float32), 'Wq': jax.random.normal(ks[1], (D, H * HD), jnp.float32) * sc, 'Wk': jax.random.normal(ks[2], (D, KV * HD), jnp.float32) * sc, 'Wv': jax.random.normal(ks[3], (D, KV * HD), jnp.float32) * sc, 'Wo': jax.random.normal(ks[4], (H * HD, D), jnp.float32) * sc}
    _L0_attn_a_in = _L0_attn_a_setup()

    def _L0_attn_b_setup():
        import jax, jax.numpy as jnp
        import numpy as np
        HEADS = 16
        DIM_HEAD = 64
        SEG = 32
        SCALE = DIM_HEAD ** (-0.5)
        INNER = HEADS * DIM_HEAD

        def elu1(x):
            return jax.nn.elu(x) + 1.0

        def rope(t, pos):
            d = t.shape[-1]
            freqs = 10000.0 ** (-jnp.arange(0, d, 2, dtype=jnp.float32) / d)
            ang = pos[:, None] * freqs
            cos = jnp.repeat(jnp.cos(ang), 2, axis=-1)
            sin = jnp.repeat(jnp.sin(ang), 2, axis=-1)
            t2 = t.reshape(t.shape[:-1] + (d // 2, 2))
            rot = jnp.stack((-t2[..., 1], t2[..., 0]), axis=-1).reshape(t.shape)
            return t * cos + rot * sin

        def _reference_tuple_inner(x, w_qkv, w_out, ln_g, ln_b, mem_beta):
            B, N, D = x.shape
            mu = x.mean(-1, keepdims=True)
            var = x.var(-1, keepdims=True)
            xn = (x - mu) / jnp.sqrt(var + 1e-05) * ln_g + ln_b
            qkv = xn @ w_qkv
            q, k, v = jnp.split(qkv, 3, axis=-1)

            def to_heads(t):
                return t.reshape(B, N, HEADS, DIM_HEAD).transpose(0, 2, 1, 3)
            q, k, v = map(to_heads, (q, k, v))
            next_k, next_v = (k, v)
            pos = jnp.arange(N, dtype=jnp.float32)
            qr, kr = (rope(q, pos), rope(k, pos))
            W = N // SEG

            def to_segs(t):
                return t.reshape(B, HEADS, W, SEG, DIM_HEAD).transpose(2, 0, 1, 3, 4)
            qs, ks, vs, qnope, knope = map(to_segs, (qr, kr, v, q, k))
            mask = jnp.tril(jnp.ones((SEG, SEG), bool))
            beta = jax.nn.sigmoid(mem_beta)
            mem0 = jnp.zeros((B, HEADS, DIM_HEAD, DIM_HEAD), x.dtype)
            z0 = jnp.full((B, HEADS, DIM_HEAD), 1e-06, x.dtype)

            def step(carry, inp):
                mem, z = carry
                q_s, k_s, v_s, qn_s, kn_s = inp
                scores = jnp.einsum('bhnd,bhmd->bhnm', q_s, k_s) * SCALE
                scores = jnp.where(mask, scores, -jnp.inf)
                sdpa = jnp.einsum('bhnm,bhmd->bhnd', jax.nn.softmax(scores, axis=-1), v_s)
                sq = elu1(qn_s)
                num = jnp.einsum('bhnk,bhkv->bhnv', sq, mem)
                den = jnp.einsum('bhnk,bhk->bhn', sq, z)[..., None]
                mem_out = num / (den + 1e-06)
                out = beta * mem_out + (1.0 - beta) * sdpa
                sk = elu1(kn_s)
                prev_v = jnp.einsum('bhnk,bhkv->bhnv', sk, mem) / jnp.einsum('bhnk,bhk->bhn', sk, z)[..., None]
                mem = mem + jnp.einsum('bhnk,bhnv->bhkv', sk, v_s - prev_v)
                z = z + sk.sum(axis=2)
                return ((mem, z), out)
            _, outs = jax.lax.scan(step, (mem0, z0), (qs, ks, vs, qnope, knope))
            o = outs.transpose(1, 0, 3, 2, 4).reshape(B, N, INNER)
            out = o @ w_out
            return (out, next_k, next_v)
        key = jax.random.key(seed)
        k1, k2, k3 = jax.random.split(key, 3)
        B, N, D = (4, 512, 128)
        x = jax.random.normal(k1, (B, N, D), dtype=jnp.float32)
        w_qkv = jax.random.normal(k2, (D, 3 * INNER), dtype=jnp.float32) * 0.02
        w_out = jax.random.normal(k3, (INNER, D), dtype=jnp.float32) * 0.02
        ln_g = jnp.ones((D,), jnp.float32)
        ln_b = jnp.zeros((D,), jnp.float32)
        mem_beta = jnp.zeros((1, HEADS, 1, 1), jnp.float32)
        return {'x': x, 'w_qkv': w_qkv, 'w_out': w_out, 'ln_g': ln_g, 'ln_b': ln_b, 'mem_beta': mem_beta}
    _L0_attn_b_in = _L0_attn_b_setup()

    def _L0_ffn_setup():
        import jax, jax.numpy as jnp
        import numpy as np
        B, S, D, E, K = (4, 256, 128, 8, 2)
        H = 4 * D
        key = jax.random.key(seed)
        ks = jax.random.split(key, 4)
        sc = lambda n: 1.0 / np.sqrt(n)
        return {'x': jax.random.normal(ks[0], (B, S, D), jnp.float32), 'gate_w': jax.random.normal(ks[1], (D, E), jnp.float32) * sc(D), 'gate_b': jnp.zeros((E,), jnp.float32), 'w1': jax.random.normal(ks[2], (E, D, H), jnp.float32) * sc(D), 'b1': jnp.zeros((E, H), jnp.float32), 'w2': jax.random.normal(ks[3], (E, H, D), jnp.float32) * sc(H), 'b2': jnp.zeros((E, D), jnp.float32)}
    _L0_ffn_in = _L0_ffn_setup()

    def _L1_attn_a_setup():
        import jax, jax.numpy as jnp
        import numpy as np
        B, T, H, S = (8, 512, 128, 16)
        LN_EPS = 1e-05

        def _forward(x, W_in, b_in, B_mat, C_mat, W_B, b_B, W_D, b_D, W_out, b_out, W_ig, b_ig, W_fg, b_fg, gamma, beta):
            xp = x @ W_in + b_in
            Bx = (xp @ W_B + b_B) @ B_mat
            ig = jax.nn.sigmoid(xp @ W_ig + b_ig)
            fg = jax.nn.sigmoid(xp @ W_fg + b_fg)

            def step(h, inp):
                fg_t, ig_t, bx_t = inp
                h = fg_t * h + ig_t * bx_t
                return (h, h)
            h0 = jnp.zeros((xp.shape[0], B_mat.shape[1]), xp.dtype)
            xs = (jnp.swapaxes(fg, 0, 1), jnp.swapaxes(ig, 0, 1), jnp.swapaxes(Bx, 0, 1))
            _, hs = jax.lax.scan(step, h0, xs)
            hs = jnp.swapaxes(hs, 0, 1)
            y = jnp.tanh(hs @ C_mat + (xp @ W_D + b_D))
            y = y @ W_out + b_out + xp
            mu = jnp.mean(y, axis=-1, keepdims=True)
            var = jnp.var(y, axis=-1, keepdims=True)
            y = (y - mu) * jax.lax.rsqrt(var + LN_EPS) * gamma + beta
            return y
        key = jax.random.key(seed)
        ks = jax.random.split(key, 16)
        inv_h = 1.0 / np.sqrt(H)
        d = {'x': jax.random.normal(ks[0], (B, T, H), jnp.float32), 'W_in': jax.random.normal(ks[1], (H, H), jnp.float32) * inv_h, 'b_in': jnp.zeros((H,), jnp.float32), 'B_mat': jax.random.normal(ks[2], (H, S), jnp.float32) * 0.1, 'C_mat': jax.random.normal(ks[3], (S, H), jnp.float32) * 0.1, 'W_B': jax.random.normal(ks[4], (H, H), jnp.float32) * inv_h, 'b_B': jnp.zeros((H,), jnp.float32), 'W_D': jax.random.normal(ks[5], (H, H), jnp.float32) * inv_h, 'b_D': jnp.zeros((H,), jnp.float32), 'W_out': jax.random.normal(ks[6], (H, H), jnp.float32) * inv_h, 'b_out': jnp.zeros((H,), jnp.float32), 'W_ig': jax.random.normal(ks[7], (H, S), jnp.float32) * inv_h, 'b_ig': jnp.zeros((S,), jnp.float32), 'W_fg': jax.random.normal(ks[8], (H, S), jnp.float32) * inv_h, 'b_fg': jnp.zeros((S,), jnp.float32), 'gamma': jnp.ones((H,), jnp.float32), 'beta': jnp.zeros((H,), jnp.float32)}
        return d
    _L1_attn_a_in = _L1_attn_a_setup()

    def _L1_attn_b_setup():
        import jax, jax.numpy as jnp
        import numpy as np
        EPS = 1e-08
        LOG_INIT = -1e+38

        def wkv_log_space(w, u, k, v, ln_a_p0, ln_a_m0, ln_b0):

            def step(carry, kv):
                ln_a_p, ln_a_m, ln_b = carry
                kt, vt = kv
                ln_v_p = jnp.log(jnp.maximum(vt, 0.0) + EPS)
                ln_v_m = jnp.log(jnp.maximum(-vt, 0.0) + EPS)
                uk = u + kt
                ln_den = jnp.logaddexp(uk, ln_b)
                wkv = jnp.exp(jnp.logaddexp(uk + ln_v_p, ln_a_p) - ln_den) - jnp.exp(jnp.logaddexp(uk + ln_v_m, ln_a_m) - ln_den)
                ln_a_p = jnp.logaddexp(ln_a_p - w, kt + ln_v_p)
                ln_a_m = jnp.logaddexp(ln_a_m - w, kt + ln_v_m)
                ln_b = jnp.logaddexp(ln_b - w, kt)
                return ((ln_a_p, ln_a_m, ln_b), wkv)
            kT = jnp.swapaxes(k, 0, 1)
            vT = jnp.swapaxes(v, 0, 1)
            _, wkv = jax.lax.scan(step, (ln_a_p0, ln_a_m0, ln_b0), (kT, vT))
            return jnp.swapaxes(wkv, 0, 1)
        key = jax.random.key(seed)
        B, T, D = (4, 512, 128)
        ks = jax.random.split(key, 10)
        s = 1.0 / np.sqrt(D)
        return {'x': jax.random.normal(ks[0], (B, T, D), jnp.float32), 'time_decay': jax.random.normal(ks[1], (D,), jnp.float32) * 0.5, 'time_first': jax.random.normal(ks[2], (D,), jnp.float32) * 0.5, 'time_mix_k': jax.random.uniform(ks[3], (1, 1, D), jnp.float32), 'time_mix_v': jax.random.uniform(ks[4], (1, 1, D), jnp.float32), 'time_mix_r': jax.random.uniform(ks[5], (1, 1, D), jnp.float32), 'W_key': jax.random.normal(ks[6], (D, D), jnp.float32) * s, 'W_value': jax.random.normal(ks[7], (D, D), jnp.float32) * s, 'W_receptance': jax.random.normal(ks[8], (D, D), jnp.float32) * s, 'W_output': jax.random.normal(ks[9], (D, D), jnp.float32) * s}
    _L1_attn_b_in = _L1_attn_b_setup()

    def _L1_ffn_setup():
        import jax, jax.numpy as jnp
        import numpy as np
        DIM = 128
        HIDDEN = 384
        SCALE = 1.0 / 127.0

        def _dequant(w_int, dtype):
            return w_int.astype(dtype) * jnp.asarray(SCALE, dtype)
        key = jax.random.key(seed)
        k_x, k_g, k_u, k_d = jax.random.split(key, 4)
        x = jax.random.normal(k_x, (4, 256, DIM), dtype=jnp.float32)
        w_gate = jax.random.randint(k_g, (HIDDEN, DIM), -127, 128, dtype=jnp.int32)
        w_up = jax.random.randint(k_u, (HIDDEN, DIM), -127, 128, dtype=jnp.int32)
        w_down = jax.random.randint(k_d, (DIM, HIDDEN), -127, 128, dtype=jnp.int32)
        return {'x': x, 'w_gate': w_gate, 'w_up': w_up, 'w_down': w_down}
    _L1_ffn_in = _L1_ffn_setup()
    _d = {'L0_attn_a_x': _L0_attn_a_in['x'], 'L0_attn_a_Wq': _L0_attn_a_in['Wq'], 'L0_attn_a_Wk': _L0_attn_a_in['Wk'], 'L0_attn_a_Wv': _L0_attn_a_in['Wv'], 'L0_attn_a_Wo': _L0_attn_a_in['Wo'], 'L0_attn_b_w_qkv': _L0_attn_b_in['w_qkv'], 'L0_attn_b_w_out': _L0_attn_b_in['w_out'], 'L0_attn_b_ln_g': _L0_attn_b_in['ln_g'], 'L0_attn_b_ln_b': _L0_attn_b_in['ln_b'], 'L0_attn_b_mem_beta': _L0_attn_b_in['mem_beta'], 'L0_ffn_gate_w': _L0_ffn_in['gate_w'], 'L0_ffn_gate_b': _L0_ffn_in['gate_b'], 'L0_ffn_w1': _L0_ffn_in['w1'], 'L0_ffn_b1': _L0_ffn_in['b1'], 'L0_ffn_w2': _L0_ffn_in['w2'], 'L0_ffn_b2': _L0_ffn_in['b2'], 'L1_attn_a_W_in': _L1_attn_a_in['W_in'], 'L1_attn_a_b_in': _L1_attn_a_in['b_in'], 'L1_attn_a_B_mat': _L1_attn_a_in['B_mat'], 'L1_attn_a_C_mat': _L1_attn_a_in['C_mat'], 'L1_attn_a_W_B': _L1_attn_a_in['W_B'], 'L1_attn_a_b_B': _L1_attn_a_in['b_B'], 'L1_attn_a_W_D': _L1_attn_a_in['W_D'], 'L1_attn_a_b_D': _L1_attn_a_in['b_D'], 'L1_attn_a_W_out': _L1_attn_a_in['W_out'], 'L1_attn_a_b_out': _L1_attn_a_in['b_out'], 'L1_attn_a_W_ig': _L1_attn_a_in['W_ig'], 'L1_attn_a_b_ig': _L1_attn_a_in['b_ig'], 'L1_attn_a_W_fg': _L1_attn_a_in['W_fg'], 'L1_attn_a_b_fg': _L1_attn_a_in['b_fg'], 'L1_attn_a_gamma': _L1_attn_a_in['gamma'], 'L1_attn_a_beta': _L1_attn_a_in['beta'], 'L1_attn_b_time_decay': _L1_attn_b_in['time_decay'], 'L1_attn_b_time_first': _L1_attn_b_in['time_first'], 'L1_attn_b_time_mix_k': _L1_attn_b_in['time_mix_k'], 'L1_attn_b_time_mix_v': _L1_attn_b_in['time_mix_v'], 'L1_attn_b_time_mix_r': _L1_attn_b_in['time_mix_r'], 'L1_attn_b_W_key': _L1_attn_b_in['W_key'], 'L1_attn_b_W_value': _L1_attn_b_in['W_value'], 'L1_attn_b_W_receptance': _L1_attn_b_in['W_receptance'], 'L1_attn_b_W_output': _L1_attn_b_in['W_output'], 'L1_ffn_w_gate': _L1_ffn_in['w_gate'], 'L1_ffn_w_up': _L1_ffn_in['w_up'], 'L1_ffn_w_down': _L1_ffn_in['w_down']}
    _x0 = _d['L0_attn_a_x']
    _d['L0_attn_a_x'] = jax.random.normal(jax.random.fold_in(jax.random.key(seed), 1), (8, 512, 128), dtype=_x0.dtype)
    del _x0
    return _d

def reference(L0_attn_a_x, L0_attn_a_Wq, L0_attn_a_Wk, L0_attn_a_Wv, L0_attn_a_Wo, L0_attn_b_w_qkv, L0_attn_b_w_out, L0_attn_b_ln_g, L0_attn_b_ln_b, L0_attn_b_mem_beta, L0_ffn_gate_w, L0_ffn_gate_b, L0_ffn_w1, L0_ffn_b1, L0_ffn_w2, L0_ffn_b2, L1_attn_a_W_in, L1_attn_a_b_in, L1_attn_a_B_mat, L1_attn_a_C_mat, L1_attn_a_W_B, L1_attn_a_b_B, L1_attn_a_W_D, L1_attn_a_b_D, L1_attn_a_W_out, L1_attn_a_b_out, L1_attn_a_W_ig, L1_attn_a_b_ig, L1_attn_a_W_fg, L1_attn_a_b_fg, L1_attn_a_gamma, L1_attn_a_beta, L1_attn_b_time_decay, L1_attn_b_time_first, L1_attn_b_time_mix_k, L1_attn_b_time_mix_v, L1_attn_b_time_mix_r, L1_attn_b_W_key, L1_attn_b_W_value, L1_attn_b_W_receptance, L1_attn_b_W_output, L1_ffn_w_gate, L1_ffn_w_up, L1_ffn_w_down):

    def _L0_attn_a_ref(x, Wq, Wk, Wv, Wo):
        import jax, jax.numpy as jnp
        import numpy as np
        import math
        B, S, D = (4, 256, 128)
        H, KV = (16, 4)
        HD = D // H
        GROUPS = H // KV

        def _alibi_slopes(n):
            start = 2.0 ** (-2.0 ** (-(math.log2(n) - 3)))
            return np.array([start * start ** i for i in range(n)], dtype=np.float32)
        b, s, _ = x.shape
        scale = HD ** (-0.5)
        q = (x @ Wq).reshape(b, s, H, HD).transpose(0, 2, 1, 3)
        k = (x @ Wk).reshape(b, s, KV, HD).transpose(0, 2, 1, 3)
        v = (x @ Wv).reshape(b, s, KV, HD).transpose(0, 2, 1, 3)
        k = jnp.repeat(k, GROUPS, axis=1)
        v = jnp.repeat(v, GROUPS, axis=1)
        attn = jnp.einsum('bhqd,bhkd->bhqk', q, k) * scale
        slopes = jnp.asarray(_alibi_slopes(H))
        pos = jnp.arange(s, dtype=jnp.float32)
        rel = pos[None, :] - pos[:, None]
        attn = attn + slopes[None, :, None, None] * rel[None, None, :, :]
        attn = jax.nn.softmax(attn, axis=-1)
        out = jnp.einsum('bhqk,bhkd->bhqd', attn, v)
        out = out.transpose(0, 2, 1, 3).reshape(b, s, H * HD)
        return out @ Wo

    def _L0_attn_b_ref(x, w_qkv, w_out, ln_g, ln_b, mem_beta):
        import jax, jax.numpy as jnp
        import numpy as np
        HEADS = 16
        DIM_HEAD = 64
        SEG = 32
        SCALE = DIM_HEAD ** (-0.5)
        INNER = HEADS * DIM_HEAD

        def elu1(x):
            return jax.nn.elu(x) + 1.0

        def rope(t, pos):
            d = t.shape[-1]
            freqs = 10000.0 ** (-jnp.arange(0, d, 2, dtype=jnp.float32) / d)
            ang = pos[:, None] * freqs
            cos = jnp.repeat(jnp.cos(ang), 2, axis=-1)
            sin = jnp.repeat(jnp.sin(ang), 2, axis=-1)
            t2 = t.reshape(t.shape[:-1] + (d // 2, 2))
            rot = jnp.stack((-t2[..., 1], t2[..., 0]), axis=-1).reshape(t.shape)
            return t * cos + rot * sin

        def _reference_tuple_inner(x, w_qkv, w_out, ln_g, ln_b, mem_beta):
            B, N, D = x.shape
            mu = x.mean(-1, keepdims=True)
            var = x.var(-1, keepdims=True)
            xn = (x - mu) / jnp.sqrt(var + 1e-05) * ln_g + ln_b
            qkv = xn @ w_qkv
            q, k, v = jnp.split(qkv, 3, axis=-1)

            def to_heads(t):
                return t.reshape(B, N, HEADS, DIM_HEAD).transpose(0, 2, 1, 3)
            q, k, v = map(to_heads, (q, k, v))
            next_k, next_v = (k, v)
            pos = jnp.arange(N, dtype=jnp.float32)
            qr, kr = (rope(q, pos), rope(k, pos))
            W = N // SEG

            def to_segs(t):
                return t.reshape(B, HEADS, W, SEG, DIM_HEAD).transpose(2, 0, 1, 3, 4)
            qs, ks, vs, qnope, knope = map(to_segs, (qr, kr, v, q, k))
            mask = jnp.tril(jnp.ones((SEG, SEG), bool))
            beta = jax.nn.sigmoid(mem_beta)
            mem0 = jnp.zeros((B, HEADS, DIM_HEAD, DIM_HEAD), x.dtype)
            z0 = jnp.full((B, HEADS, DIM_HEAD), 1e-06, x.dtype)

            def step(carry, inp):
                mem, z = carry
                q_s, k_s, v_s, qn_s, kn_s = inp
                scores = jnp.einsum('bhnd,bhmd->bhnm', q_s, k_s) * SCALE
                scores = jnp.where(mask, scores, -jnp.inf)
                sdpa = jnp.einsum('bhnm,bhmd->bhnd', jax.nn.softmax(scores, axis=-1), v_s)
                sq = elu1(qn_s)
                num = jnp.einsum('bhnk,bhkv->bhnv', sq, mem)
                den = jnp.einsum('bhnk,bhk->bhn', sq, z)[..., None]
                mem_out = num / (den + 1e-06)
                out = beta * mem_out + (1.0 - beta) * sdpa
                sk = elu1(kn_s)
                prev_v = jnp.einsum('bhnk,bhkv->bhnv', sk, mem) / jnp.einsum('bhnk,bhk->bhn', sk, z)[..., None]
                mem = mem + jnp.einsum('bhnk,bhnv->bhkv', sk, v_s - prev_v)
                z = z + sk.sum(axis=2)
                return ((mem, z), out)
            _, outs = jax.lax.scan(step, (mem0, z0), (qs, ks, vs, qnope, knope))
            o = outs.transpose(1, 0, 3, 2, 4).reshape(B, N, INNER)
            out = o @ w_out
            return (out, next_k, next_v)
        return _reference_tuple_inner(x, w_qkv, w_out, ln_g, ln_b, mem_beta)[0]

    def _L0_ffn_ref(x, gate_w, gate_b, w1, b1, w2, b2):
        import jax, jax.numpy as jnp
        import numpy as np
        B, S, D, E, K = (4, 256, 128, 8, 2)
        H = 4 * D
        Bx, Sx, Dx = x.shape
        n_exp = w1.shape[0]
        logits = jnp.einsum('bsd,de->bse', x, gate_w) + gate_b
        scores = jax.nn.softmax(logits, axis=-1)
        topk_s, topk_i = jax.lax.top_k(scores, K)
        onehot = jax.nn.one_hot(topk_i, n_exp, dtype=scores.dtype)
        dispatch = jnp.einsum('bske,bsk->bse', onehot, topk_s)
        xf = x.reshape(-1, Dx)
        wf = dispatch.reshape(-1, n_exp)
        out = jnp.zeros_like(xf)
        for i in range(n_exp):
            wi = wf[:, i:i + 1]
            h = jax.nn.relu(xf * wi @ w1[i] + b1[i])
            y = h @ w2[i] + b2[i]
            out = jnp.where(wi > 0, y, out)
        return out.reshape(Bx, Sx, Dx)

    def _L1_attn_a_ref(x, W_in, b_in, B_mat, C_mat, W_B, b_B, W_D, b_D, W_out, b_out, W_ig, b_ig, W_fg, b_fg, gamma, beta):
        import jax, jax.numpy as jnp
        import numpy as np
        B, T, H, S = (8, 512, 128, 16)
        LN_EPS = 1e-05

        def _forward(x, W_in, b_in, B_mat, C_mat, W_B, b_B, W_D, b_D, W_out, b_out, W_ig, b_ig, W_fg, b_fg, gamma, beta):
            xp = x @ W_in + b_in
            Bx = (xp @ W_B + b_B) @ B_mat
            ig = jax.nn.sigmoid(xp @ W_ig + b_ig)
            fg = jax.nn.sigmoid(xp @ W_fg + b_fg)

            def step(h, inp):
                fg_t, ig_t, bx_t = inp
                h = fg_t * h + ig_t * bx_t
                return (h, h)
            h0 = jnp.zeros((xp.shape[0], B_mat.shape[1]), xp.dtype)
            xs = (jnp.swapaxes(fg, 0, 1), jnp.swapaxes(ig, 0, 1), jnp.swapaxes(Bx, 0, 1))
            _, hs = jax.lax.scan(step, h0, xs)
            hs = jnp.swapaxes(hs, 0, 1)
            y = jnp.tanh(hs @ C_mat + (xp @ W_D + b_D))
            y = y @ W_out + b_out + xp
            mu = jnp.mean(y, axis=-1, keepdims=True)
            var = jnp.var(y, axis=-1, keepdims=True)
            y = (y - mu) * jax.lax.rsqrt(var + LN_EPS) * gamma + beta
            return y
        return _forward(x, W_in, b_in, B_mat, C_mat, W_B, b_B, W_D, b_D, W_out, b_out, W_ig, b_ig, W_fg, b_fg, gamma, beta)

    def _L1_attn_b_ref(x, time_decay, time_first, time_mix_k, time_mix_v, time_mix_r, W_key, W_value, W_receptance, W_output):
        import jax, jax.numpy as jnp
        import numpy as np
        EPS = 1e-08
        LOG_INIT = -1e+38

        def wkv_log_space(w, u, k, v, ln_a_p0, ln_a_m0, ln_b0):

            def step(carry, kv):
                ln_a_p, ln_a_m, ln_b = carry
                kt, vt = kv
                ln_v_p = jnp.log(jnp.maximum(vt, 0.0) + EPS)
                ln_v_m = jnp.log(jnp.maximum(-vt, 0.0) + EPS)
                uk = u + kt
                ln_den = jnp.logaddexp(uk, ln_b)
                wkv = jnp.exp(jnp.logaddexp(uk + ln_v_p, ln_a_p) - ln_den) - jnp.exp(jnp.logaddexp(uk + ln_v_m, ln_a_m) - ln_den)
                ln_a_p = jnp.logaddexp(ln_a_p - w, kt + ln_v_p)
                ln_a_m = jnp.logaddexp(ln_a_m - w, kt + ln_v_m)
                ln_b = jnp.logaddexp(ln_b - w, kt)
                return ((ln_a_p, ln_a_m, ln_b), wkv)
            kT = jnp.swapaxes(k, 0, 1)
            vT = jnp.swapaxes(v, 0, 1)
            _, wkv = jax.lax.scan(step, (ln_a_p0, ln_a_m0, ln_b0), (kT, vT))
            return jnp.swapaxes(wkv, 0, 1)
        B, T, D = x.shape
        last_x = jnp.concatenate([jnp.zeros((B, 1, D), x.dtype), x[:, :-1, :]], axis=1)
        k = (x * time_mix_k + last_x * (1.0 - time_mix_k)) @ W_key.T
        v = (x * time_mix_v + last_x * (1.0 - time_mix_v)) @ W_value.T
        r = (x * time_mix_r + last_x * (1.0 - time_mix_r)) @ W_receptance.T
        sr = jax.nn.sigmoid(r)
        w = jnp.exp(time_decay)
        u = time_first
        init = jnp.full((B, D), LOG_INIT, x.dtype)
        wkv = wkv_log_space(w, u, k, v, init, init, init)
        return wkv * sr @ W_output.T

    def _L1_ffn_ref(x, w_gate, w_up, w_down):
        import jax, jax.numpy as jnp
        import numpy as np
        DIM = 128
        HIDDEN = 384
        SCALE = 1.0 / 127.0

        def _dequant(w_int, dtype):
            return w_int.astype(dtype) * jnp.asarray(SCALE, dtype)
        wg = _dequant(w_gate, x.dtype)
        wu = _dequant(w_up, x.dtype)
        wd = _dequant(w_down, x.dtype)
        gate = jnp.einsum('bsd,hd->bsh', x, wg)
        up = jnp.einsum('bsd,hd->bsh', x, wu)
        h = jax.nn.silu(gate) * up
        return jnp.einsum('bsh,dh->bsd', h, wd)
    x = L0_attn_a_x
    x = x + _L0_attn_a_ref(_layernorm(x, axis=-1), L0_attn_a_Wq, L0_attn_a_Wk, L0_attn_a_Wv, L0_attn_a_Wo)
    x = x + _L0_ffn_ref(_layernorm(x, axis=-1), L0_ffn_gate_w, L0_ffn_gate_b, L0_ffn_w1, L0_ffn_b1, L0_ffn_w2, L0_ffn_b2)
    x = x + _L0_attn_b_ref(_layernorm(x, axis=-1), L0_attn_b_w_qkv, L0_attn_b_w_out, L0_attn_b_ln_g, L0_attn_b_ln_b, L0_attn_b_mem_beta)
    x = x + _L0_ffn_ref(_layernorm(x, axis=-1), L0_ffn_gate_w, L0_ffn_gate_b, L0_ffn_w1, L0_ffn_b1, L0_ffn_w2, L0_ffn_b2)
    x = x + _L1_attn_a_ref(_layernorm(x, axis=-1), L1_attn_a_W_in, L1_attn_a_b_in, L1_attn_a_B_mat, L1_attn_a_C_mat, L1_attn_a_W_B, L1_attn_a_b_B, L1_attn_a_W_D, L1_attn_a_b_D, L1_attn_a_W_out, L1_attn_a_b_out, L1_attn_a_W_ig, L1_attn_a_b_ig, L1_attn_a_W_fg, L1_attn_a_b_fg, L1_attn_a_gamma, L1_attn_a_beta)
    x = x + _L1_ffn_ref(_layernorm(x, axis=-1), L1_ffn_w_gate, L1_ffn_w_up, L1_ffn_w_down)
    x = x + _L1_attn_b_ref(_layernorm(x, axis=-1), L1_attn_b_time_decay, L1_attn_b_time_first, L1_attn_b_time_mix_k, L1_attn_b_time_mix_v, L1_attn_b_time_mix_r, L1_attn_b_W_key, L1_attn_b_W_value, L1_attn_b_W_receptance, L1_attn_b_W_output)
    x = x + _L1_ffn_ref(_layernorm(x, axis=-1), L1_ffn_w_gate, L1_ffn_w_up, L1_ffn_w_down)
    return x

_drawn_inputs = setup_inputs


def setup_inputs(seed=0):
    import zlib

    import numpy as np

    out = dict(_drawn_inputs(seed))
    spreads = {'L0_attn_b_ln_g': (1.0, 0.2),
     'L0_attn_b_ln_b': (0.0, 0.1),
     'L0_attn_b_mem_beta': (0.0, 0.703),
     'L0_ffn_gate_b': (0.0, 0.1),
     'L0_ffn_b1': (0.0, 0.1),
     'L0_ffn_b2': (0.0, 0.1),
     'L1_attn_a_b_in': (0.0, 0.1),
     'L1_attn_a_b_B': (0.0, 0.292),
     'L1_attn_a_b_D': (0.0, 0.1),
     'L1_attn_a_b_out': (0.0, 0.1),
     'L1_attn_a_b_ig': (0.0, 0.8),
     'L1_attn_a_b_fg': (0.0, 0.8),
     'L1_attn_a_gamma': (1.0, 0.2),
     'L1_attn_a_beta': (0.0, 0.1)}
    factors = {'L0_attn_a_Wq': 5.738,
     'L0_attn_a_Wk': 4.3,
     'L1_attn_b_time_decay': 8.0,
     'L1_attn_b_time_first': 8.0,
     'L1_attn_b_time_mix_k': 8.0,
     'L1_attn_b_time_mix_v': 8.0,
     'L1_attn_b_time_mix_r': 8.0,
     'L1_attn_b_W_key': 8.0,
     'L1_attn_b_W_value': 8.0,
     'L1_attn_b_W_receptance': 8.0,
     'L1_attn_b_W_output': 8.0}
    for name, (base, spread) in spreads.items():
        noise = np.random.default_rng([zlib.crc32(name.encode()), seed]).standard_normal(out[name].shape)
        drawn = base * np.exp(spread * noise) if base else spread * noise
        out[name] = jnp.asarray(drawn.astype(out[name].dtype))
    for name, factor in factors.items():
        out[name] = (out[name] * factor).astype(out[name].dtype)
    return out
```

```python
from contextlib import ExitStack
import math

import numpy as np

import concourse.bass as bass
from concourse import mybir

P = 128
B, T = 8, 512
N = B * T
F32, BF16 = mybir.dt.float32, mybir.dt.bfloat16
I32 = mybir.dt.int32
ALU, ACT, AX = mybir.AluOpType, mybir.ActivationFunctionType, mybir.AxisListType

HID = 384
HC = HID // P
FREE = 2
ONE = 1


def start_counters(nc, counters):
    with nc.Block() as block:
        @block.sync
        def _(sp):
            for counter in counters:
                sp.sem_inc(counter, ONE)


def batch(b):
    return bass.ds(b * T, T) if not isinstance(b, int) else slice(b * T, b * T + T)



def norm_pe(pe, s, done, again=False):
    src = s.xn if again else s.x
    with pe.Fori(0, B // 2) as pair:
        b = pair * 2
        for u in range(2):
            pe.wait_ge(s.centered, ONE + b + done)
            if again:
                pe.wait_ge(s.normed, ONE + b + (done - B + u + 1))
            pe.matmul(s.bank(u), s.avg[:, :], src[:, batch(b + u)], start=True, stop=True).then_inc(s.mean_ready, 1)
        for u in range(2):
            pe.wait_ge(s.squared, ONE + b + (done + u + 1))
            pe.wait_ge(s.logged, ONE + b + done)
            pe.matmul(s.bank(2 + u), s.avg[:, :], s.sq[:, u, :], start=True, stop=True).then_inc(s.var_ready, 1)


def norm_act(act, s, done):
    if done:
        act.wait_ge(s.warmed, ONE + done // B * 2)
    act.activation(s.scrap[:, 0:1], s.eps[:, 0:1], ACT.Ln).then_inc(s.warmed, 1)
    with act.Fori(0, B // 2) as pair:
        b = pair * 2
        for u in range(2):
            act.wait_ge(s.centered, ONE + b + (done + u + 1))
            act.wait_ge(s.var_ready, ONE + b + done)
            act.activation(s.sq[:, u, :], s.xn[:, batch(b + u)], ACT.Square).then_inc(s.squared, 1)
        for u in range(2):
            act.wait_ge(s.var_ready, ONE + b + (done + u + 1))
            act.activation(s.rs[:, batch(b + u)], s.bank(2 + u), ACT.Ln, bias=s.eps[:, 0:1]).then_inc(s.logged, 1)
    act.wait_ge(s.warmed, ONE + done // B * 2 + 1)
    act.activation(s.scrap[:, 0:1], s.eps[:, 0:1], ACT.Exp).then_inc(s.warmed, 1)
    act.wait_ge(s.logged, ONE + done + B)
    with act.Fori(0, B) as b:
        act.activation(s.rs[:, batch(b)], s.rs[:, batch(b)], ACT.Exp, scale=-0.5).then_inc(s.rstd_ready, 1)


def norm_dve(dve, s, done, again=False):
    src = s.xn if again else s.x
    with dve.Fori(0, B // 2) as pair:
        b = pair * 2
        for u in range(2):
            dve.wait_ge(s.mean_ready, ONE + b + (done + u + 1))
            dve.tensor_tensor(s.xn[:, batch(b + u)], src[:, batch(b + u)], s.bank(u), ALU.subtract).then_inc(s.centered, 1)
    dve.wait_ge(s.centered, ONE + done + B)
    with dve.Fori(0, B) as b:
        dve.wait_ge(s.rstd_ready, ONE + b + (done + 1))
        dve.tensor_tensor(s.xn[:, batch(b)], s.xn[:, batch(b)], s.rs[:, batch(b)], ALU.mult).then_inc(s.normed, 1)



def swiglu_layer(nc, s, ctx, done, tag):
    counters = []

    def sem(name):
        counters.append(nc.alloc_semaphore(name=f"{tag}_{name}"))
        return counters[-1]

    gate_ready, up_ready = sem("gate_ready"), sem("up_ready")
    silu_ready, h_ready = sem("silu_ready"), sem("h_ready")
    down_ready, x_added = sem("down_ready"), sem("x_added")
    sg = s.work[:, 0:2 * T].rearrange("p (n t) -> p n t", n=2)
    h = s.work[:, 2 * T:(2 + 2 * HC) * T].rearrange("p (n t) -> p n t", n=2 * HC)
    start_counters(nc, counters + FREE * [h_ready])
    block = ctx.enter_context(nc.Block())

    @block.tensor
    def _(pe):
        norm_pe(pe, s, done)
        with pe.Fori(0, B // 2) as pair:
            b = pair * 2
            for u in range(2):
                pe.wait_ge(s.normed, ONE + b + (done + u + 1))
                for c in range(HC):
                    k = HC * u + c
                    pe.wait_ge(h_ready, ONE + b * HC + (k + 1))
                    pe.matmul(s.bank(k % 2), s.wgate[:, P * c:P * c + P], s.xn[:, batch(b + u)],
                              start=True, stop=True).then_inc(gate_ready, 1)
                    pe.matmul(s.bank(2 + k % 2), s.wup[:, P * c:P * c + P], s.xn[:, batch(b + u)],
                              start=True, stop=True).then_inc(up_ready, 1)
            for u in range(2):
                pe.wait_ge(x_added, ONE + b)
                for c in range(HC):
                    pe.wait_ge(h_ready, ONE + b * HC + (HC * u + c + 1 + FREE))
                    mm = pe.matmul(s.bank(4 + u), s.wdown[:, P * c:P * c + P], h[:, HC * u + c, :],
                                   start=c == 0, stop=c == HC - 1)
                mm.then_inc(down_ready, 1)

    @block.scalar
    def _(act):
        norm_act(act, s, done)
        with act.Fori(0, B // 2) as pair:
            b = pair * 2
            for k in range(2 * HC):
                act.wait_ge(gate_ready, ONE + b * HC + (k + 1))
                act.wait_ge(h_ready, ONE + b * HC + (k + 1))
                act.activation(sg[:, k % 2, :], s.bank(k % 2), ACT.Silu).then_inc(silu_ready, 1)

    @block.vector
    def _(dve):
        norm_dve(dve, s, done)
        with dve.Fori(0, B // 2) as pair:
            b = pair * 2
            dve.wait_ge(down_ready, ONE + b)
            for k in range(2 * HC):
                dve.wait_ge(silu_ready, ONE + b * HC + (k + 1))
                dve.wait_ge(up_ready, ONE + b * HC + (k + 1))
                dve.tensor_tensor(h[:, k, :], s.bank(2 + k % 2), sg[:, k % 2, :], ALU.mult).then_inc(h_ready, 1)
            for u in range(2):
                dve.wait_ge(down_ready, ONE + b + (u + 1))
                dve.tensor_tensor(s.x[:, batch(b + u)], s.x[:, batch(b + u)], s.bank(4 + u), ALU.add).then_inc(x_added, 1)
        dve.wait_ge(x_added, ONE + B)
    return counters



def ssm_layer(nc, s, ctx, done, tag):
    counters = []

    def sem(name):
        counters.append(nc.alloc_semaphore(name=f"{tag}_{name}"))
        return counters[-1]

    xp_ready, t_ready, gates_ready, tb_ready = sem("xp_ready"), sem("t_ready"), sem("gates_ready"), sem("tb_ready")
    xp_mm, bx_ready, gated, drive_ready = sem("xp_mm"), sem("bx_ready"), sem("gated"), sem("drive_ready")
    states_ready, pre_ready, tanh_ready, y_ready = sem("states"), sem("pre_ready"), sem("tanh_ready"), sem("y_ready")
    res_ready, mean_ready, centered, squared = sem("res_ready"), sem("mean_ready"), sem("centered"), sem("squared")
    var_ready, var_kept, ln_done, rstd, scaled, x_added = (
        sem("var_ready"), sem("var_kept"), sem("ln_done"), sem("rstd"), sem("scaled"), sem("x_added"))
    zeroed = sem("zeroed")
    S = s.W_ig.shape[1]
    w = s.work
    xp = w[:, 0:2 * T].rearrange("p (u t) -> p u t", u=2)
    tb = w[:, 2 * T:4 * T].rearrange("p (u t) -> p u t", u=2)
    hs = w[:, 4 * T:6 * T].rearrange("p (u t) -> p u t", u=2)
    y = w[:, 6 * T:8 * T].rearrange("p (u t) -> p u t", u=2)
    ig = w[0:S, 8 * T:10 * T].rearrange("p (u t) -> p u t", u=2)
    fg = w[0:S, 10 * T:12 * T].rearrange("p (u t) -> p u t", u=2)
    drive = w[0:S, 12 * T:14 * T].rearrange("p (u t) -> p u t", u=2)
    bank = lambda u, i: s.bank(4 * u + i)
    start_counters(nc, counters)
    block = ctx.enter_context(nc.Block())

    @block.tensor
    def _(pe):
        norm_pe(pe, s, done)
        pe.wait_ge(zeroed, ONE + 1)
        with pe.Fori(0, B // 2) as pair:
            b = pair * 2
            for u in range(2):
                pe.wait_ge(s.normed, ONE + b + (done + u + 1))
                pe.wait_ge(gated, ONE + b * 2)
                pe.matmul(bank(u, 0), s.W_in, s.xn[:, batch(b + u)], start=True, stop=True).then_inc(xp_mm, 1)
            for u in range(2):
                pe.wait_ge(xp_ready, ONE + b + (u + 1))
                pe.wait_ge(drive_ready, ONE + b)
                pe.matmul(bank(u, 1), s.W_B, xp[:, u, :], start=True, stop=True).then_inc(t_ready, 1)
                pe.wait_ge(centered, ONE + b)
                pe.matmul(bank(u, 2)[0:S, :], s.W_ig, xp[:, u, :], start=True, stop=True)
                pe.matmul(bank(u, 0)[0:S, :], s.W_fg, xp[:, u, :], start=True, stop=True).then_inc(gates_ready, 1)
                pe.wait_ge(var_kept, ONE + b)
                pe.matmul(bank(u, 3), s.W_D, xp[:, u, :], start=True, stop=False)
            for u in range(2):
                pe.wait_ge(tb_ready, ONE + b + (u + 1))
                pe.matmul(bank(u, 1)[0:S, :], s.B_mat, tb[:, u, :], start=True, stop=True).then_inc(bx_ready, 1)
            for u in range(2):
                pe.wait_ge(states_ready, ONE + b + (u + 1))
                pe.matmul(bank(u, 3), s.C_mat, hs[:, u, :], start=False, stop=True).then_inc(pre_ready, 1)
            for u in range(2):
                pe.wait_ge(tanh_ready, ONE + b + (u + 1))
                pe.matmul(bank(u, 3), s.W_out, y[:, u, :], start=True, stop=True).then_inc(y_ready, 1)
            for u in range(2):
                pe.wait_ge(res_ready, ONE + b + (u + 1))
                pe.wait_ge(gated, ONE + b * 2 + (2 * u + 2))
                pe.matmul(bank(u, 2), s.avg, s.xn[:, batch(b + u)], start=True, stop=True).then_inc(mean_ready, 1)
            for u in range(2):
                pe.wait_ge(squared, ONE + b + (u + 1))
                pe.matmul(bank(u, 3), s.avg, s.sq[:, u, :], start=True, stop=True).then_inc(var_ready, 1)

    @block.scalar
    def _(act):
        norm_act(act, s, done)
        with act.Fori(0, B // 2) as pair:
            b = pair * 2
            for u in range(2):
                act.wait_ge(xp_mm, ONE + b + (u + 1))
                act.wait_ge(res_ready, ONE + b)
                act.activation(xp[:, u, :], bank(u, 0), ACT.Identity, bias=s.b_in).then_inc(xp_ready, 1)
            for u in range(2):
                act.wait_ge(t_ready, ONE + b + (u + 1))
                act.wait_ge(bx_ready, ONE + b)
                act.activation(tb[:, u, :], bank(u, 1), ACT.Identity, bias=s.b_B).then_inc(tb_ready, 1)
            for u in range(2):
                act.wait_ge(gates_ready, ONE + b + (u + 1))
                act.wait_ge(states_ready, ONE + b)
                act.activation(ig[:, u, :], bank(u, 2)[0:S, :], ACT.Sigmoid, bias=s.b_ig).then_inc(gated, 1)
                act.activation(fg[:, u, :], bank(u, 0)[0:S, :], ACT.Sigmoid, bias=s.b_fg).then_inc(gated, 1)
            for u in range(2):
                act.wait_ge(pre_ready, ONE + b + (u + 1))
                act.wait_ge(y_ready, ONE + b)
                act.activation(y[:, u, :], bank(u, 3), ACT.Tanh, bias=s.b_D).then_inc(tanh_ready, 1)
            for u in range(2):
                act.wait_ge(centered, ONE + b + (u + 1))
                act.wait_ge(var_ready, ONE + b)
                act.activation(s.sq[:, u, :], s.xn[:, batch(b + u)], ACT.Square).then_inc(squared, 1)
            for u in range(2):
                act.wait_ge(var_ready, ONE + b + (u + 1))
                act.wait_ge(s.normed, ONE + b + (done + u + 1))
                act.activation(s.rs[:, batch(b + u)], bank(u, 3), ACT.Identity).then_inc(var_kept, 1)
        act.wait_ge(var_kept, ONE + B)
        act.activation(s.rs[:, :], s.rs[:, :], ACT.Ln, bias=s.eps[:, 0:1]).then_inc(ln_done, 1)
        act.wait_ge(ln_done, ONE + 1)
        for b in range(B):
            act.activation(s.rs[:, batch(b)], s.rs[:, batch(b)], ACT.Exp, scale=-0.5).then_inc(rstd, 1)

    @block.vector
    def _(dve):
        dve.memset(hs, 0.0).then_inc(zeroed, 1)
        norm_dve(dve, s, done)
        with dve.Fori(0, B // 2) as pair:
            b = pair * 2
            for u in range(2):
                dve.wait_ge(bx_ready, ONE + b + (u + 1))
                dve.wait_ge(gated, ONE + b * 2 + (2 * u + 2))
                dve.wait_ge(states_ready, ONE + b + u)
                dve.tensor_tensor(drive[:, u, :], bank(u, 1)[0:S, :], ig[:, u, :], ALU.mult).then_inc(drive_ready, 1)
                dve.wait_ge(drive_ready, ONE + b + (u + 1))
                dve.wait_ge(pre_ready, ONE + b)
                dve.tensor_tensor_scan(hs[0:S, u, :], fg[:, u, :], drive[:, u, :], 0.0, ALU.mult, ALU.add).then_inc(states_ready, 1)
            for u in range(2):
                dve.wait_ge(y_ready, ONE + b + (u + 1))
                dve.scalar_tensor_tensor(s.xn[:, batch(b + u)], bank(u, 3), s.b_out, xp[:, u, :], ALU.add, ALU.add).then_inc(res_ready, 1)
            for u in range(2):
                dve.wait_ge(mean_ready, ONE + b + (u + 1))
                dve.wait_ge(res_ready, ONE + b + (u + 1))
                dve.tensor_tensor(s.xn[:, batch(b + u)], s.xn[:, batch(b + u)], bank(u, 2), ALU.subtract).then_inc(centered, 1)
        for b in range(B):
            dve.wait_ge(rstd, ONE + b + 1)
            dve.wait_ge(centered, ONE + b + 1)
            dve.scalar_tensor_tensor(s.xn[:, batch(b)], s.xn[:, batch(b)], s.gamma, s.rs[:, batch(b)], ALU.mult, ALU.mult).then_inc(scaled, 1)
            dve.wait_ge(scaled, ONE + b + 1)
            dve.scalar_tensor_tensor(s.x[:, batch(b)], s.xn[:, batch(b)], s.beta, s.x[:, batch(b)], ALU.add, ALU.add).then_inc(x_added, 1)
        dve.wait_ge(x_added, ONE + B)
    return counters



def rwkv_layer(nc, s, ctx, done, tag):
    counters = []

    def sem(name):
        counters.append(nc.alloc_semaphore(name=f"{tag}_{name}"))
        return counters[-1]

    NEG = -1e38
    shifted, delta_ready, mixed, krv_ready = sem("shifted"), sem("delta"), sem("mixed"), sem("krv_ready")
    max_ready, peak_ready, exponents, exps = sem("max_ready"), sem("peak_ready"), sem("exponents"), sem("exps")
    kv_ready, sums_ready, r_ready = sem("kv_ready"), sem("sums_ready"), sem("r_ready")
    parts, num_ready, den_ready, gated = sem("parts"), sem("num_ready"), sem("den_ready"), sem("gated")
    consts, den_log, inv_ready, wkv_ready, out_ready, x_added = (
        sem("consts"), sem("den_log"), sem("inv_ready"), sem("wkv_ready"), sem("out_ready"), sem("x_added"))
    at = [0]

    def buf(n):
        a = at[0]
        at[0] += n
        return s.work[:, a:a + n]

    def two(n):
        return buf(2 * n).rearrange("p (u t) -> p u t", u=2)

    last, delta = two(T), two(T)
    xk, xv, xr = two(T), two(T), two(T)
    m, A, Z = two(T + 1), two(T + 1), two(T + 1)
    E = buf(2 * 4 * T).rearrange("p (u n t) -> p u n t", u=2, n=4)
    kv, peak, th = two(T), two(T), two(T)
    negw_row = buf(T)
    c = buf(2)
    neg_w, w_pos = c[:, 0:1], c[:, 1:2]
    bank = lambda u, i: s.bank(4 * u + i)
    start_counters(nc, counters)
    block = ctx.enter_context(nc.Block())

    @block.tensor
    def _(pe):
        norm_pe(pe, s, done)
        with pe.Fori(0, B // 2) as pair:
            b = pair * 2
            for u in range(2):
                pe.wait_ge(mixed, ONE + b * 3 + (3 * u + 3))
                pe.wait_ge(num_ready, ONE + b)
                pe.matmul(bank(u, 0), s.W_key, xk[:, u, :], start=True, stop=True)
                pe.matmul(bank(u, 1), s.W_value, xv[:, u, :], start=True, stop=True)
                pe.matmul(bank(u, 2), s.W_receptance, xr[:, u, :], start=True, stop=True).then_inc(krv_ready, 1)
        with pe.Fori(0, B // 2) as pair:
            b = pair * 2
            for u in range(2):
                pe.wait_ge(wkv_ready, ONE + b + (u + 1))
                pe.wait_ge(x_added, ONE + b)
                pe.matmul(bank(u, 3), s.W_output, s.xn[:, batch(b + u)], start=True, stop=True).then_inc(out_ready, 1)

    @block.scalar
    def _(act):
        norm_act(act, s, done)
        act.activation(w_pos, s.time_decay, ACT.Exp).then_inc(consts, 1)
        with act.Fori(0, B // 2) as pair:
            b = pair * 2
            for u in range(2):
                act.wait_ge(s.normed, ONE + b + (done + u + 1))
                act.wait_ge(mixed, ONE + b * 3)
                act.wait_ge(consts, ONE + 3)
                act.activation(last[:, u, 1:T], s.xn[:, bass.ds((b + u) * T, T - 1)], ACT.Copy).then_inc(shifted, 1)
            for u in range(2):
                act.wait_ge(exponents, ONE + b * 4 + (4 * u + 4))
                act.activation(E[:, u, :, :], E[:, u, :, :], ACT.Exp).then_inc(exps, 1)
            for u in range(2):
                act.wait_ge(krv_ready, ONE + b + (u + 1))
                act.wait_ge(num_ready, ONE + b)
                act.activation(th[:, u, :], bank(u, 2), ACT.Tanh, scale=0.5).then_inc(r_ready, 1)
        act.wait_ge(den_ready, ONE + B)
        act.activation(s.rs[:, :], s.rs[:, :], ACT.Ln).then_inc(den_log, 1)
        act.wait_ge(den_log, ONE + 1)
        for b in range(B):
            act.activation(s.rs[:, batch(b)], s.rs[:, batch(b)], ACT.Exp, scale=-1.0).then_inc(inv_ready, 1)

    @block.vector
    def _(dve):
        dve.memset(last[:, :, 0:1], 0.0)
        dve.memset(A[:, :, 0:1], 0.0)
        dve.memset(Z[:, :, 0:1], 0.0)
        dve.memset(m[:, :, 0:1], NEG).then_inc(consts, 1)
        dve.memset(negw_row, 0.0).then_inc(consts, 1)
        norm_dve(dve, s, done)
        dve.wait_ge(consts, ONE + 3)
        dve.tensor_scalar(negw_row, negw_row, w_pos, None, ALU.subtract).then_inc(consts, 1)
        dve.tensor_scalar(neg_w, w_pos, -1.0, None, ALU.mult).then_inc(consts, 1)
        with dve.Fori(0, B // 2) as pair:
            b = pair * 2
            for u in range(2):
                xb = s.xn[:, batch(b + u)]
                dve.wait_ge(shifted, ONE + b + (u + 1))
                dve.wait_ge(mixed, ONE + b * 3)
                dve.tensor_tensor(delta[:, u, :], xb, last[:, u, :], ALU.subtract).then_inc(delta_ready, 1)
                dve.wait_ge(delta_ready, ONE + b + (u + 1))
                dve.wait_ge(krv_ready, ONE + b)
                for out, mix in ((xk, s.mix_k), (xv, s.mix_v), (xr, s.mix_r)):
                    dve.scalar_tensor_tensor(out[:, u, :], delta[:, u, :], mix, last[:, u, :], ALU.mult, ALU.add).then_inc(mixed, 1)
            for u in range(2):
                k, before, now = bank(u, 0), m[:, u, 0:T], m[:, u, 1:T + 1]
                dve.wait_ge(consts, ONE + 5)
                dve.wait_ge(krv_ready, ONE + b + (u + 1))
                dve.wait_ge(num_ready, ONE + b)
                dve.tensor_tensor_scan(now, negw_row, k, NEG, ALU.add, ALU.max).then_inc(max_ready, 1)
                dve.wait_ge(max_ready, ONE + b + (u + 1))
                dve.scalar_tensor_tensor(peak[:, u, :], k, s.time_first, before, ALU.add, ALU.max).then_inc(peak_ready, 1)
                dve.tensor_tensor(E[:, u, 0, :], k, now, ALU.subtract).then_inc(exponents, 1)
                dve.scalar_tensor_tensor(E[:, u, 1, :], before, neg_w, now, ALU.add, ALU.subtract).then_inc(exponents, 1)
                dve.wait_ge(peak_ready, ONE + b + (u + 1))
                dve.scalar_tensor_tensor(E[:, u, 2, :], k, s.time_first, peak[:, u, :], ALU.add, ALU.subtract).then_inc(exponents, 1)
                dve.tensor_tensor(E[:, u, 3, :], before, peak[:, u, :], ALU.subtract).then_inc(exponents, 1)
            for u in range(2):
                v = bank(u, 1)
                ek, decay, own, past = (E[:, u, n, :] for n in range(4))
                dve.wait_ge(exps, ONE + b + (u + 1))
                dve.tensor_tensor(kv[:, u, :], ek, v, ALU.mult).then_inc(kv_ready, 1)
                dve.tensor_tensor_scan(Z[:, u, 1:T + 1], decay, ek, 0.0, ALU.mult, ALU.add).then_inc(sums_ready, 1)
                dve.wait_ge(kv_ready, ONE + b + (u + 1))
                dve.tensor_tensor_scan(A[:, u, 1:T + 1], decay, kv[:, u, :], 0.0, ALU.mult, ALU.add).then_inc(sums_ready, 1)
                dve.wait_ge(sums_ready, ONE + b * 2 + (2 * u + 2))
                dve.tensor_tensor(kv[:, u, :], past, Z[:, u, 0:T], ALU.mult).then_inc(parts, 1)
                dve.tensor_tensor(peak[:, u, :], past, A[:, u, 0:T], ALU.mult).then_inc(parts, 1)
                dve.tensor_tensor(ek, own, v, ALU.mult).then_inc(parts, 1)
                dve.wait_ge(parts, ONE + b * 4 + (4 * u + 1))
                dve.tensor_tensor(s.rs[:, batch(b + u)], own, kv[:, u, :], ALU.add).then_inc(den_ready, 1)
                dve.wait_ge(parts, ONE + b * 4 + (4 * u + 3))
                dve.tensor_tensor(peak[:, u, :], peak[:, u, :], ek, ALU.add).then_inc(parts, 1)
                dve.wait_ge(r_ready, ONE + b + (u + 1))
                dve.wait_ge(parts, ONE + b * 4 + (4 * u + 4))
                dve.wait_ge(mixed, ONE + b * 3 + (3 * u + 3))
                dve.scalar_tensor_tensor(s.xn[:, batch(b + u)], th[:, u, :], 1.0, peak[:, u, :], ALU.add, ALU.mult).then_inc(num_ready, 1)
        dve.wait_ge(num_ready, ONE + B)
        for b in range(B):
            dve.wait_ge(inv_ready, ONE + b + 1)
            dve.scalar_tensor_tensor(s.xn[:, batch(b)], s.xn[:, batch(b)], 0.5, s.rs[:, batch(b)], ALU.mult, ALU.mult).then_inc(wkv_ready, 1)
        for b in range(B):
            dve.wait_ge(out_ready, ONE + b + 1)
            dve.tensor_tensor(s.x[:, batch(b)], s.x[:, batch(b)], bank(b % 2, 3), ALU.add).then_inc(x_added, 1)
        dve.wait_ge(x_added, ONE + B)
    return counters



HEADS, KV, HD = 16, 4, 8
QUAD = HEADS // KV
TILES = T // P
SLOTS = [(i, j) for i in range(3) for j in range(3)]
BIAS_ROW = len(SLOTS) * HD
MAX_ROW = 96


def gqa_layer(nc, s, ctx, done, tag):
    counters = []

    def sem(name):
        counters.append(nc.alloc_semaphore(name=f"{tag}_{name}"))
        return counters[-1]

    misc_ready, misc_read = sem("misc_ready"), sem("misc_read")
    tables = sem("tables")
    split = sem("split")
    scores_ready, scores_read = sem("scores_ready"), sem("scores_read")
    cut, max_cut = sem("cut"), sem("max_cut")
    keyed_ready, exp_ready, pv_ready = sem("keyed_ready"), sem("exp_ready"), sem("pv_ready")
    raw_ready, inv_ready, xv_ready = sem("raw_ready"), sem("inv_ready"), sem("xv_ready")
    zeroed = sem("zeroed")

    at = [0]

    def f32(n):
        a = at[0]
        at[0] += n
        return s.work[:, a:a + n]

    def bf16(n):
        return f32(n // 2).bitcast(BF16)

    sel = bf16(GQA_BF16_COLS)
    sel_q = sel[:, 0:HEADS * 3 * P].rearrange("p (h i r) -> p h i r", h=HEADS, i=3)
    sel_k = sel[:, HEADS * 3 * P:(HEADS + KV) * 3 * P].rearrange("p (h i r) -> p h i r", h=KV, i=3)
    ident_b = sel[:, (HEADS + KV) * 3 * P:(HEADS + KV) * 3 * P + P]
    parts = bf16(6 * T).rearrange("p (a i t) -> p a i t", a=2, i=3)
    rest = f32(2 * T).rearrange("p (a t) -> p a t", a=2)
    qop = bf16(HEADS * T).rearrange("p (q i t) -> p q i t", q=KV, i=QUAD)
    kop = bf16(KV * T).rearrange("p (g t) -> p g t", g=KV)
    vaug = f32(TILES * KV * 32).rearrange("p (n g c) -> p n g c", n=TILES, g=KV)
    mx = f32(2 * 16).rearrange("p (a n) -> p a n", a=2)
    mrest = f32(2 * 16).rearrange("p (a n) -> p a n", a=2)
    mrow = bf16(2 * 16 * 32).rearrange("p (a n c) -> p a n c", a=2, n=16)
    E = f32(2 * QUAD * T).rearrange("p (a i t) -> p a i t", a=2, i=QUAD)
    raw = f32(T)
    inv = f32(16)
    on = f32(T).rearrange("p (n h d) -> p n h d", n=TILES, h=HEADS)
    oT = f32(T)
    xv = oT
    assert at[0] <= s.work.shape[1]
    misc, pv = s.bank(7), s.bank(6)

    uses = (["q", "k", "v"] + [("ksel", g) for g in range(KV)] + [("qsel", 0, i) for i in range(QUAD)]
            + [("qsel", 1, i) for i in range(QUAD)])
    for q in range(KV):
        uses += [("qsel", q + 2, i) for i in range(QUAD) if q + 2 < KV] + [("turn", q)]
    uses += ["back", "out"]
    use = {name: n for n, name in enumerate(uses)}
    U = len(uses)
    RING = 16 + QUAD
    SPLITS = 6
    start_counters(nc, counters)
    block = ctx.enter_context(nc.Block())

    @block.sync
    def _(sp):
        sp.dma_start(sel, s.gqa_tables).then_inc(tables, 16)
        sp.wait_ge(tables, ONE + 16)

    @block.tensor
    def _(pe):
        norm_pe(pe, s, done)
        pe.wait_ge(tables, ONE + 16)
        pe.wait_ge(zeroed, ONE + 3)
        with pe.Fori(0, B) as b:
            def misc_free(name):
                pe.wait_ge(misc_read, ONE + b * U + use[name])

            def qsel(q, i):
                misc_free(("qsel", q, i))
                pe.wait_ge(split, ONE + b * SPLITS + SPLITS)
                for n in range(3):
                    mm = pe.matmul(misc, sel_q[:, q * QUAD + i, n, :], parts[:, 0, n, :], start=n == 0, stop=n == 2)
                mm.then_inc(misc_ready, 1)

            def scores(q, n):
                r = q * RING + n
                i, qt = n // TILES, n % TILES
                if qt == 0:
                    pe.wait_ge(misc_read, ONE + b * U + (use[("qsel", q, i)] + 1))
                if r >= 2:
                    pe.wait_ge(scores_read, ONE + b * (KV * RING) + (r - 1))
                else:
                    pe.wait_ge(scores_read, ONE + b * (KV * RING))
                pe.matmul(s.bank(r % 2), qop[:, q, i, qt * P:(qt + 1) * P], kop[:, q, :],
                          start=True, stop=True).then_inc(scores_ready, 1)

            def max_rows(q):
                pe.wait_ge(max_cut, ONE + b * KV + (q + 1))
                for i in range(QUAD):
                    r = q * RING + 16 + i
                    pe.wait_ge(scores_read, ONE + b * (KV * RING) + (r - 1))
                    for qt in range(TILES):
                        mm = pe.matmul(s.bank(r % 2)[MAX_ROW:P, qt * P:(qt + 1) * P], mrow[:, q % 2, 4 * i + qt, :],
                                       ident_b, start=True, stop=True)
                    mm.then_inc(scores_ready, 1)

            def keyed(q, kt, half):
                g = q * 8 + kt * 2 + half
                pe.wait_ge(scores_read, ONE + b * (KV * RING) + (q * RING + 16 + 2 * half + 2))
                if g >= 2:
                    pe.wait_ge(exp_ready, ONE + b * 32 + (g - 1))
                else:
                    pe.wait_ge(exp_ready, ONE + b * 32)
                for j in range(2):
                    mm = pe.matmul(s.bank(2 + 2 * half + j), kop[:, q, kt * P:(kt + 1) * P],
                                   qop[:, q, 2 * half + j, :], start=True, stop=True)
                mm.then_inc(keyed_ready, 1)

            def values(q, kt):
                pe.wait_ge(exp_ready, ONE + b * 32 + (q * 8 + kt * 2 + 2))
                if kt == 0:
                    pe.wait_ge(raw_ready, ONE + b * KV + q)
                for i in range(QUAD):
                    mm = pe.matmul(pv[32 * i:32 * i + 32, :], vaug[:, kt, q, :], E[:, kt % 2, i, :],
                                   start=kt == 0, stop=kt == TILES - 1)
                mm.then_inc(pv_ready, 1)

            pe.wait_ge(s.normed, ONE + b + (done + 1))
            misc_free("q")
            pe.matmul(misc, s.Wq, s.xn[:, batch(b)], start=True, stop=True).then_inc(misc_ready, 1)
            misc_free("k")
            pe.matmul(misc, s.Wk, s.xn[:, batch(b)], start=True, stop=True).then_inc(misc_ready, 1)
            misc_free("v")
            pe.wait_ge(xv_ready, ONE + b + 1)
            for n in range(TILES):
                mm = pe.matmul(misc[:, 32 * n:32 * n + 32], xv[:, n * P:(n + 1) * P], s.Wv, start=True, stop=True)
            mm.then_inc(misc_ready, 1)
            for g in range(KV):
                misc_free(("ksel", g))
                pe.wait_ge(split, ONE + b * SPLITS + SPLITS)
                for n in range(3):
                    mm = pe.matmul(misc, sel_k[:, g, n, :], parts[:, 1, n, :], start=n == 0, stop=n == 2)
                mm.then_inc(misc_ready, 1)
            for i in range(QUAD):
                qsel(0, i)
            pe.wait_ge(misc_read, ONE + b * U + use[("qsel", 0, 0)])
            for n in range(16):
                scores(0, n)
            for i in range(QUAD):
                qsel(1, i)
            max_rows(0)
            for q in range(KV):
                for n in range(16):
                    if q + 1 < KV:
                        scores(q + 1, n)
                    if n % 2 == 0:
                        keyed(q, n // 4, n // 2 % 2)
                    if n % 4 == 2 and q + 2 < KV:
                        qsel(q + 2, n // 4)
                    if n % 4 == 3 and n > 4:
                        values(q, n // 4 - 1)
                values(q, TILES - 1)
                if q + 1 < KV:
                    max_rows(q + 1)
                pe.wait_ge(raw_ready, ONE + b * KV + (q + 1))
                misc_free(("turn", q))
                for n in range(TILES):
                    mm = pe.transpose(misc[:, n * P:(n + 1) * P], raw[:, n * P:(n + 1) * P], s.ident)
                mm.then_inc(misc_ready, 1)
            misc_free("back")
            for n in range(TILES):
                mm = pe.transpose(misc[:, n * P:(n + 1) * P], on[:, n, :, :].rearrange("p h d -> p (h d)"), s.ident)
            mm.then_inc(misc_ready, 1)
            misc_free("out")
            pe.matmul(misc, s.Wo, oT, start=True, stop=True).then_inc(misc_ready, 1)

    @block.scalar
    def _(act):
        norm_act(act, s, done)
        with act.Fori(0, B) as b:
            def qsel(q, i):
                n = use[("qsel", q, i)]
                act.wait_ge(misc_ready, ONE + b * U + (n + 1))
                act.wait_ge(keyed_ready, ONE + b * 32)
                act.activation(qop[:, q, i, :], misc, ACT.Identity,
                               bias=s.slopes[:, q * QUAD + i:q * QUAD + i + 1]).then_inc(misc_read, 1)

            act.wait_ge(s.normed, ONE + b + (done + 1))
            act.wait_ge(misc_read, ONE + b * U)
            act.activation(xv, s.xn[:, batch(b)], ACT.Copy).then_inc(xv_ready, 1)
            for i in range(QUAD):
                qsel(0, i)
            for i in range(QUAD):
                qsel(1, i)
            for q in range(KV):
                for n in range(0, 16, 2):
                    kt, half, g = n // 4, n // 2 % 2, q * 8 + n // 2
                    act.wait_ge(keyed_ready, ONE + b * 32 + (g + 1))
                    act.wait_ge(pv_ready, ONE + b * 16 + max(0, 4 * q + kt - 1))
                    act.activation(E[:, kt % 2, 2 * half:2 * half + 2, :], s.psum[:, 2 + 2 * half:4 + 2 * half, :],
                                   ACT.Exp).then_inc(exp_ready, 1)
                    if n % 4 == 2 and q + 2 < KV:
                        qsel(q + 2, n // 4)
                act.wait_ge(pv_ready, ONE + b * 16 + 4 * q + 4)
                act.wait_ge(misc_ready, ONE + b * U + (use[("turn", q - 1)] + 1 if q else 0))
                act.activation(raw, pv, ACT.Copy).then_inc(raw_ready, 1)

    @block.vector
    def _(dve):
        dve.memset(mrow, 0.0).then_inc(zeroed, 1)
        dve.memset(vaug, 0.0).then_inc(zeroed, 1)
        dve.wait_ge(zeroed, ONE + 2)
        dve.memset(vaug[:, :, :, HD:HD + 1], 1.0).then_inc(zeroed, 1)
        norm_dve(dve, s, done)
        dve.wait_ge(zeroed, ONE + 3)
        with dve.Fori(0, B) as b:
            def misc_there(name):
                dve.wait_ge(misc_ready, ONE + b * U + (use[name] + 1))

            dve.wait_ge(split, ONE + b * SPLITS)
            for a, name, scale in ((0, "q", HD ** -0.5), (1, "k", 1.0)):
                misc_there(name)
                dve.tensor_scalar(parts[:, a, 0, :], misc, scale, None, ALU.mult).then_inc(split, 1)
                dve.wait_ge(split, ONE + b * SPLITS + (3 * a + 1))
                dve.scalar_tensor_tensor(rest[:, a, :], misc, scale, parts[:, a, 0, :], ALU.mult, ALU.subtract).then_inc(misc_read, 1)
                dve.wait_ge(misc_read, ONE + b * U + (use[name] + 1))
                dve.tensor_copy(parts[:, a, 1, :], rest[:, a, :]).then_inc(split, 1)
                dve.wait_ge(split, ONE + b * SPLITS + (3 * a + 2))
                dve.tensor_tensor(parts[:, a, 2, :], rest[:, a, :], parts[:, a, 1, :], ALU.subtract).then_inc(split, 1)
            misc_there("v")
            dve.wait_ge(pv_ready, ONE + b * 16)
            dve.tensor_copy(vaug[:, :, :, 0:HD], misc[:, 0:TILES * 32].rearrange("p (n g d) -> p n g d", n=TILES, g=KV)).then_inc(misc_read, 1)
            for g in range(KV):
                misc_there(("ksel", g))
                dve.tensor_tensor(kop[:, g, :], misc, s.key_rows, ALU.add).then_inc(misc_read, 1)

            def maxima(q):
                for n in range(16):
                    dve.wait_ge(scores_ready, ONE + b * (KV * RING) + (q * RING + n + 1))
                    dve.tensor_reduce(mx[:, q % 2, n:n + 1], s.bank((q * RING + n) % 2), AX.X, ALU.max).then_inc(scores_read, 1)

            def max_parts(q):
                m, r, c = mx[:, q % 2, :], mrest[:, q % 2, :], b * (3 * KV) + 3 * q
                dve.wait_ge(scores_read, ONE + b * (KV * RING) + (q * RING + 16))
                dve.tensor_scalar(mrow[:, q % 2, :, 0], m, -1.0, None, ALU.mult).then_inc(cut, 1)
                dve.wait_ge(cut, ONE + c + 1)
                dve.scalar_tensor_tensor(r, m, -1.0, mrow[:, q % 2, :, 0], ALU.mult, ALU.subtract).then_inc(cut, 1)
                dve.wait_ge(cut, ONE + c + 2)
                dve.tensor_copy(mrow[:, q % 2, :, 1], r).then_inc(cut, 1)
                dve.wait_ge(cut, ONE + c + 3)
                dve.tensor_tensor(mrow[:, q % 2, :, 2], r, mrow[:, q % 2, :, 1], ALU.subtract).then_inc(max_cut, 1)

            def max_rows(q):
                for i in range(QUAD):
                    r = q * RING + 16 + i
                    dve.wait_ge(scores_ready, ONE + b * (KV * RING) + (r + 1))
                    dve.tensor_copy(qop[MAX_ROW:P, q, i, :], s.bank(r % 2)[MAX_ROW:P, :]).then_inc(scores_read, 1)

            maxima(0)
            max_parts(0)
            max_rows(0)
            for q in range(KV):
                if q + 1 < KV:
                    maxima(q + 1)
                    max_parts(q + 1)
                    max_rows(q + 1)
                misc_there(("turn", q))
                turned = misc.rearrange("p (n i c) -> p n i c", n=TILES, i=QUAD)
                dve.wait_ge(misc_read, ONE + b * U + use[("turn", q)])
                dve.reciprocal(inv.rearrange("p (n i) -> p n i", n=TILES), turned[:, :, :, HD]).then_inc(inv_ready, 1)
                dve.wait_ge(inv_ready, ONE + b * KV + (q + 1))
                for n in range(TILES):
                    last = dve.tensor_tensor(on[:, n, q * QUAD:(q + 1) * QUAD, :], turned[:, n, :, 0:HD],
                                             inv[:, 4 * n:4 * n + 4].unsqueeze(2).to_broadcast([P, QUAD, HD]), ALU.mult)
                last.then_inc(misc_read, 1)
            misc_there("back")
            dve.tensor_copy(oT, misc).then_inc(misc_read, 1)
            misc_there("out")
            dve.tensor_tensor(s.x[:, batch(b)], s.x[:, batch(b)], misc, ALU.add).then_inc(misc_read, 1)
        dve.wait_ge(misc_read, ONE + B * U)
    return counters



IH, ID = 16, 64
SEG = 32
SEGS = T // SEG
CH = IH * ID // P
G = 4
MW = ID + 1
SWAP = [i ^ 1 for i in range(32)]


def infini_layer(nc, s, ctx, done, tag):
    counters = []

    def sem(name):
        counters.append(nc.alloc_semaphore(name=f"{tag}_{name}"))
        return counters[-1]

    affine = sem("affine")
    proj_ready, proj_read, exp_ready, capped = sem("proj_ready"), sem("proj_read"), sem("exp_ready"), sem("capped")
    rot_ready, cos_ready, sin_ready, roped = sem("rot_ready"), sem("cos_ready"), sem("sin_ready"), sem("roped")
    scores_ready, masked, row_max, shifted = sem("scores_ready"), sem("masked"), sem("row_max"), sem("shifted")
    sm_exp, row_sum, weight_ready, probs, turned = (
        sem("sm_exp"), sem("row_sum"), sem("weight"), sem("probs"), sem("turned"))
    v_ready, v_kept = sem("v_ready"), sem("v_kept")
    skt_ready, skt_kept = sem("skt_ready"), sem("skt_kept")
    recall_k, recall_q, k_inv, prev_ready, d_dve, d_pool = (
        sem("recall_k"), sem("recall_q"), sem("k_inv"), sem("prev"), sem("d_dve"), sem("d_pool"))
    updated, state_ready = sem("updated"), sem("state_ready")
    q_den, q_out, pv_ready, o_ready, ot_ready, ot_kept = (
        sem("q_den"), sem("q_out"), sem("pv_ready"), sem("o_ready"), sem("ot_ready"), sem("ot_kept"))
    out_ready, x_added, consts, beta_ready = sem("out_ready"), sem("x_added"), sem("consts"), sem("beta_ready")

    at = [0]

    def f32(n):
        a = at[0]
        at[0] += n
        return s.work[:, a:a + n]

    sq = f32(CH * T).rearrange("p (c t) -> p c t", c=CH)
    sk = f32(CH * T).rearrange("p (c t) -> p c t", c=CH)
    v = f32(SEGS * 256).rearrange("p (t n) -> p t n", t=SEGS)
    state = f32(CH * 2 * MW).rearrange("p (c n) -> p c n", c=CH)
    PT = f32(SEGS * 4 * SEG).rearrange("p (n m) -> p n m", n=4)
    D = f32(16 * MW).rearrange("p (a g n) -> p a g n", a=4, g=G)
    ones_z = f32(G * MW)
    z0 = f32(ID)
    xa = f32(T)
    betas = f32(8)
    beta, gain = betas[:, 0:4], betas[:, 4:8]
    start = at[0]
    e_buf = f32(2 * T).rearrange("p (a t) -> p a t", a=2)
    rot = f32(2 * T).rearrange("p (a t) -> p a t", a=2)
    tc = f32(2 * T).rearrange("p (a t) -> p a t", a=2)
    zr = f32(4 * T).rearrange("p (a t) -> p a t", a=4)
    stat = f32(3 * 64).rearrange("p (a n) -> p a n", a=3)
    end = at[0]
    at[0] = start
    skt = f32(2 * 256).rearrange("p (a n) -> p a n", a=2)
    prev = f32(256).rearrange("p (n d) -> p n d", n=4)
    mo = f32(256).rearrange("p (n d) -> p n d", n=4)
    o = f32(2 * 256).rearrange("p (a n) -> p a n", a=2)
    small = f32(16)
    assert max(end, at[0]) <= s.work.shape[1]
    sm = s.rs[:, 0:4 * T].rearrange("p (n m) -> p n m", n=4)
    oT = s.rs[:, 0:CH * T].rearrange("p (c t) -> p c t", c=CH)
    wq = lambda c: s.w_qkv[:, c * P:(c + 1) * P]
    wk = lambda c: s.w_qkv[:, (CH + c) * P:(CH + c + 1) * P]
    wv = s.w_qkv[:, 2 * CH * P:3 * CH * P].rearrange("p (j g n) -> p g j n", j=2, g=G)
    tok = lambda t: slice(t * SEG, (t + 1) * SEG)
    part = lambda g: slice(32 * g, 32 * g + 32)
    half = lambda e: slice(64 * e, 64 * e + 64)
    tile_of = lambda t, j, e: 2 * e + t // 8
    cols_of = lambda t, j: slice((t % 8 * 2 + j) * SEG, (t % 8 * 2 + j + 1) * SEG)
    DS = 4 * (SEGS - 1)
    NP = 2 * CH
    start_counters(nc, counters)
    block = ctx.enter_context(nc.Block())

    @block.tensor
    def _(pe):
        norm_pe(pe, s, done)
        norm_pe(pe, s, done + B, again=True)
        pe.wait_ge(consts, ONE + 5)
        with pe.Fori(0, B) as b:
            def scores(c):
                j, g = c // G, c % G
                for t in range(SEGS):
                    for e in range(2):
                        mm = pe.matmul(s.psum[part(g), 4 + tile_of(t, j, e), cols_of(t, j)],
                                       zr[half(e), (2 * c) % 4, tok(t)], zr[half(e), (2 * c + 1) % 4, tok(t)],
                                       start=True, stop=True)
                mm.then_inc(scores_ready, 1)

            pe.wait_ge(affine, ONE + b + 1)
            pe.wait_ge(x_added, ONE + b)
            for c in range(CH):
                for z, w in ((0, wq(c)), (1, wk(c))):
                    n = 2 * c + z
                    pe.wait_ge(proj_read, ONE + b * NP + max(0, n - 3))
                    if c and z:
                        pe.wait_ge(roped, ONE + b * NP + 2 * c)
                    pe.matmul(s.bank(n % 4), w, xa, start=True, stop=True).then_inc(proj_ready, 1)
                if c:
                    scores(c - 1)
            for n in range(SEGS // 2):
                if n == 0:
                    pe.wait_ge(roped, ONE + b * NP + NP)
                pe.wait_ge(proj_read, ONE + b * NP + NP)
                pe.wait_ge(v_kept, ONE + b * 8 + max(0, n - 1))
                for u in range(2):
                    for g in range(G):
                        mm = pe.matmul(s.bank(n % 2)[part(g), 256 * u:256 * u + 256], xa[:, tok(2 * n + u)], wv[:, g],
                                       start=True, stop=True)
                mm.then_inc(v_ready, 1)
                if n == 0:
                    scores(CH - 1)

            def keys_turned(t):
                pe.wait_ge(skt_kept, ONE + b * SEGS + t)
                for j in range(2):
                    for g in range(G):
                        mm = pe.matmul(s.bank(5)[part(g), P * j:P * j + P], sk[:, 4 * j + g, tok(t)], s.ident,
                                       start=True, stop=True)
                mm.then_inc(skt_ready, 1)

            def out_turned(t):
                pe.wait_ge(o_ready, ONE + b * SEGS + (t + 1))
                pe.wait_ge(ot_kept, ONE + b * SEGS + t)
                for j in range(2):
                    mm = pe.transpose(s.bank(6)[:, P * j:P * j + P], o[:, t % 2, P * j:P * j + P], s.ident)
                mm.then_inc(ot_ready, 1)

            pe.wait_ge(v_kept, ONE + b * 8 + 8)
            pe.wait_ge(masked, ONE + b * 4 + 4)
            for j in range(2):
                for e in range(2):
                    mm = pe.matmul(s.bank(2 + j)[half(e), 0:G * MW], z0, ones_z, start=True, stop=False, skip_group_check=True)
                mm.then_inc(updated, 1)
            keys_turned(0)
            pe.wait_ge(turned, ONE + b * 4 + 4)

            def recall(bank, at, operand, t, j, done_sem, before):
                for g in range(G):
                    if g == G - 1:
                        pe.wait_ge(*before)
                    mm = pe.matmul(bank[part(g), at:at + 2 * MW], operand[:, 4 * j + g, tok(t)],
                                   state[:, 4 * j + g, :], start=True, stop=True)
                mm.then_inc(done_sem, 1)

            def local(t, g):
                for j in range(2):
                    for e in range(2):
                        a = 2 * j + e
                        mm = pe.matmul(s.bank(4)[part(g), ID * a:ID * a + ID], PT[part(g), tile_of(t, j, e), cols_of(t, j)],
                                       v[part(g), t, ID * a:ID * a + ID], start=True, stop=True,
                                       tile_position=(32 * g, 32 * g))
                mm.then_inc(pv_ready, 1)

            for t in range(SEGS):
                for j in range(2):
                    pe.wait_ge(state_ready, ONE + b * (4 * SEGS) + (4 * t + 2 * j + 2))
                    pe.wait_ge(prev_ready, ONE + b * 32 + max(0, 2 * t + j - 1))
                    recall(s.bank(j), 0, sk, t, j, recall_k,
                           (pv_ready, ONE + b * (G * SEGS) + (G * t + 2)) if j
                           else (o_ready, ONE + b * SEGS + t))
                    local(t, 2 * j)
                    pe.wait_ge(q_out, ONE + b * SEGS + t)
                    recall(s.bank(7), j * 2 * MW, sq, t, j, recall_q,
                           (pv_ready, ONE + b * (G * SEGS) + (G * t + 2 * j + 1)))
                    local(t, 2 * j + 1)
                if t + 1 < SEGS:
                    keys_turned(t + 1)
                if t:
                    out_turned(t - 1)
                if t + 1 < SEGS:
                    for j in range(2):
                        pe.wait_ge(d_dve, ONE + b * DS + (4 * t + 2 * j + 2))
                        pe.wait_ge(d_pool, ONE + b * DS + (4 * t + 2 * j + 2))
                        pe.wait_ge(skt_kept, ONE + b * SEGS + (t + 1))
                        for e in range(2):
                            mm = pe.matmul(s.bank(2 + j)[half(e), 0:G * MW], skt[:, t % 2, P * j + 64 * e:P * j + 64 * e + 64],
                                           D[:, 2 * j + e, :, :].rearrange("p g n -> p (g n)"),
                                           start=False, stop=t == SEGS - 2, skip_group_check=True)
                        mm.then_inc(updated, 1)
            out_turned(SEGS - 1)
            pe.wait_ge(ot_kept, ONE + b * SEGS + SEGS)
            pe.wait_ge(q_out, ONE + b * SEGS + SEGS)
            for c in range(CH):
                mm = pe.matmul(s.bank(7), s.w_out[:, c * P:(c + 1) * P], oT[:, c, :], start=c == 0, stop=c == CH - 1)
            mm.then_inc(out_ready, 1)

    @block.scalar
    def _(act):
        act.activation(beta, s.mem_beta, ACT.Sigmoid).then_inc(beta_ready, 1)
        act.activation(gain, s.mem_beta, ACT.Sigmoid, scale=-1.0).then_inc(beta_ready, 1)
        norm_act(act, s, done)
        norm_act(act, s, done + B)
        with act.Fori(0, B) as b:
            for n in range(NP):
                act.wait_ge(proj_ready, ONE + b * NP + (n + 1))
                act.wait_ge(proj_read, ONE + b * NP + max(0, n - 1))
                act.wait_ge(ot_ready, ONE + b * SEGS)
                act.activation(e_buf[:, n % 2, :], s.bank(n % 4), ACT.Exp).then_inc(exp_ready, 1)
            for n in range(4):
                act.wait_ge(shifted, ONE + b * 4 + (n + 1))
                act.activation(sm[:, n, :], sm[:, n, :], ACT.Exp).then_inc(sm_exp, 1)
            for n in range(SEGS // 2):
                act.wait_ge(v_ready, ONE + b * 8 + (n + 1))
                act.activation(v[:, 2 * n:2 * n + 2, :], s.bank(n % 2).rearrange("p (u m) -> p u m", u=2), ACT.Copy).then_inc(v_kept, 1)

            def keys_kept(t):
                act.wait_ge(skt_ready, ONE + b * SEGS + (t + 1))
                act.wait_ge(updated, ONE + b * (2 * SEGS) + max(0, 2 * t))
                act.activation(skt[:, t % 2, :], s.bank(5)[:, 0:256], ACT.Copy).then_inc(skt_kept, 1)

            def out_kept(t):
                act.wait_ge(ot_ready, ONE + b * SEGS + (t + 1))
                act.activation(oT[:, :, tok(t)], s.bank(6)[:, 0:256].rearrange("p (c t) -> p c t", c=CH), ACT.Copy).then_inc(ot_kept, 1)

            act.wait_ge(sin_ready, ONE + b * NP + NP)
            act.wait_ge(roped, ONE + b * NP + NP)
            act.wait_ge(scores_ready, ONE + b * CH + CH)
            act.wait_ge(turned, ONE + b * 4 + 4)
            for t in range(SEGS):
                for j in range(2):
                    act.wait_ge(updated, ONE + b * (2 * SEGS) + (2 * t + j + 1))
                    if t:
                        act.wait_ge(recall_q, ONE + b * (2 * SEGS) + (2 * t - 1 + j))
                    else:
                        act.wait_ge(recall_q, ONE + b * (2 * SEGS))
                    for e in range(2):
                        act.activation(state[half(e), 4 * j:4 * j + 4, MW * e:MW * e + MW],
                                       s.bank(2 + j)[half(e), 0:G * MW].rearrange("p (g n) -> p g n", g=G),
                                       ACT.Copy).then_inc(state_ready, 1)
                keys_kept(t)
                if t > 1:
                    out_kept(t - 2)
            out_kept(SEGS - 2)
            out_kept(SEGS - 1)

    @block.gpsimd
    def _(pool):
        with pool.Fori(0, B) as b:
            for n in range(NP):
                pool.wait_ge(rot_ready, ONE + b * NP + (n + 1))
                pool.tensor_tensor(rot[:, n % 2, :], rot[:, n % 2, :], s.rope_sin, ALU.mult).then_inc(sin_ready, 1)
            for n in range(4):
                pool.wait_ge(row_max, ONE + b * 4 + (n + 1))
                pool.tensor_tensor(sm[:, n, :].rearrange("p (a k) -> p a k", k=SEG), sm[:, n, :].rearrange("p (a k) -> p a k", k=SEG),
                                   stat[:, 0, 16 * n:16 * n + 16].unsqueeze(2).to_broadcast([P, 16, SEG]), ALU.subtract).then_inc(shifted, 1)
            for n in range(4):
                pool.wait_ge(weight_ready, ONE + b * 8 + (2 * n + 2))
                pool.tensor_tensor(sm[:, n, :].rearrange("p (a k) -> p a k", k=SEG), sm[:, n, :].rearrange("p (a k) -> p a k", k=SEG),
                                   stat[:, 1, 16 * n:16 * n + 16].unsqueeze(2).to_broadcast([P, 16, SEG]), ALU.mult).then_inc(probs, 1)
            for t in range(SEGS - 1):
                for j in range(2):
                    pool.wait_ge(prev_ready, ONE + b * 32 + (2 * t + j + 1))
                    pool.wait_ge(v_kept, ONE + b * 8 + 8)
                    pool.wait_ge(updated, ONE + b * (2 * SEGS) + (2 * t + j + 1))
                    for g in (2, 3):
                        pool.tensor_tensor(D[part(g), 2 * j:2 * j + 2, g, 0:ID],
                                           v[part(g), t, P * j:P * j + P].rearrange("p (e d) -> p e d", e=2),
                                           prev[part(g), 2 * j:2 * j + 2, :], ALU.subtract).then_inc(d_pool, 1)

    @block.vector
    def _(dve):
        dve.memset(z0, 1e-6 / P).then_inc(consts, 1)
        dve.memset(ones_z, 0.0).then_inc(consts, 1)
        dve.memset(D, 0.0).then_inc(consts, 1)
        dve.memset(state, 0.0).then_inc(consts, 1)
        dve.wait_ge(consts, ONE + 4)
        dve.memset(ones_z.rearrange("p (g n) -> p g n", g=G)[:, :, ID:MW], 1.0)
        for g in range(G):
            last = dve.memset(D[part(g), :, g, ID:MW], 1.0)
        last.then_inc(consts, 1)
        norm_dve(dve, s, done)
        norm_dve(dve, s, done + B, again=True)
        dve.wait_ge(beta_ready, ONE + 2)
        with dve.Fori(0, B) as b:
            dve.wait_ge(s.normed, ONE + b + (done + B + 1))
            dve.wait_ge(v_ready, ONE + b * 8)
            dve.tensor_scalar(xa, s.xn[:, batch(b)], s.ln_g, s.ln_b, ALU.mult, ALU.add).then_inc(affine, 1)

            def rope_sum(n):
                dve.wait_ge(sin_ready, ONE + b * NP + (n + 1))
                dve.wait_ge(cos_ready, ONE + b * NP + (n + 1))
                dve.wait_ge(scores_ready, ONE + b * CH + max(0, n // 2 - 1))
                dve.tensor_tensor(zr[:, n % 4, :], tc[:, n % 2, :], rot[:, n % 2, :], ALU.add).then_inc(roped, 1)

            dve.wait_ge(ot_ready, ONE + b * SEGS)
            for n in range(NP):
                c, bank = n // 2, s.bank(n % 4)
                dve.wait_ge(exp_ready, ONE + b * NP + (n + 1))
                dve.wait_ge(roped, ONE + b * NP + max(0, n - 1))
                dve.tensor_tensor(tc[:, n % 2, :], bank, s.rope_cos, ALU.mult).then_inc(cos_ready, 1)
                dve.stream_shuffle(rot[:, n % 2, :], bank, SWAP).then_inc(rot_ready, 1)
                dve.tensor_scalar(e_buf[:, n % 2, :], e_buf[:, n % 2, :], 1.0, None, ALU.min).then_inc(capped, 1)
                if n:
                    rope_sum(n - 1)
                dve.wait_ge(capped, ONE + b * NP + (n + 1))
                dve.scalar_tensor_tensor((sk if n % 2 else sq)[:, c, :], bank, 0.0, e_buf[:, n % 2, :], ALU.max, ALU.add).then_inc(proj_read, 1)
            rope_sum(NP - 1)
            for n in range(4):
                dve.wait_ge(scores_ready, ONE + b * CH + CH)
                dve.wait_ge(out_ready, ONE + b)
                grid = lambda a: a.rearrange("p (a k) -> p a k", k=SEG)
                dve.scalar_tensor_tensor(grid(sm[:, n, :]), grid(s.bank(4 + n)), ID ** -0.5,
                                         s.causal.unsqueeze(1).to_broadcast([P, 16, SEG]), ALU.mult, ALU.add).then_inc(masked, 1)
                dve.wait_ge(masked, ONE + b * 4 + (n + 1))
                dve.tensor_reduce(stat[:, 0, 16 * n:16 * n + 16], grid(sm[:, n, :]), AX.X, ALU.max).then_inc(row_max, 1)
            for n in range(4):
                st = slice(16 * n, 16 * n + 16)
                dve.wait_ge(sm_exp, ONE + b * 4 + (n + 1))
                dve.tensor_reduce(stat[:, 2, st], grid(sm[:, n, :]), AX.X, ALU.add).then_inc(row_sum, 1)
                dve.wait_ge(row_sum, ONE + b * 4 + (n + 1))
                dve.reciprocal(stat[:, 1, st], stat[:, 2, st]).then_inc(weight_ready, 1)
                dve.wait_ge(weight_ready, ONE + b * 8 + (2 * n + 1))
                dve.tensor_tensor(stat[:, 1, st].rearrange("p (t j) -> p t j", j=2), stat[:, 1, st].rearrange("p (t j) -> p t j", j=2),
                                  gain.rearrange("p (j e) -> p e j", e=2)[:, n // 2].unsqueeze(1).to_broadcast([P, 8, 2]), ALU.mult).then_inc(weight_ready, 1)
            for n in range(4):
                dve.wait_ge(probs, ONE + b * 4 + (n + 1))
                dve.transpose(PT[:, n, :], sm[:, n, :]).then_inc(turned, 1)

            den = lambda bank, n: bank[:, 0:n * MW].rearrange("p (a n) -> p a n", a=n)[:, :, ID]
            num = lambda bank, n: bank[:, 0:n * MW].rearrange("p (a n) -> p a n", a=n)[:, :, 0:ID]
            for t in range(SEGS):
                for j in range(2):
                    a = slice(2 * j, 2 * j + 2)
                    dve.wait_ge(recall_k, ONE + b * 32 + (2 * t + j + 1))
                    dve.wait_ge(prev_ready, ONE + b * 32 + 2 * t + j)
                    dve.reciprocal(small[:, a], den(s.bank(j), 2)).then_inc(k_inv, 1)
                    dve.wait_ge(k_inv, ONE + b * 32 + (2 * t + j + 1))
                    dve.wait_ge(d_pool, ONE + b * DS + 4 * t)
                    dve.wait_ge(d_dve, ONE + b * DS + 4 * t)
                    dve.tensor_tensor(prev[:, a, :], num(s.bank(j), 2),
                                      small[:, a].unsqueeze(2).to_broadcast([P, 2, ID]), ALU.mult).then_inc(prev_ready, 1)
                    if t + 1 < SEGS:
                        dve.wait_ge(prev_ready, ONE + b * 32 + (2 * t + j + 1))
                        dve.wait_ge(v_kept, ONE + b * 8 + 8)
                        dve.wait_ge(updated, ONE + b * (2 * SEGS) + (2 * t + j + 1))
                        for g in (0, 1):
                            dve.tensor_tensor(D[part(g), a, g, 0:ID], v[part(g), t, P * j:P * j + P].rearrange("p (e d) -> p e d", e=2),
                                              prev[part(g), a, :], ALU.subtract).then_inc(d_dve, 1)
                dve.wait_ge(recall_q, ONE + b * 32 + (2 * t + 2))
                dve.wait_ge(q_out, ONE + b * SEGS + t)
                dve.tensor_scalar(small[:, 4:8], den(s.bank(7), 4), 1e-6, None, ALU.add).then_inc(q_den, 1)
                dve.wait_ge(q_den, ONE + b * (3 * SEGS) + (3 * t + 1))
                dve.reciprocal(small[:, 8:12], small[:, 4:8]).then_inc(q_den, 1)
                dve.wait_ge(q_den, ONE + b * (3 * SEGS) + (3 * t + 2))
                dve.tensor_tensor(small[:, 12:16], small[:, 8:12], beta, ALU.mult).then_inc(q_den, 1)
                dve.wait_ge(q_den, ONE + b * (3 * SEGS) + (3 * t + 3))
                dve.wait_ge(o_ready, ONE + b * SEGS + t)
                dve.tensor_tensor(mo, num(s.bank(7), 4), small[:, 12:16].unsqueeze(2).to_broadcast([P, 4, ID]), ALU.mult).then_inc(q_out, 1)
                dve.wait_ge(q_out, ONE + b * SEGS + (t + 1))
                dve.wait_ge(pv_ready, ONE + b * (G * SEGS) + (G * t + G))
                dve.wait_ge(ot_ready, ONE + b * SEGS + max(0, t - 1))
                dve.tensor_tensor(o[:, t % 2, :], s.bank(4)[:, 0:256], mo.rearrange("p n d -> p (n d)"), ALU.add).then_inc(o_ready, 1)
            dve.wait_ge(out_ready, ONE + b + 1)
            dve.tensor_tensor(s.x[:, batch(b)], s.x[:, batch(b)], s.bank(7), ALU.add).then_inc(x_added, 1)
        dve.wait_ge(x_added, ONE + B)
    return counters



E, MC = 8, 4
EXPERT = 2 * MC * P
TOK = N // P


def moe_layer(nc, s, ctx, done, tag):
    counters = []

    def sem(name):
        counters.append(nc.alloc_semaphore(name=f"{tag}_{name}"))
        return counters[-1]

    zeroed = sem("zeroed")
    weights_in, step, exped, logits_ready = sem("weights_in"), sem("step"), sem("exped"), sem("logits_ready")
    turned, kept, choice_ready = sem("turned"), sem("kept"), sem("choice_ready")
    masked_b1, c_ready, c_kept, csum_ready = sem("masked_b1"), sem("c_ready"), sem("c_kept"), sem("csum_ready")
    spread, spread_read = sem("spread"), sem("spread_read")
    scaled, xe_ready, up_ready = sem("scaled"), sem("xe_ready"), sem("up_ready")
    h_act, h_dve, down_ready, x_added = sem("h_act"), sem("h_dve"), sem("down_ready"), sem("x_added")

    at = [0]

    def f32(n, rows=P):
        a = at[0]
        at[0] += n
        return s.work[0:rows, a:a + n]

    experts = f32(E * EXPERT)
    up_w = lambda e, c: experts[:, e * EXPERT + c * P:e * EXPERT + (c + 1) * P]
    down_w = lambda e, c: up_w(e, MC + c)
    h = f32(2 * MC * T).rearrange("p (n c t) -> p n c t", n=2, c=MC)
    xe = f32(2 * T).rearrange("p (n t) -> p n t", n=2)
    choice = f32(N)
    choice_b = f32(N // 2).bitcast(BF16)
    pick_expert = f32(E * P // 2).bitcast(BF16).rearrange("p (e m) -> p e m", e=E)
    pick_score = f32(P)
    fix = f32(P)
    fix_c = f32(P, 2 * E)
    csum = f32(1)
    rb1 = f32(E * MC)
    rb1_own = f32(E * MC * 2 * E).rearrange("p (e c j) -> p e c j", e=E, c=MC)
    tile_e = lambda a: a.rearrange("p (i e) -> p i e", e=E)
    score, t0, t1, first = (tile_e(f32(TOK * E)) for _ in range(4))
    both = f32(TOK * 2 * E).rearrange("p (i e) -> p i e", e=2 * E)
    best = f32(TOK)
    assert at[0] <= s.work.shape[1]
    wide = lambda a: a.unsqueeze(2).to_broadcast([P, TOK, E])
    each = lambda a: a.unsqueeze(1).to_broadcast([P, TOK, E])
    logits = tile_e(s.bank(4)[:, 0:TOK * E])
    SPREADS = E + 1
    start_counters(nc, counters)
    block = ctx.enter_context(nc.Block())

    @block.sync
    def _(sp):
        sp.dma_start(experts, s.expert_w).then_inc(weights_in, 16)
        sp.wait_ge(weights_in, ONE + 16)

    @block.tensor
    def _(pe):
        norm_pe(pe, s, done)
        pe.wait_ge(s.normed, ONE + done + B)
        for i in range(TOK):
            mm = pe.matmul(s.bank(4)[:, i * E:(i + 1) * E], s.xn[:, i * P:(i + 1) * P], s.gate_w, start=True, stop=True)
        mm.then_inc(logits_ready, 1)
        pe.wait_ge(weights_in, ONE + 16)
        pe.wait_ge(masked_b1, ONE + 2)
        for e in range(E):
            for c in range(MC):
                mm = pe.matmul(s.bank(7)[0:2 * E, 0:P], rb1_own[:, e, c, :], down_w(e, c),
                               start=e == 0 and c == 0, stop=e == E - 1 and c == MC - 1)
        mm.then_inc(c_ready, 1)
        pe.wait_ge(c_kept, ONE + 1)
        pe.matmul(s.bank(7)[:, P:P + 1], fix_c, s.ones[0:2 * E, :], start=True, stop=True).then_inc(csum_ready, 1)
        pe.wait_ge(choice_ready, ONE + 1)
        for b in range(B):
            pe.wait_ge(kept, ONE + max(0, b - 1))
            for n in range(4):
                mm = pe.transpose(s.bank(5 + b % 2)[0:2 * E, n * P:(n + 1) * P], both[:, 4 * b + n, :], s.ident)
            mm.then_inc(turned, 1)
        pe.wait_ge(kept, ONE + B)
        pe.wait_ge(choice_ready, ONE + 2)
        pe.wait_ge(masked_b1, ONE + 4)
        pe.wait_ge(c_kept, ONE + 3)
        with pe.Fori(0, B // 2) as pair:
            b = pair * 2

            def spread_row(u, n):
                r = u * SPREADS + (n + 1) % SPREADS
                pe.wait_ge(spread_read, ONE + b * SPREADS + max(0, r - 1))
                if n == E:
                    pe.matmul(s.bank(6 + r % 2), pick_score, choice[:, batch(b + u)], start=True, stop=True).then_inc(spread, 1)
                else:
                    pe.matmul(s.bank(6 + r % 2), pick_expert[:, n, :], choice_b[:, batch(b + u)],
                              start=True, stop=True).then_inc(spread, 1)

            def up(u, e):
                k = u * E + e
                pe.wait_ge(xe_ready, ONE + b * E + (k + 1))
                for c in range(MC):
                    h_side = h_act if c < 2 else h_dve
                    pe.wait_ge(h_side, ONE + b * 2 * E + max(0, 2 * k - 1 + c % 2))
                    mm = pe.matmul(s.bank(c), up_w(e, c), xe[:, k % 2, :], start=True, stop=True)
                    mm.then_inc(up_ready, 1)

            def down(u, e):
                k = u * E + e
                if e == 0:
                    pe.wait_ge(x_added, ONE + b)
                    pe.matmul(s.bank(4 + u), fix, choice[:, batch(b + u)], start=True, stop=False)
                for c in range(MC):
                    pe.wait_ge(h_act if c < 2 else h_dve, ONE + b * 2 * E + (2 * k + 1 + c % 2))
                    mm = pe.matmul(s.bank(4 + u), down_w(e, c), h[:, k % 2, c, :], start=False, stop=e == E - 1 and c == MC - 1)
                mm.then_inc(down_ready, 1)

            spread_row(0, E)
            spread_row(0, 0)
            for u in range(2):
                for e in range(E):
                    if e + 1 < E:
                        spread_row(u, e + 1)
                    elif u == 0:
                        spread_row(1, E)
                    up(u, e)
                    if e:
                        down(u, e - 1)
                    elif u:
                        down(0, E - 1)
                    if e == E - 1 and u == 0:
                        spread_row(1, 0)
            down(1, E - 1)

    @block.gpsimd
    def _(pool):
        pool.memset(choice, 0.0).then_inc(zeroed, 1)
        pool.memset(fix, 0.0).then_inc(zeroed, 1)

    @block.scalar
    def _(act):
        norm_act(act, s, done)
        act.wait_ge(step, ONE + 3)
        act.activation(t0, t0, ACT.Exp).then_inc(exped, 1)
        act.wait_ge(zeroed, ONE + 2)
        for b in range(B):
            act.wait_ge(turned, ONE + b + 1)
            act.activation(choice[0:2 * E, batch(b)], s.bank(5 + b % 2)[0:2 * E, :], ACT.Copy).then_inc(kept, 1)
        with act.Fori(0, B // 2) as pair:
            b = pair * 2
            for k in range(2 * E):
                act.wait_ge(down_ready, ONE + b * E + max(0, k - 1))
                for c in range(2):
                    act.wait_ge(up_ready, ONE + b * E * MC + (k * MC + c + 1))
                    act.activation(h[:, k % 2, c, :], s.bank(c), ACT.Relu,
                                   bias=s.b1[:, k % E * MC + c:k % E * MC + c + 1]).then_inc(h_act, 1)

    @block.vector
    def _(dve):
        dve.tensor_scalar(rb1, s.b1, 0.0, None, ALU.max).then_inc(masked_b1, 1)
        dve.wait_ge(masked_b1, ONE + 1)
        dve.tensor_tensor(rb1_own, rb1.rearrange("p (e c) -> p e c", e=E).unsqueeze(3).to_broadcast([P, E, MC, 2 * E]),
                          s.expert_eye.rearrange("p (e j) -> p e j", e=E).unsqueeze(2).to_broadcast([P, E, MC, 2 * E]),
                          ALU.mult).then_inc(masked_b1, 1)
        dve.tensor_copy(pick_expert, s.ident[:, 0:E].unsqueeze(2).to_broadcast([P, E, P])).then_inc(masked_b1, 1)
        dve.tensor_copy(pick_score, s.score_rows.to_broadcast([P, P])).then_inc(masked_b1, 1)
        norm_dve(dve, s, done)

        def after(n):
            dve.wait_ge(step, ONE + n)

        dve.wait_ge(logits_ready, ONE + 1)
        dve.tensor_tensor(score, logits, each(s.gate_b), ALU.add).then_inc(step, 1)
        after(1)
        dve.tensor_reduce(best, score, AX.X, ALU.max).then_inc(step, 1)
        after(2)
        dve.tensor_tensor(t0, score, wide(best), ALU.subtract).then_inc(step, 1)
        dve.wait_ge(exped, ONE + 1)
        after(3)
        dve.tensor_reduce(best, t0, AX.X, ALU.add).then_inc(step, 1)
        after(4)
        dve.reciprocal(best, best).then_inc(step, 1)
        after(5)
        dve.tensor_tensor(score, t0, wide(best), ALU.mult).then_inc(step, 1)
        n = 6
        for is_best, pool in ((first, score), (t1, t0)):
            if is_best is t1:
                after(n)
                dve.scalar_tensor_tensor(t0, first, -2.0, score, ALU.mult, ALU.add).then_inc(step, 1)
                n += 1
            after(n)
            dve.tensor_reduce(best, pool, AX.X, ALU.max).then_inc(step, 1)
            after(n + 1)
            dve.tensor_tensor(is_best, pool, wide(best), ALU.is_equal).then_inc(step, 1)
            after(n + 2)
            dve.tensor_tensor(is_best, is_best, each(s.low_first), ALU.mult).then_inc(step, 1)
            after(n + 3)
            dve.tensor_reduce(best, is_best, AX.X, ALU.max).then_inc(step, 1)
            after(n + 4)
            dve.tensor_tensor(is_best, is_best, wide(best), ALU.is_equal).then_inc(step, 1)
            n += 5
        after(n)
        dve.tensor_tensor(t1, t1, first, ALU.add).then_inc(step, 1)
        after(n + 1)
        dve.scalar_tensor_tensor(t1, score, 0.0, t1, ALU.is_gt, ALU.mult).then_inc(step, 1)
        after(n + 2)
        dve.tensor_tensor(t1, t1, each(s.high_first), ALU.mult).then_inc(step, 1)
        after(n + 3)
        dve.tensor_reduce(best, t1, AX.X, ALU.max).then_inc(step, 1)
        after(n + 4)
        dve.tensor_tensor(both[:, :, 0:E], t1, wide(best), ALU.is_equal).then_inc(step, 1)
        after(n + 5)
        dve.tensor_tensor(both[:, :, E:2 * E], both[:, :, 0:E], score, ALU.mult).then_inc(choice_ready, 1)

        dve.wait_ge(c_ready, ONE + 1)
        dve.tensor_copy(fix_c, s.bank(7)[0:2 * E, 0:P]).then_inc(c_kept, 1)
        dve.wait_ge(csum_ready, ONE + 1)
        dve.wait_ge(c_kept, ONE + 1)
        dve.wait_ge(zeroed, ONE + 2)
        dve.tensor_copy(csum, s.bank(7)[:, P:P + 1]).then_inc(c_kept, 1)
        dve.tensor_tensor(fix[0:2 * E, :], fix_c, s.b2[0:2 * E, :], ALU.add).then_inc(c_kept, 1)
        dve.wait_ge(kept, ONE + B)
        dve.tensor_copy(choice_b, choice).then_inc(choice_ready, 1)
        dve.wait_ge(c_kept, ONE + 3)
        with dve.Fori(0, B // 2) as pair:
            b = pair * 2

            def score_tokens(u):
                r = u * SPREADS
                dve.wait_ge(spread, ONE + b * SPREADS + (r + 1))
                dve.tensor_tensor(s.xn[:, batch(b + u)], s.xn[:, batch(b + u)], s.bank(6 + r % 2), ALU.mult).then_inc(spread_read, 1)

            def own_tokens(u, e):
                k, r = u * E + e, u * SPREADS + e + 1
                dve.wait_ge(spread, ONE + b * SPREADS + (r + 1))
                if e == 0:
                    dve.wait_ge(spread_read, ONE + b * SPREADS + (u * SPREADS + 1))
                dve.wait_ge(up_ready, ONE + b * E * MC + max(0, k - 1) * MC)
                dve.tensor_tensor(xe[:, k % 2, :], s.xn[:, batch(b + u)], s.bank(6 + r % 2), ALU.mult).then_inc(spread_read, 1)
                dve.wait_ge(spread_read, ONE + b * SPREADS + (r + 1))
                dve.sem_inc(xe_ready, 1)

            def add(u):
                dve.wait_ge(down_ready, ONE + b * E + (u * E + E))
                dve.scalar_tensor_tensor(s.x[:, batch(b + u)], s.bank(4 + u), csum, s.x[:, batch(b + u)],
                                         ALU.subtract, ALU.add).then_inc(x_added, 1)

            score_tokens(0)
            own_tokens(0, 0)
            for k in range(2 * E):
                u, e = k // E, k % E
                if e == 1 and u == 1:
                    add(0)
                if e + 1 < E:
                    own_tokens(u, e + 1)
                elif u == 0:
                    score_tokens(1)
                dve.wait_ge(down_ready, ONE + b * E + max(0, k - 1))
                for c in range(2, MC):
                    dve.wait_ge(up_ready, ONE + b * E * MC + (k * MC + c + 1))
                    dve.tensor_scalar(h[:, k % 2, c, :], s.bank(c), s.b1[:, e * MC + c:e * MC + c + 1], 0.0,
                                      ALU.add, ALU.max).then_inc(h_dve, 1)
                if e == E - 1 and u == 0:
                    own_tokens(1, 0)
            add(1)
        dve.wait_ge(x_added, ONE + B)
    return counters



def _columns(sizes):
    at, out = 0, {}
    for name, n in sizes:
        out[name] = (at, at + n)
        at += n
    return out, at


WEIGHTS, WEIGHT_COLS = _columns(
    [("avg", P), ("ident", P), ("slopes", 16), ("key_rows", T)]
    + [("w_qkv", 3 * CH * P), ("w_out", CH * P), ("ln_g", 1), ("ln_b", 1), ("mem_beta", 4)]
    + [("rope_cos", T), ("rope_sin", T), ("causal", SEG)]
    + [("Wq", P), ("Wk", P), ("Wv", 32), ("Wo", P)]
    + [(name, P) for name in ("W_in", "W_B", "W_D", "W_out", "C_mat")] + [(name, 16) for name in ("W_ig", "W_fg", "B_mat")]
    + [(name, 1) for name in ("b_in", "b_B", "b_D", "b_out", "b_ig", "b_fg", "gamma", "beta")]
    + [(name, P) for name in ("W_key", "W_value", "W_receptance", "W_output")]
    + [(name, 1) for name in ("time_decay", "time_first", "mix_k", "mix_v", "mix_r")]
    + [("gate_w", E), ("gate_b", E), ("b1", E * MC), ("b2", P)]
    + [("low_first", E), ("high_first", E), ("expert_eye", E * 2 * E), ("score_rows", 1), ("ones", 1)]
)
INTS, INT_COLS = _columns([("wgate", HID), ("wup", HID), ("wdown", HID)])


class Shared:
    pass


GQA_BF16_COLS = (HEADS + KV) * 3 * P + P


def build(nc, x_in, weights, ints, gqa_tables, expert_w, out, layers):
    with ExitStack() as ctx:
        def sb(name, shape, dt=F32):
            return ctx.enter_context(nc.sbuf_tensor(name, shape, dt))

        def sem(name):
            return ctx.enter_context(nc.semaphore("norm_" + name))

        w = sb("w", [P, WEIGHT_COLS])
        wf = sb("wf", [P, INT_COLS])
        weight = lambda name: w[:, WEIGHTS[name][0]:WEIGHTS[name][1]]
        integer = lambda name: wf[:, INTS[name][0]:INTS[name][1]]
        s = Shared()
        s.avg, s.ident, s.slopes, s.key_rows = weight("avg"), weight("ident"), weight("slopes"), weight("key_rows")
        s.w_qkv, s.w_out, s.ln_g, s.ln_b = weight("w_qkv"), weight("w_out"), weight("ln_g"), weight("ln_b")
        s.mem_beta, s.rope_cos, s.rope_sin, s.causal = weight("mem_beta"), weight("rope_cos"), weight("rope_sin"), weight("causal")
        s.Wq, s.Wk, s.Wv, s.Wo = weight("Wq"), weight("Wk"), weight("Wv"), weight("Wo")
        s.W_in, s.W_B, s.W_D, s.W_out = weight("W_in"), weight("W_B"), weight("W_D"), weight("W_out")
        s.C_mat, s.W_ig, s.W_fg, s.B_mat = weight("C_mat"), weight("W_ig"), weight("W_fg"), weight("B_mat")
        s.b_in, s.b_B, s.b_D, s.b_out = weight("b_in"), weight("b_B"), weight("b_D"), weight("b_out")
        s.b_ig, s.b_fg, s.gamma, s.beta = weight("b_ig"), weight("b_fg"), weight("gamma"), weight("beta")
        s.W_key, s.W_value, s.W_receptance, s.W_output = weight("W_key"), weight("W_value"), weight("W_receptance"), weight("W_output")
        s.time_decay, s.time_first, s.mix_k, s.mix_v = weight("time_decay"), weight("time_first"), weight("mix_k"), weight("mix_v")
        s.mix_r, s.gate_w, s.gate_b, s.b1 = weight("mix_r"), weight("gate_w"), weight("gate_b"), weight("b1")
        s.b2, s.low_first, s.high_first, s.expert_eye = weight("b2"), weight("low_first"), weight("high_first"), weight("expert_eye")
        s.score_rows, s.ones = weight("score_rows"), weight("ones")
        s.wgate, s.wup, s.wdown = integer("wgate"), integer("wup"), integer("wdown")
        s.b_ig, s.b_fg = s.b_ig[0:16, :], s.b_fg[0:16, :]

        s.gqa_tables, s.expert_w = gqa_tables, expert_w
        s.x = sb("x", [P, N])
        s.xn = sb("xn", [P, N])
        s.rs = sb("rs", [P, N])
        s.sq = sb("sq", [P, 2, T])
        s.eps = sb("eps", [P, 1])
        s.scrap = sb("scrap", [P, 1])
        s.work = sb("work", [P, 23 * 1024])
        wi = s.work[:, 0:INT_COLS].bitcast(I32)
        s.psum = ctx.enter_context(nc.psum_tensor("psum", [P, 8, T], F32))
        s.bank = lambda i: s.psum[:, i, :]
        s.centered, s.squared, s.mean_ready = sem("centered"), sem("squared"), sem("mean_ready")
        s.var_ready, s.logged, s.rstd_ready = sem("var_ready"), sem("logged"), sem("rstd_ready")
        s.normed, s.warmed = sem("normed"), sem("warmed")
        norm_counters = (s.centered, s.squared, s.mean_ready, s.var_ready, s.logged, s.rstd_ready, s.normed, s.warmed)
        loaded = ctx.enter_context(nc.semaphore("loaded"))
        consts = ctx.enter_context(nc.semaphore("consts"))
        stored = ctx.enter_context(nc.semaphore("stored"))

        start_counters(nc, norm_counters)
        with nc.Block() as block:
            @block.sync
            def _(sp):
                sp.dma_start(s.x[:, :], x_in).then_inc(loaded, 16)
                sp.dma_start(w[:, :], weights).then_inc(loaded, 16)
                sp.dma_start(wi, ints).then_inc(loaded, 16)
                sp.wait_ge(loaded, 48)

            @block.vector
            def _(dve):
                dve.memset(s.eps[:, :], 1e-5).then_inc(consts, 1)
                dve.wait_ge(loaded, 48)
                dve.tensor_scalar(wf[:, :], wi, float(np.float32(1.0 / 127.0)), None, ALU.mult).then_inc(consts, 1)
                dve.wait_ge(consts, 2)

        done = 0
        for n, kind in enumerate(layers):
            with ExitStack() as own:
                counters = LAYERS[kind](nc, s, own, done, f"l{n}")
            nc.all_engine_barrier()
            nc.clear_and_free_semaphores(counters)
            nc.all_engine_barrier()
            done += 2 * B if kind == "infini" else B

        with nc.Block() as block:
            @block.sync
            def _(sp):
                sp.dma_start(out, s.x[:, :]).then_inc(stored, 16)
                sp.wait_ge(stored, 16)


LAYERS = {"swiglu": swiglu_layer, "ssm": ssm_layer, "rwkv": rwkv_layer, "gqa": gqa_layer, "infini": infini_layer,
          "moe": moe_layer}



def gqa_constants():
    bf = np.dtype("bfloat16")
    start = 2.0 ** (-2.0 ** (-(math.log2(HEADS) - 3)))
    slope = np.array([start * start ** i for i in range(HEADS)], dtype=np.float32)
    slopes, rows = np.zeros((P, HEADS), np.float32), np.zeros((P, T), np.float32)
    position = np.arange(T)
    left = slope
    for i in range(3):
        part = left.astype(bf).astype(np.float32)
        left = left - part
        for j, pos in enumerate((position // 256 * 256, position % 256)):
            slopes[BIAS_ROW + 2 * i + j] = part
            rows[BIAS_ROW + 2 * i + j] = pos
    rows[MAX_ROW:MAX_ROW + 3] = 1
    tables = np.zeros((P, GQA_BF16_COLS), bf)
    for side, heads, at in ((0, HEADS, 0), (1, KV, HEADS * 3 * P)):
        for h in range(heads):
            for n, pair in enumerate(SLOTS):
                for d in range(HD):
                    tables[h * HD + d, at + (h * 3 + pair[side]) * P + n * HD + d] = 1
    tables[:, (HEADS + KV) * 3 * P:] = np.eye(P)
    return slopes, rows, tables


def infini_constants():
    freqs = np.float32(10000.0) ** (-np.arange(0, ID, 2, dtype=np.float32) / np.float32(ID))
    angle = (np.arange(T, dtype=np.float32)[:, None] * freqs).astype(np.float32)
    feature = np.arange(P) % ID
    cos = np.cos(angle)[:, feature // 2].T
    sin = np.sin(angle)[:, feature // 2].T * np.where(feature % 2, 1.0, -1.0).astype(np.float32)[:, None]
    row, column = np.arange(P) % SEG, np.arange(SEG)
    causal = np.where(column[None, :] <= row[:, None], np.float32(0), np.float32(-1e30))
    return cos.astype(np.float32), sin.astype(np.float32), causal.astype(np.float32)


def lay_out(i):
    f = lambda name: np.asarray(i[name])
    x = np.ascontiguousarray(f("L0_attn_a_x").reshape(N, P).T)
    avg = np.full((P, P), 1.0 / P, np.float32)
    col = lambda a: np.concatenate([a.reshape(-1, 1), np.zeros((P - a.size, 1), a.dtype)])
    rows = lambda a: np.concatenate([a, np.zeros((P - a.shape[0], a.shape[1]), a.dtype)])
    parts = {"avg": avg, "ident": np.eye(P, dtype=np.float32)}
    parts["slopes"], parts["key_rows"], gqa_tables = gqa_constants()
    parts["w_qkv"] = f("L0_attn_b_w_qkv")
    parts["w_out"] = f("L0_attn_b_w_out").reshape(CH, P, P).transpose(1, 0, 2).reshape(P, CH * P)
    parts["ln_g"], parts["ln_b"] = col(f("L0_attn_b_ln_g")), col(f("L0_attn_b_ln_b"))
    gate = f("L0_attn_b_mem_beta").reshape(2, G, 2).transpose(1, 0, 2).reshape(G, 1, 4)
    parts["mem_beta"] = np.broadcast_to(gate, (G, 32, 4)).reshape(P, 4)
    parts["rope_cos"], parts["rope_sin"], parts["causal"] = infini_constants()
    for name in ("Wq", "Wv", "Wo"):
        parts[name] = f("L0_attn_a_" + name)
    parts["Wk"] = np.concatenate([f("L0_attn_a_Wk"), np.zeros((P, P - KV * HD), np.float32)], axis=1)
    for name in ("W_in", "W_B", "W_D", "W_out", "W_ig", "W_fg", "B_mat"):
        parts[name] = f("L1_attn_a_" + name)
    parts["C_mat"] = rows(f("L1_attn_a_C_mat"))
    for name in ("b_in", "b_B", "b_D", "b_out", "b_ig", "b_fg", "gamma", "beta"):
        parts[name] = col(f("L1_attn_a_" + name))
    for name in ("W_key", "W_value", "W_receptance", "W_output"):
        parts[name] = f("L1_attn_b_" + name).T
    for name in ("time_decay", "time_first"):
        parts[name] = col(f("L1_attn_b_" + name))
    for name in "kvr":
        parts["mix_" + name] = col(f("L1_attn_b_time_mix_" + name))
    everywhere = lambda a: np.broadcast_to(a.reshape(1, -1), (P, a.size))
    parts["gate_w"], parts["gate_b"] = f("L0_ffn_gate_w"), everywhere(f("L0_ffn_gate_b"))
    parts["b1"] = f("L0_ffn_b1").reshape(E * MC, P).T
    parts["b2"] = rows(f("L0_ffn_b2"))
    index = np.arange(E, dtype=np.float32)
    parts["low_first"], parts["high_first"] = everywhere(E - index), everywhere(index + 1)
    parts["expert_eye"] = everywhere(np.eye(E, 2 * E, dtype=np.float32))
    parts["score_rows"] = ((np.arange(P) >= E) & (np.arange(P) < 2 * E)).astype(np.float32).reshape(P, 1)
    parts["ones"] = np.ones((P, 1), np.float32)
    weights = np.concatenate([parts[name] for name in WEIGHTS], axis=1)
    wd = f("L1_ffn_w_down")
    ints = np.concatenate([
        f("L1_ffn_w_gate").T, f("L1_ffn_w_up").T,
        wd.T.reshape(HC, P, P).transpose(1, 0, 2).reshape(P, HID)], axis=1)
    up = f("L0_ffn_w1").transpose(1, 0, 2)
    down = f("L0_ffn_w2").reshape(E, MC, P, P).transpose(2, 0, 1, 3).reshape(P, E, MC * P)
    expert_w = np.ascontiguousarray(np.concatenate([up, down], axis=2).reshape(P, E * EXPERT))
    return {"x_in": x, "weights": np.ascontiguousarray(weights), "ints": np.ascontiguousarray(ints),
            "gqa_tables": gqa_tables, "expert_w": expert_w}


MODEL = ["gqa", "moe", "infini", "moe", "ssm", "swiglu", "rwkv", "swiglu"]


def kernel(**inputs):
    import concourse.bacc as bacc
    from concourse.bass_utils import run_bass_kernel_spmd

    arrays = lay_out(inputs)
    nc = bacc.Bacc("TRN2", target_bir_lowering=False, num_devices=1)
    args = [nc.dram_tensor(name, a.shape, mybir.dt.from_np(a.dtype), kind="ExternalInput").ap()
            for name, a in arrays.items()]
    out = nc.dram_tensor("out", (P, N), F32, kind="ExternalOutput").ap()
    build(nc, *args, out, MODEL)
    results = run_bass_kernel_spmd(nc, [arrays], core_ids=[0]).results
    return np.ascontiguousarray(results[0]["out"].T).reshape(B, T, P)
```

```python
from contextlib import ExitStack
import math

import numpy as np

import concourse.bass as bass
from concourse import mybir

P = 128
B, T = 8, 512
N = B * T
F32, BF16 = mybir.dt.float32, mybir.dt.bfloat16
I32 = mybir.dt.int32
ALU, ACT, AX = mybir.AluOpType, mybir.ActivationFunctionType, mybir.AxisListType

HID = 384
HC = HID // P
FREE = 2
ONE = 1


def start_counters(nc, counters):
    with nc.Block() as block:
        @block.sync
        def _(sp):
            for counter in counters:
                sp.sem_inc(counter, ONE)


def batch(b):
    return bass.ds(b * T, T) if not isinstance(b, int) else slice(b * T, b * T + T)



def norm_pe(pe, s, done, again=False):
    src = s.xn if again else s.x
    with pe.Fori(0, B // 2) as pair:
        b = pair * 2
        for u in range(2):
            pe.wait_ge(s.centered, ONE + b + done)
            if again:
                pe.wait_ge(s.normed, ONE + b + (done - B + u + 1))
            pe.matmul(s.bank(u), s.avg[:, :], src[:, batch(b + u)], start=True, stop=True).then_inc(s.mean_ready, 1)
        for u in range(2):
            pe.wait_ge(s.squared, ONE + b + (done + u + 1))
            pe.wait_ge(s.logged, ONE + b + done)
            pe.matmul(s.bank(2 + u), s.avg[:, :], s.sq[:, u, :], start=True, stop=True).then_inc(s.var_ready, 1)


def norm_act(act, s, done):
    if done:
        act.wait_ge(s.warmed, ONE + done // B * 2)
    act.activation(s.scrap[:, 0:1], s.eps[:, 0:1], ACT.Ln).then_inc(s.warmed, 1)
    with act.Fori(0, B // 2) as pair:
        b = pair * 2
        for u in range(2):
            act.wait_ge(s.centered, ONE + b + (done + u + 1))
            act.wait_ge(s.var_ready, ONE + b + done)
            act.activation(s.sq[:, u, :], s.xn[:, batch(b + u)], ACT.Square).then_inc(s.squared, 1)
        for u in range(2):
            act.wait_ge(s.var_ready, ONE + b + (done + u + 1))
            act.activation(s.rs[:, batch(b + u)], s.bank(2 + u), ACT.Ln, bias=s.eps[:, 0:1]).then_inc(s.logged, 1)
    act.wait_ge(s.warmed, ONE + done // B * 2 + 1)
    act.activation(s.scrap[:, 0:1], s.eps[:, 0:1], ACT.Exp).then_inc(s.warmed, 1)
    act.wait_ge(s.logged, ONE + done + B)
    with act.Fori(0, B) as b:
        act.activation(s.rs[:, batch(b)], s.rs[:, batch(b)], ACT.Exp, scale=-0.5).then_inc(s.rstd_ready, 1)


def norm_dve(dve, s, done, again=False):
    src = s.xn if again else s.x
    with dve.Fori(0, B // 2) as pair:
        b = pair * 2
        for u in range(2):
            dve.wait_ge(s.mean_ready, ONE + b + (done + u + 1))
            dve.tensor_tensor(s.xn[:, batch(b + u)], src[:, batch(b + u)], s.bank(u), ALU.subtract).then_inc(s.centered, 1)
    dve.wait_ge(s.centered, ONE + done + B)
    with dve.Fori(0, B) as b:
        dve.wait_ge(s.rstd_ready, ONE + b + (done + 1))
        dve.tensor_tensor(s.xn[:, batch(b)], s.xn[:, batch(b)], s.rs[:, batch(b)], ALU.mult).then_inc(s.normed, 1)



def swiglu_layer(nc, s, ctx, done, tag):
    counters = []

    def sem(name):
        counters.append(nc.alloc_semaphore(name=f"{tag}_{name}"))
        return counters[-1]

    gate_ready, up_ready = sem("gate_ready"), sem("up_ready")
    silu_ready, h_ready = sem("silu_ready"), sem("h_ready")
    down_ready, x_added = sem("down_ready"), sem("x_added")
    sg = s.work[:, 0:2 * T].rearrange("p (n t) -> p n t", n=2)
    h = s.work[:, 2 * T:(2 + 2 * HC) * T].rearrange("p (n t) -> p n t", n=2 * HC)
    start_counters(nc, counters + FREE * [h_ready])
    block = ctx.enter_context(nc.Block())

    @block.tensor
    def _(pe):
        norm_pe(pe, s, done)
        with pe.Fori(0, B // 2) as pair:
            b = pair * 2
            for u in range(2):
                pe.wait_ge(s.normed, ONE + b + (done + u + 1))
                for c in range(HC):
                    k = HC * u + c
                    pe.wait_ge(h_ready, ONE + b * HC + (k + 1))
                    pe.matmul(s.bank(k % 2), s.wgate[:, P * c:P * c + P], s.xn[:, batch(b + u)],
                              start=True, stop=True).then_inc(gate_ready, 1)
                    pe.matmul(s.bank(2 + k % 2), s.wup[:, P * c:P * c + P], s.xn[:, batch(b + u)],
                              start=True, stop=True).then_inc(up_ready, 1)
            for u in range(2):
                pe.wait_ge(x_added, ONE + b)
                for c in range(HC):
                    pe.wait_ge(h_ready, ONE + b * HC + (HC * u + c + 1 + FREE))
                    mm = pe.matmul(s.bank(4 + u), s.wdown[:, P * c:P * c + P], h[:, HC * u + c, :],
                                   start=c == 0, stop=c == HC - 1)
                mm.then_inc(down_ready, 1)

    @block.scalar
    def _(act):
        norm_act(act, s, done)
        with act.Fori(0, B // 2) as pair:
            b = pair * 2
            for k in range(2 * HC):
                act.wait_ge(gate_ready, ONE + b * HC + (k + 1))
                act.wait_ge(h_ready, ONE + b * HC + (k + 1))
                act.activation(sg[:, k % 2, :], s.bank(k % 2), ACT.Silu).then_inc(silu_ready, 1)

    @block.vector
    def _(dve):
        norm_dve(dve, s, done)
        with dve.Fori(0, B // 2) as pair:
            b = pair * 2
            dve.wait_ge(down_ready, ONE + b)
            for k in range(2 * HC):
                dve.wait_ge(silu_ready, ONE + b * HC + (k + 1))
                dve.wait_ge(up_ready, ONE + b * HC + (k + 1))
                dve.tensor_tensor(h[:, k, :], s.bank(2 + k % 2), sg[:, k % 2, :], ALU.mult).then_inc(h_ready, 1)
            for u in range(2):
                dve.wait_ge(down_ready, ONE + b + (u + 1))
                dve.tensor_tensor(s.x[:, batch(b + u)], s.x[:, batch(b + u)], s.bank(4 + u), ALU.add).then_inc(x_added, 1)
        dve.wait_ge(x_added, ONE + B)
    return counters



def ssm_layer(nc, s, ctx, done, tag):
    counters = []

    def sem(name):
        counters.append(nc.alloc_semaphore(name=f"{tag}_{name}"))
        return counters[-1]

    xp_ready, t_ready, gates_ready, tb_ready = sem("xp_ready"), sem("t_ready"), sem("gates_ready"), sem("tb_ready")
    xp_mm, bx_ready, gated, drive_ready = sem("xp_mm"), sem("bx_ready"), sem("gated"), sem("drive_ready")
    states_ready, pre_ready, tanh_ready, y_ready = sem("states"), sem("pre_ready"), sem("tanh_ready"), sem("y_ready")
    res_ready, mean_ready, centered, squared = sem("res_ready"), sem("mean_ready"), sem("centered"), sem("squared")
    var_ready, var_kept, ln_done, rstd, scaled, x_added = (
        sem("var_ready"), sem("var_kept"), sem("ln_done"), sem("rstd"), sem("scaled"), sem("x_added"))
    zeroed = sem("zeroed")
    S = s.W_ig.shape[1]
    w = s.work
    xp = w[:, 0:2 * T].rearrange("p (u t) -> p u t", u=2)
    tb = w[:, 2 * T:4 * T].rearrange("p (u t) -> p u t", u=2)
    hs = w[:, 4 * T:6 * T].rearrange("p (u t) -> p u t", u=2)
    y = w[:, 6 * T:8 * T].rearrange("p (u t) -> p u t", u=2)
    ig = w[0:S, 8 * T:10 * T].rearrange("p (u t) -> p u t", u=2)
    fg = w[0:S, 10 * T:12 * T].rearrange("p (u t) -> p u t", u=2)
    drive = w[0:S, 12 * T:14 * T].rearrange("p (u t) -> p u t", u=2)
    bank = lambda u, i: s.bank(4 * u + i)
    start_counters(nc, counters)
    block = ctx.enter_context(nc.Block())

    @block.tensor
    def _(pe):
        norm_pe(pe, s, done)
        pe.wait_ge(zeroed, ONE + 1)
        with pe.Fori(0, B // 2) as pair:
            b = pair * 2
            for u in range(2):
                pe.wait_ge(s.normed, ONE + b + (done + u + 1))
                pe.wait_ge(gated, ONE + b * 2)
                pe.matmul(bank(u, 0), s.W_in, s.xn[:, batch(b + u)], start=True, stop=True).then_inc(xp_mm, 1)
            for u in range(2):
                pe.wait_ge(xp_ready, ONE + b + (u + 1))
                pe.wait_ge(drive_ready, ONE + b)
                pe.matmul(bank(u, 1), s.W_B, xp[:, u, :], start=True, stop=True).then_inc(t_ready, 1)
                pe.wait_ge(centered, ONE + b)
                pe.matmul(bank(u, 2)[0:S, :], s.W_ig, xp[:, u, :], start=True, stop=True)
                pe.matmul(bank(u, 0)[0:S, :], s.W_fg, xp[:, u, :], start=True, stop=True).then_inc(gates_ready, 1)
                pe.wait_ge(var_kept, ONE + b)
                pe.matmul(bank(u, 3), s.W_D, xp[:, u, :], start=True, stop=False)
            for u in range(2):
                pe.wait_ge(tb_ready, ONE + b + (u + 1))
                pe.matmul(bank(u, 1)[0:S, :], s.B_mat, tb[:, u, :], start=True, stop=True).then_inc(bx_ready, 1)
            for u in range(2):
                pe.wait_ge(states_ready, ONE + b + (u + 1))
                pe.matmul(bank(u, 3), s.C_mat, hs[:, u, :], start=False, stop=True).then_inc(pre_ready, 1)
            for u in range(2):
                pe.wait_ge(tanh_ready, ONE + b + (u + 1))
                pe.matmul(bank(u, 3), s.W_out, y[:, u, :], start=True, stop=True).then_inc(y_ready, 1)
            for u in range(2):
                pe.wait_ge(res_ready, ONE + b + (u + 1))
                pe.wait_ge(gated, ONE + b * 2 + (2 * u + 2))
                pe.matmul(bank(u, 2), s.avg, s.xn[:, batch(b + u)], start=True, stop=True).then_inc(mean_ready, 1)
            for u in range(2):
                pe.wait_ge(squared, ONE + b + (u + 1))
                pe.matmul(bank(u, 3), s.avg, s.sq[:, u, :], start=True, stop=True).then_inc(var_ready, 1)

    @block.scalar
    def _(act):
        norm_act(act, s, done)
        with act.Fori(0, B // 2) as pair:
            b = pair * 2
            for u in range(2):
                act.wait_ge(xp_mm, ONE + b + (u + 1))
                act.wait_ge(res_ready, ONE + b)
                act.activation(xp[:, u, :], bank(u, 0), ACT.Identity, bias=s.b_in).then_inc(xp_ready, 1)
            for u in range(2):
                act.wait_ge(t_ready, ONE + b + (u + 1))
                act.wait_ge(bx_ready, ONE + b)
                act.activation(tb[:, u, :], bank(u, 1), ACT.Identity, bias=s.b_B).then_inc(tb_ready, 1)
            for u in range(2):
                act.wait_ge(gates_ready, ONE + b + (u + 1))
                act.wait_ge(states_ready, ONE + b)
                act.activation(ig[:, u, :], bank(u, 2)[0:S, :], ACT.Sigmoid, bias=s.b_ig).then_inc(gated, 1)
                act.activation(fg[:, u, :], bank(u, 0)[0:S, :], ACT.Sigmoid, bias=s.b_fg).then_inc(gated, 1)
            for u in range(2):
                act.wait_ge(pre_ready, ONE + b + (u + 1))
                act.wait_ge(y_ready, ONE + b)
                act.activation(y[:, u, :], bank(u, 3), ACT.Tanh, bias=s.b_D).then_inc(tanh_ready, 1)
            for u in range(2):
                act.wait_ge(centered, ONE + b + (u + 1))
                act.wait_ge(var_ready, ONE + b)
                act.activation(s.sq[:, u, :], s.xn[:, batch(b + u)], ACT.Square).then_inc(squared, 1)
            for u in range(2):
                act.wait_ge(var_ready, ONE + b + (u + 1))
                act.wait_ge(s.normed, ONE + b + (done + u + 1))
                act.activation(s.rs[:, batch(b + u)], bank(u, 3), ACT.Identity).then_inc(var_kept, 1)
        act.wait_ge(var_kept, ONE + B)
        act.activation(s.rs[:, :], s.rs[:, :], ACT.Ln, bias=s.eps[:, 0:1]).then_inc(ln_done, 1)
        act.wait_ge(ln_done, ONE + 1)
        for b in range(B):
            act.activation(s.rs[:, batch(b)], s.rs[:, batch(b)], ACT.Exp, scale=-0.5).then_inc(rstd, 1)

    @block.vector
    def _(dve):
        dve.memset(hs, 0.0).then_inc(zeroed, 1)
        norm_dve(dve, s, done)
        with dve.Fori(0, B // 2) as pair:
            b = pair * 2
            for u in range(2):
                dve.wait_ge(bx_ready, ONE + b + (u + 1))
                dve.wait_ge(gated, ONE + b * 2 + (2 * u + 2))
                dve.wait_ge(states_ready, ONE + b + u)
                dve.tensor_tensor(drive[:, u, :], bank(u, 1)[0:S, :], ig[:, u, :], ALU.mult).then_inc(drive_ready, 1)
                dve.wait_ge(drive_ready, ONE + b + (u + 1))
                dve.wait_ge(pre_ready, ONE + b)
                dve.tensor_tensor_scan(hs[0:S, u, :], fg[:, u, :], drive[:, u, :], 0.0, ALU.mult, ALU.add).then_inc(states_ready, 1)
            for u in range(2):
                dve.wait_ge(y_ready, ONE + b + (u + 1))
                dve.scalar_tensor_tensor(s.xn[:, batch(b + u)], bank(u, 3), s.b_out, xp[:, u, :], ALU.add, ALU.add).then_inc(res_ready, 1)
            for u in range(2):
                dve.wait_ge(mean_ready, ONE + b + (u + 1))
                dve.wait_ge(res_ready, ONE + b + (u + 1))
                dve.tensor_tensor(s.xn[:, batch(b + u)], s.xn[:, batch(b + u)], bank(u, 2), ALU.subtract).then_inc(centered, 1)
        for b in range(B):
            dve.wait_ge(rstd, ONE + b + 1)
            dve.wait_ge(centered, ONE + b + 1)
            dve.scalar_tensor_tensor(s.xn[:, batch(b)], s.xn[:, batch(b)], s.gamma, s.rs[:, batch(b)], ALU.mult, ALU.mult).then_inc(scaled, 1)
            dve.wait_ge(scaled, ONE + b + 1)
            dve.scalar_tensor_tensor(s.x[:, batch(b)], s.xn[:, batch(b)], s.beta, s.x[:, batch(b)], ALU.add, ALU.add).then_inc(x_added, 1)
        dve.wait_ge(x_added, ONE + B)
    return counters



def rwkv_layer(nc, s, ctx, done, tag):
    counters = []

    def sem(name):
        counters.append(nc.alloc_semaphore(name=f"{tag}_{name}"))
        return counters[-1]

    NEG = -1e38
    shifted, delta_ready, mixed, krv_ready = sem("shifted"), sem("delta"), sem("mixed"), sem("krv_ready")
    max_ready, peak_ready, exponents, exps = sem("max_ready"), sem("peak_ready"), sem("exponents"), sem("exps")
    kv_ready, sums_ready, r_ready = sem("kv_ready"), sem("sums_ready"), sem("r_ready")
    parts, num_ready, den_ready, gated = sem("parts"), sem("num_ready"), sem("den_ready"), sem("gated")
    consts, den_log, inv_ready, wkv_ready, out_ready, x_added = (
        sem("consts"), sem("den_log"), sem("inv_ready"), sem("wkv_ready"), sem("out_ready"), sem("x_added"))
    at = [0]

    def buf(n):
        a = at[0]
        at[0] += n
        return s.work[:, a:a + n]

    def two(n):
        return buf(2 * n).rearrange("p (u t) -> p u t", u=2)

    last, delta = two(T), two(T)
    xk, xv, xr = two(T), two(T), two(T)
    m, A, Z = two(T + 1), two(T + 1), two(T + 1)
    E = buf(2 * 4 * T).rearrange("p (u n t) -> p u n t", u=2, n=4)
    kv, peak, th = two(T), two(T), two(T)
    negw_row = buf(T)
    c = buf(2)
    neg_w, w_pos = c[:, 0:1], c[:, 1:2]
    bank = lambda u, i: s.bank(4 * u + i)
    start_counters(nc, counters)
    block = ctx.enter_context(nc.Block())

    @block.tensor
    def _(pe):
        norm_pe(pe, s, done)
        with pe.Fori(0, B // 2) as pair:
            b = pair * 2
            for u in range(2):
                pe.wait_ge(mixed, ONE + b * 3 + (3 * u + 3))
                pe.wait_ge(num_ready, ONE + b)
                pe.matmul(bank(u, 0), s.W_key, xk[:, u, :], start=True, stop=True)
                pe.matmul(bank(u, 1), s.W_value, xv[:, u, :], start=True, stop=True)
                pe.matmul(bank(u, 2), s.W_receptance, xr[:, u, :], start=True, stop=True).then_inc(krv_ready, 1)
        with pe.Fori(0, B // 2) as pair:
            b = pair * 2
            for u in range(2):
                pe.wait_ge(wkv_ready, ONE + b + (u + 1))
                pe.wait_ge(x_added, ONE + b)
                pe.matmul(bank(u, 3), s.W_output, s.xn[:, batch(b + u)], start=True, stop=True).then_inc(out_ready, 1)

    @block.scalar
    def _(act):
        norm_act(act, s, done)
        act.activation(w_pos, s.time_decay, ACT.Exp).then_inc(consts, 1)
        with act.Fori(0, B // 2) as pair:
            b = pair * 2
            for u in range(2):
                act.wait_ge(s.normed, ONE + b + (done + u + 1))
                act.wait_ge(mixed, ONE + b * 3)
                act.wait_ge(consts, ONE + 3)
                act.activation(last[:, u, 1:T], s.xn[:, bass.ds((b + u) * T, T - 1)], ACT.Copy).then_inc(shifted, 1)
            for u in range(2):
                act.wait_ge(exponents, ONE + b * 4 + (4 * u + 4))
                act.activation(E[:, u, :, :], E[:, u, :, :], ACT.Exp).then_inc(exps, 1)
            for u in range(2):
                act.wait_ge(krv_ready, ONE + b + (u + 1))
                act.wait_ge(num_ready, ONE + b)
                act.activation(th[:, u, :], bank(u, 2), ACT.Tanh, scale=0.5).then_inc(r_ready, 1)
        act.wait_ge(den_ready, ONE + B)
        act.activation(s.rs[:, :], s.rs[:, :], ACT.Ln).then_inc(den_log, 1)
        act.wait_ge(den_log, ONE + 1)
        for b in range(B):
            act.activation(s.rs[:, batch(b)], s.rs[:, batch(b)], ACT.Exp, scale=-1.0).then_inc(inv_ready, 1)

    @block.vector
    def _(dve):
        dve.memset(last[:, :, 0:1], 0.0)
        dve.memset(A[:, :, 0:1], 0.0)
        dve.memset(Z[:, :, 0:1], 0.0)
        dve.memset(m[:, :, 0:1], NEG).then_inc(consts, 1)
        dve.memset(negw_row, 0.0).then_inc(consts, 1)
        norm_dve(dve, s, done)
        dve.wait_ge(consts, ONE + 3)
        dve.tensor_scalar(negw_row, negw_row, w_pos, None, ALU.subtract).then_inc(consts, 1)
        dve.tensor_scalar(neg_w, w_pos, -1.0, None, ALU.mult).then_inc(consts, 1)
        with dve.Fori(0, B // 2) as pair:
            b = pair * 2
            for u in range(2):
                xb = s.xn[:, batch(b + u)]
                dve.wait_ge(shifted, ONE + b + (u + 1))
                dve.wait_ge(mixed, ONE + b * 3)
                dve.tensor_tensor(delta[:, u, :], xb, last[:, u, :], ALU.subtract).then_inc(delta_ready, 1)
                dve.wait_ge(delta_ready, ONE + b + (u + 1))
                dve.wait_ge(krv_ready, ONE + b)
                for out, mix in ((xk, s.mix_k), (xv, s.mix_v), (xr, s.mix_r)):
                    dve.scalar_tensor_tensor(out[:, u, :], delta[:, u, :], mix, last[:, u, :], ALU.mult, ALU.add).then_inc(mixed, 1)
            for u in range(2):
                k, before, now = bank(u, 0), m[:, u, 0:T], m[:, u, 1:T + 1]
                dve.wait_ge(consts, ONE + 5)
                dve.wait_ge(krv_ready, ONE + b + (u + 1))
                dve.wait_ge(num_ready, ONE + b)
                dve.tensor_tensor_scan(now, negw_row, k, NEG, ALU.add, ALU.max).then_inc(max_ready, 1)
                dve.wait_ge(max_ready, ONE + b + (u + 1))
                dve.scalar_tensor_tensor(peak[:, u, :], k, s.time_first, before, ALU.add, ALU.max).then_inc(peak_ready, 1)
                dve.tensor_tensor(E[:, u, 0, :], k, now, ALU.subtract).then_inc(exponents, 1)
                dve.scalar_tensor_tensor(E[:, u, 1, :], before, neg_w, now, ALU.add, ALU.subtract).then_inc(exponents, 1)
                dve.wait_ge(peak_ready, ONE + b + (u + 1))
                dve.scalar_tensor_tensor(E[:, u, 2, :], k, s.time_first, peak[:, u, :], ALU.add, ALU.subtract).then_inc(exponents, 1)
                dve.tensor_tensor(E[:, u, 3, :], before, peak[:, u, :], ALU.subtract).then_inc(exponents, 1)
            for u in range(2):
                v = bank(u, 1)
                ek, decay, own, past = (E[:, u, n, :] for n in range(4))
                dve.wait_ge(exps, ONE + b + (u + 1))
                dve.tensor_tensor(kv[:, u, :], ek, v, ALU.mult).then_inc(kv_ready, 1)
                dve.tensor_tensor_scan(Z[:, u, 1:T + 1], decay, ek, 0.0, ALU.mult, ALU.add).then_inc(sums_ready, 1)
                dve.wait_ge(kv_ready, ONE + b + (u + 1))
                dve.tensor_tensor_scan(A[:, u, 1:T + 1], decay, kv[:, u, :], 0.0, ALU.mult, ALU.add).then_inc(sums_ready, 1)
                dve.wait_ge(sums_ready, ONE + b * 2 + (2 * u + 2))
                dve.tensor_tensor(kv[:, u, :], past, Z[:, u, 0:T], ALU.mult).then_inc(parts, 1)
                dve.tensor_tensor(peak[:, u, :], past, A[:, u, 0:T], ALU.mult).then_inc(parts, 1)
                dve.tensor_tensor(ek, own, v, ALU.mult).then_inc(parts, 1)
                dve.wait_ge(parts, ONE + b * 4 + (4 * u + 1))
                dve.tensor_tensor(s.rs[:, batch(b + u)], own, kv[:, u, :], ALU.add).then_inc(den_ready, 1)
                dve.wait_ge(parts, ONE + b * 4 + (4 * u + 3))
                dve.tensor_tensor(peak[:, u, :], peak[:, u, :], ek, ALU.add).then_inc(parts, 1)
                dve.wait_ge(r_ready, ONE + b + (u + 1))
                dve.wait_ge(parts, ONE + b * 4 + (4 * u + 4))
                dve.wait_ge(mixed, ONE + b * 3 + (3 * u + 3))
                dve.scalar_tensor_tensor(s.xn[:, batch(b + u)], th[:, u, :], 1.0, peak[:, u, :], ALU.add, ALU.mult).then_inc(num_ready, 1)
        dve.wait_ge(num_ready, ONE + B)
        for b in range(B):
            dve.wait_ge(inv_ready, ONE + b + 1)
            dve.scalar_tensor_tensor(s.xn[:, batch(b)], s.xn[:, batch(b)], 0.5, s.rs[:, batch(b)], ALU.mult, ALU.mult).then_inc(wkv_ready, 1)
        for b in range(B):
            dve.wait_ge(out_ready, ONE + b + 1)
            dve.tensor_tensor(s.x[:, batch(b)], s.x[:, batch(b)], bank(b % 2, 3), ALU.add).then_inc(x_added, 1)
        dve.wait_ge(x_added, ONE + B)
    return counters



HEADS, KV, HD = 16, 4, 8
QUAD = HEADS // KV
TILES = T // P
SLOTS = [(i, j) for i in range(3) for j in range(3)]
BIAS_ROW = len(SLOTS) * HD
MAX_ROW = 96


def gqa_layer(nc, s, ctx, done, tag):
    counters = []

    def sem(name):
        counters.append(nc.alloc_semaphore(name=f"{tag}_{name}"))
        return counters[-1]

    misc_ready, misc_read = sem("misc_ready"), sem("misc_read")
    tables = sem("tables")
    split = sem("split")
    scores_ready, scores_read = sem("scores_ready"), sem("scores_read")
    cut, max_cut = sem("cut"), sem("max_cut")
    keyed_ready, exp_ready, pv_ready = sem("keyed_ready"), sem("exp_ready"), sem("pv_ready")
    raw_ready, inv_ready, xv_ready = sem("raw_ready"), sem("inv_ready"), sem("xv_ready")
    zeroed = sem("zeroed")

    at = [0]

    def f32(n):
        a = at[0]
        at[0] += n
        return s.work[:, a:a + n]

    def bf16(n):
        return f32(n // 2).bitcast(BF16)

    sel = bf16(GQA_BF16_COLS)
    sel_q = sel[:, 0:HEADS * 3 * P].rearrange("p (h i r) -> p h i r", h=HEADS, i=3)
    sel_k = sel[:, HEADS * 3 * P:(HEADS + KV) * 3 * P].rearrange("p (h i r) -> p h i r", h=KV, i=3)
    ident_b = sel[:, (HEADS + KV) * 3 * P:(HEADS + KV) * 3 * P + P]
    parts = bf16(6 * T).rearrange("p (a i t) -> p a i t", a=2, i=3)
    rest = f32(2 * T).rearrange("p (a t) -> p a t", a=2)
    qop = bf16(HEADS * T).rearrange("p (q i t) -> p q i t", q=KV, i=QUAD)
    kop = bf16(KV * T).rearrange("p (g t) -> p g t", g=KV)
    vaug = f32(TILES * KV * 32).rearrange("p (n g c) -> p n g c", n=TILES, g=KV)
    mx = f32(2 * 16).rearrange("p (a n) -> p a n", a=2)
    mrest = f32(2 * 16).rearrange("p (a n) -> p a n", a=2)
    mrow = bf16(2 * 16 * 32).rearrange("p (a n c) -> p a n c", a=2, n=16)
    E = f32(2 * QUAD * T).rearrange("p (a i t) -> p a i t", a=2, i=QUAD)
    raw = f32(T)
    inv = f32(16)
    on = f32(T).rearrange("p (n h d) -> p n h d", n=TILES, h=HEADS)
    oT = f32(T)
    xv = oT
    assert at[0] <= s.work.shape[1]
    misc, pv = s.bank(7), s.bank(6)

    uses = (["q", "k", "v"] + [("ksel", g) for g in range(KV)] + [("qsel", 0, i) for i in range(QUAD)]
            + [("qsel", 1, i) for i in range(QUAD)])
    for q in range(KV):
        uses += [("qsel", q + 2, i) for i in range(QUAD) if q + 2 < KV] + [("turn", q)]
    uses += ["back", "out"]
    use = {name: n for n, name in enumerate(uses)}
    U = len(uses)
    RING = 16 + QUAD
    SPLITS = 6
    start_counters(nc, counters)
    block = ctx.enter_context(nc.Block())

    @block.sync
    def _(sp):
        sp.dma_start(sel, s.gqa_tables).then_inc(tables, 16)
        sp.wait_ge(tables, ONE + 16)

    @block.tensor
    def _(pe):
        norm_pe(pe, s, done)
        pe.wait_ge(tables, ONE + 16)
        pe.wait_ge(zeroed, ONE + 3)
        with pe.Fori(0, B) as b:
            def misc_free(name):
                pe.wait_ge(misc_read, ONE + b * U + use[name])

            def qsel(q, i):
                misc_free(("qsel", q, i))
                pe.wait_ge(split, ONE + b * SPLITS + SPLITS)
                for n in range(3):
                    mm = pe.matmul(misc, sel_q[:, q * QUAD + i, n, :], parts[:, 0, n, :], start=n == 0, stop=n == 2)
                mm.then_inc(misc_ready, 1)

            def scores(q, n):
                r = q * RING + n
                i, qt = n // TILES, n % TILES
                if qt == 0:
                    pe.wait_ge(misc_read, ONE + b * U + (use[("qsel", q, i)] + 1))
                if r >= 2:
                    pe.wait_ge(scores_read, ONE + b * (KV * RING) + (r - 1))
                else:
                    pe.wait_ge(scores_read, ONE + b * (KV * RING))
                pe.matmul(s.bank(r % 2), qop[:, q, i, qt * P:(qt + 1) * P], kop[:, q, :],
                          start=True, stop=True).then_inc(scores_ready, 1)

            def max_rows(q):
                pe.wait_ge(max_cut, ONE + b * KV + (q + 1))
                for i in range(QUAD):
                    r = q * RING + 16 + i
                    pe.wait_ge(scores_read, ONE + b * (KV * RING) + (r - 1))
                    for qt in range(TILES):
                        mm = pe.matmul(s.bank(r % 2)[MAX_ROW:P, qt * P:(qt + 1) * P], mrow[:, q % 2, 4 * i + qt, :],
                                       ident_b, start=True, stop=True)
                    mm.then_inc(scores_ready, 1)

            def keyed(q, kt, half):
                g = q * 8 + kt * 2 + half
                pe.wait_ge(scores_read, ONE + b * (KV * RING) + (q * RING + 16 + 2 * half + 2))
                if g >= 2:
                    pe.wait_ge(exp_ready, ONE + b * 32 + (g - 1))
                else:
                    pe.wait_ge(exp_ready, ONE + b * 32)
                for j in range(2):
                    mm = pe.matmul(s.bank(2 + 2 * half + j), kop[:, q, kt * P:(kt + 1) * P],
                                   qop[:, q, 2 * half + j, :], start=True, stop=True)
                mm.then_inc(keyed_ready, 1)

            def values(q, kt):
                pe.wait_ge(exp_ready, ONE + b * 32 + (q * 8 + kt * 2 + 2))
                if kt == 0:
                    pe.wait_ge(raw_ready, ONE + b * KV + q)
                for i in range(QUAD):
                    mm = pe.matmul(pv[32 * i:32 * i + 32, :], vaug[:, kt, q, :], E[:, kt % 2, i, :],
                                   start=kt == 0, stop=kt == TILES - 1)
                mm.then_inc(pv_ready, 1)

            pe.wait_ge(s.normed, ONE + b + (done + 1))
            misc_free("q")
            pe.matmul(misc, s.Wq, s.xn[:, batch(b)], start=True, stop=True).then_inc(misc_ready, 1)
            misc_free("k")
            pe.matmul(misc, s.Wk, s.xn[:, batch(b)], start=True, stop=True).then_inc(misc_ready, 1)
            misc_free("v")
            pe.wait_ge(xv_ready, ONE + b + 1)
            for n in range(TILES):
                mm = pe.matmul(misc[:, 32 * n:32 * n + 32], xv[:, n * P:(n + 1) * P], s.Wv, start=True, stop=True)
            mm.then_inc(misc_ready, 1)
            for g in range(KV):
                misc_free(("ksel", g))
                pe.wait_ge(split, ONE + b * SPLITS + SPLITS)
                for n in range(3):
                    mm = pe.matmul(misc, sel_k[:, g, n, :], parts[:, 1, n, :], start=n == 0, stop=n == 2)
                mm.then_inc(misc_ready, 1)
            for i in range(QUAD):
                qsel(0, i)
            pe.wait_ge(misc_read, ONE + b * U + use[("qsel", 0, 0)])
            for n in range(16):
                scores(0, n)
            for i in range(QUAD):
                qsel(1, i)
            max_rows(0)
            for q in range(KV):
                for n in range(16):
                    if q + 1 < KV:
                        scores(q + 1, n)
                    if n % 2 == 0:
                        keyed(q, n // 4, n // 2 % 2)
                    if n % 4 == 2 and q + 2 < KV:
                        qsel(q + 2, n // 4)
                    if n % 4 == 3 and n > 4:
                        values(q, n // 4 - 1)
                values(q, TILES - 1)
                if q + 1 < KV:
                    max_rows(q + 1)
                pe.wait_ge(raw_ready, ONE + b * KV + (q + 1))
                misc_free(("turn", q))
                for n in range(TILES):
                    mm = pe.transpose(misc[:, n * P:(n + 1) * P], raw[:, n * P:(n + 1) * P], s.ident)
                mm.then_inc(misc_ready, 1)
            misc_free("back")
            for n in range(TILES):
                mm = pe.transpose(misc[:, n * P:(n + 1) * P], on[:, n, :, :].rearrange("p h d -> p (h d)"), s.ident)
            mm.then_inc(misc_ready, 1)
            misc_free("out")
            pe.matmul(misc, s.Wo, oT, start=True, stop=True).then_inc(misc_ready, 1)

    @block.scalar
    def _(act):
        norm_act(act, s, done)
        with act.Fori(0, B) as b:
            def qsel(q, i):
                n = use[("qsel", q, i)]
                act.wait_ge(misc_ready, ONE + b * U + (n + 1))
                act.wait_ge(keyed_ready, ONE + b * 32)
                act.activation(qop[:, q, i, :], misc, ACT.Identity,
                               bias=s.slopes[:, q * QUAD + i:q * QUAD + i + 1]).then_inc(misc_read, 1)

            act.wait_ge(s.normed, ONE + b + (done + 1))
            act.wait_ge(misc_read, ONE + b * U)
            act.activation(xv, s.xn[:, batch(b)], ACT.Copy).then_inc(xv_ready, 1)
            for i in range(QUAD):
                qsel(0, i)
            for i in range(QUAD):
                qsel(1, i)
            for q in range(KV):
                for n in range(0, 16, 2):
                    kt, half, g = n // 4, n // 2 % 2, q * 8 + n // 2
                    act.wait_ge(keyed_ready, ONE + b * 32 + (g + 1))
                    act.wait_ge(pv_ready, ONE + b * 16 + max(0, 4 * q + kt - 1))
                    act.activation(E[:, kt % 2, 2 * half:2 * half + 2, :], s.psum[:, 2 + 2 * half:4 + 2 * half, :],
                                   ACT.Exp).then_inc(exp_ready, 1)
                    if n % 4 == 2 and q + 2 < KV:
                        qsel(q + 2, n // 4)
                act.wait_ge(pv_ready, ONE + b * 16 + 4 * q + 4)
                act.wait_ge(misc_ready, ONE + b * U + (use[("turn", q - 1)] + 1 if q else 0))
                act.activation(raw, pv, ACT.Copy).then_inc(raw_ready, 1)

    @block.vector
    def _(dve):
        dve.memset(mrow, 0.0).then_inc(zeroed, 1)
        dve.memset(vaug, 0.0).then_inc(zeroed, 1)
        dve.wait_ge(zeroed, ONE + 2)
        dve.memset(vaug[:, :, :, HD:HD + 1], 1.0).then_inc(zeroed, 1)
        norm_dve(dve, s, done)
        dve.wait_ge(zeroed, ONE + 3)
        with dve.Fori(0, B) as b:
            def misc_there(name):
                dve.wait_ge(misc_ready, ONE + b * U + (use[name] + 1))

            dve.wait_ge(split, ONE + b * SPLITS)
            for a, name, scale in ((0, "q", HD ** -0.5), (1, "k", 1.0)):
                misc_there(name)
                dve.tensor_scalar(parts[:, a, 0, :], misc, scale, None, ALU.mult).then_inc(split, 1)
                dve.wait_ge(split, ONE + b * SPLITS + (3 * a + 1))
                dve.scalar_tensor_tensor(rest[:, a, :], misc, scale, parts[:, a, 0, :], ALU.mult, ALU.subtract).then_inc(misc_read, 1)
                dve.wait_ge(misc_read, ONE + b * U + (use[name] + 1))
                dve.tensor_copy(parts[:, a, 1, :], rest[:, a, :]).then_inc(split, 1)
                dve.wait_ge(split, ONE + b * SPLITS + (3 * a + 2))
                dve.tensor_tensor(parts[:, a, 2, :], rest[:, a, :], parts[:, a, 1, :], ALU.subtract).then_inc(split, 1)
            misc_there("v")
            dve.wait_ge(pv_ready, ONE + b * 16)
            dve.tensor_copy(vaug[:, :, :, 0:HD], misc[:, 0:TILES * 32].rearrange("p (n g d) -> p n g d", n=TILES, g=KV)).then_inc(misc_read, 1)
            for g in range(KV):
                misc_there(("ksel", g))
                dve.tensor_tensor(kop[:, g, :], misc, s.key_rows, ALU.add).then_inc(misc_read, 1)

            def maxima(q):
                for n in range(16):
                    dve.wait_ge(scores_ready, ONE + b * (KV * RING) + (q * RING + n + 1))
                    dve.tensor_reduce(mx[:, q % 2, n:n + 1], s.bank((q * RING + n) % 2), AX.X, ALU.max).then_inc(scores_read, 1)

            def max_parts(q):
                m, r, c = mx[:, q % 2, :], mrest[:, q % 2, :], b * (3 * KV) + 3 * q
                dve.wait_ge(scores_read, ONE + b * (KV * RING) + (q * RING + 16))
                dve.tensor_scalar(mrow[:, q % 2, :, 0], m, -1.0, None, ALU.mult).then_inc(cut, 1)
                dve.wait_ge(cut, ONE + c + 1)
                dve.scalar_tensor_tensor(r, m, -1.0, mrow[:, q % 2, :, 0], ALU.mult, ALU.subtract).then_inc(cut, 1)
                dve.wait_ge(cut, ONE + c + 2)
                dve.tensor_copy(mrow[:, q % 2, :, 1], r).then_inc(cut, 1)
                dve.wait_ge(cut, ONE + c + 3)
                dve.tensor_tensor(mrow[:, q % 2, :, 2], r, mrow[:, q % 2, :, 1], ALU.subtract).then_inc(max_cut, 1)

            def max_rows(q):
                for i in range(QUAD):
                    r = q * RING + 16 + i
                    dve.wait_ge(scores_ready, ONE + b * (KV * RING) + (r + 1))
                    dve.tensor_copy(qop[MAX_ROW:P, q, i, :], s.bank(r % 2)[MAX_ROW:P, :]).then_inc(scores_read, 1)

            maxima(0)
            max_parts(0)
            max_rows(0)
            for q in range(KV):
                if q + 1 < KV:
                    maxima(q + 1)
                    max_parts(q + 1)
                    max_rows(q + 1)
                misc_there(("turn", q))
                turned = misc.rearrange("p (n i c) -> p n i c", n=TILES, i=QUAD)
                dve.wait_ge(misc_read, ONE + b * U + use[("turn", q)])
                dve.reciprocal(inv.rearrange("p (n i) -> p n i", n=TILES), turned[:, :, :, HD]).then_inc(inv_ready, 1)
                dve.wait_ge(inv_ready, ONE + b * KV + (q + 1))
                for n in range(TILES):
                    last = dve.tensor_tensor(on[:, n, q * QUAD:(q + 1) * QUAD, :], turned[:, n, :, 0:HD],
                                             inv[:, 4 * n:4 * n + 4].unsqueeze(2).to_broadcast([P, QUAD, HD]), ALU.mult)
                last.then_inc(misc_read, 1)
            misc_there("back")
            dve.tensor_copy(oT, misc).then_inc(misc_read, 1)
            misc_there("out")
            dve.tensor_tensor(s.x[:, batch(b)], s.x[:, batch(b)], misc, ALU.add).then_inc(misc_read, 1)
        dve.wait_ge(misc_read, ONE + B * U)
    return counters



IH, ID = 16, 64
SEG = 32
SEGS = T // SEG
CH = IH * ID // P
G = 4
MW = ID + 1
SWAP = [i ^ 1 for i in range(32)]


def infini_layer(nc, s, ctx, done, tag):
    counters = []

    def sem(name):
        counters.append(nc.alloc_semaphore(name=f"{tag}_{name}"))
        return counters[-1]

    affine = sem("affine")
    proj_ready, proj_read, exp_ready, capped = sem("proj_ready"), sem("proj_read"), sem("exp_ready"), sem("capped")
    rot_ready, cos_ready, sin_ready, roped = sem("rot_ready"), sem("cos_ready"), sem("sin_ready"), sem("roped")
    scores_ready, masked, row_max, shifted = sem("scores_ready"), sem("masked"), sem("row_max"), sem("shifted")
    sm_exp, row_sum, weight_ready, probs, turned = (
        sem("sm_exp"), sem("row_sum"), sem("weight"), sem("probs"), sem("turned"))
    v_ready, v_kept = sem("v_ready"), sem("v_kept")
    skt_ready, skt_kept = sem("skt_ready"), sem("skt_kept")
    recall_k, recall_q, k_inv, prev_ready, d_dve, d_pool = (
        sem("recall_k"), sem("recall_q"), sem("k_inv"), sem("prev"), sem("d_dve"), sem("d_pool"))
    updated, state_ready = sem("updated"), sem("state_ready")
    q_den, q_out, pv_ready, o_ready, ot_ready, ot_kept = (
        sem("q_den"), sem("q_out"), sem("pv_ready"), sem("o_ready"), sem("ot_ready"), sem("ot_kept"))
    out_ready, x_added, consts, beta_ready = sem("out_ready"), sem("x_added"), sem("consts"), sem("beta_ready")

    at = [0]

    def f32(n):
        a = at[0]
        at[0] += n
        return s.work[:, a:a + n]

    sq = f32(CH * T).rearrange("p (c t) -> p c t", c=CH)
    sk = f32(CH * T).rearrange("p (c t) -> p c t", c=CH)
    v = f32(SEGS * 256).rearrange("p (t n) -> p t n", t=SEGS)
    state = f32(CH * 2 * MW).rearrange("p (c n) -> p c n", c=CH)
    PT = f32(SEGS * 4 * SEG).rearrange("p (n m) -> p n m", n=4)
    D = f32(16 * MW).rearrange("p (a g n) -> p a g n", a=4, g=G)
    ones_z = f32(G * MW)
    z0 = f32(ID)
    xa = f32(T)
    betas = f32(8)
    beta, gain = betas[:, 0:4], betas[:, 4:8]
    start = at[0]
    e_buf = f32(2 * T).rearrange("p (a t) -> p a t", a=2)
    rot = f32(2 * T).rearrange("p (a t) -> p a t", a=2)
    tc = f32(2 * T).rearrange("p (a t) -> p a t", a=2)
    zr = f32(4 * T).rearrange("p (a t) -> p a t", a=4)
    stat = f32(3 * 64).rearrange("p (a n) -> p a n", a=3)
    end = at[0]
    at[0] = start
    skt = f32(2 * 256).rearrange("p (a n) -> p a n", a=2)
    prev = f32(256).rearrange("p (n d) -> p n d", n=4)
    mo = f32(256).rearrange("p (n d) -> p n d", n=4)
    o = f32(2 * 256).rearrange("p (a n) -> p a n", a=2)
    small = f32(16)
    assert max(end, at[0]) <= s.work.shape[1]
    sm = s.rs[:, 0:4 * T].rearrange("p (n m) -> p n m", n=4)
    oT = s.rs[:, 0:CH * T].rearrange("p (c t) -> p c t", c=CH)
    wq = lambda c: s.w_qkv[:, c * P:(c + 1) * P]
    wk = lambda c: s.w_qkv[:, (CH + c) * P:(CH + c + 1) * P]
    wv = s.w_qkv[:, 2 * CH * P:3 * CH * P].rearrange("p (j g n) -> p g j n", j=2, g=G)
    tok = lambda t: slice(t * SEG, (t + 1) * SEG)
    part = lambda g: slice(32 * g, 32 * g + 32)
    half = lambda e: slice(64 * e, 64 * e + 64)
    tile_of = lambda t, j, e: 2 * e + t // 8
    cols_of = lambda t, j: slice((t % 8 * 2 + j) * SEG, (t % 8 * 2 + j + 1) * SEG)
    DS = 4 * (SEGS - 1)
    NP = 2 * CH
    start_counters(nc, counters)
    block = ctx.enter_context(nc.Block())

    @block.tensor
    def _(pe):
        norm_pe(pe, s, done)
        norm_pe(pe, s, done + B, again=True)
        pe.wait_ge(consts, ONE + 5)
        with pe.Fori(0, B) as b:
            def scores(c):
                j, g = c // G, c % G
                for t in range(SEGS):
                    for e in range(2):
                        mm = pe.matmul(s.psum[part(g), 4 + tile_of(t, j, e), cols_of(t, j)],
                                       zr[half(e), (2 * c) % 4, tok(t)], zr[half(e), (2 * c + 1) % 4, tok(t)],
                                       start=True, stop=True)
                mm.then_inc(scores_ready, 1)

            pe.wait_ge(affine, ONE + b + 1)
            pe.wait_ge(x_added, ONE + b)
            for c in range(CH):
                for z, w in ((0, wq(c)), (1, wk(c))):
                    n = 2 * c + z
                    pe.wait_ge(proj_read, ONE + b * NP + max(0, n - 3))
                    if c and z:
                        pe.wait_ge(roped, ONE + b * NP + 2 * c)
                    pe.matmul(s.bank(n % 4), w, xa, start=True, stop=True).then_inc(proj_ready, 1)
                if c:
                    scores(c - 1)
            for n in range(SEGS // 2):
                if n == 0:
                    pe.wait_ge(roped, ONE + b * NP + NP)
                pe.wait_ge(proj_read, ONE + b * NP + NP)
                pe.wait_ge(v_kept, ONE + b * 8 + max(0, n - 1))
                for u in range(2):
                    for g in range(G):
                        mm = pe.matmul(s.bank(n % 2)[part(g), 256 * u:256 * u + 256], xa[:, tok(2 * n + u)], wv[:, g],
                                       start=True, stop=True)
                mm.then_inc(v_ready, 1)
                if n == 0:
                    scores(CH - 1)

            def keys_turned(t):
                pe.wait_ge(skt_kept, ONE + b * SEGS + t)
                for j in range(2):
                    for g in range(G):
                        mm = pe.matmul(s.bank(5)[part(g), P * j:P * j + P], sk[:, 4 * j + g, tok(t)], s.ident,
                                       start=True, stop=True)
                mm.then_inc(skt_ready, 1)

            def out_turned(t):
                pe.wait_ge(o_ready, ONE + b * SEGS + (t + 1))
                pe.wait_ge(ot_kept, ONE + b * SEGS + t)
                for j in range(2):
                    mm = pe.transpose(s.bank(6)[:, P * j:P * j + P], o[:, t % 2, P * j:P * j + P], s.ident)
                mm.then_inc(ot_ready, 1)

            pe.wait_ge(v_kept, ONE + b * 8 + 8)
            pe.wait_ge(masked, ONE + b * 4 + 4)
            for j in range(2):
                for e in range(2):
                    mm = pe.matmul(s.bank(2 + j)[half(e), 0:G * MW], z0, ones_z, start=True, stop=False, skip_group_check=True)
                mm.then_inc(updated, 1)
            keys_turned(0)
            pe.wait_ge(turned, ONE + b * 4 + 4)

            def recall(bank, at, operand, t, j, done_sem, before):
                for g in range(G):
                    if g == G - 1:
                        pe.wait_ge(*before)
                    mm = pe.matmul(bank[part(g), at:at + 2 * MW], operand[:, 4 * j + g, tok(t)],
                                   state[:, 4 * j + g, :], start=True, stop=True)
                mm.then_inc(done_sem, 1)

            def local(t, g):
                for j in range(2):
                    for e in range(2):
                        a = 2 * j + e
                        mm = pe.matmul(s.bank(4)[part(g), ID * a:ID * a + ID], PT[part(g), tile_of(t, j, e), cols_of(t, j)],
                                       v[part(g), t, ID * a:ID * a + ID], start=True, stop=True,
                                       tile_position=(32 * g, 32 * g))
                mm.then_inc(pv_ready, 1)

            for t in range(SEGS):
                for j in range(2):
                    pe.wait_ge(state_ready, ONE + b * (4 * SEGS) + (4 * t + 2 * j + 2))
                    pe.wait_ge(prev_ready, ONE + b * 32 + max(0, 2 * t + j - 1))
                    recall(s.bank(j), 0, sk, t, j, recall_k,
                           (pv_ready, ONE + b * (G * SEGS) + (G * t + 2)) if j
                           else (o_ready, ONE + b * SEGS + t))
                    local(t, 2 * j)
                    pe.wait_ge(q_out, ONE + b * SEGS + t)
                    recall(s.bank(7), j * 2 * MW, sq, t, j, recall_q,
                           (pv_ready, ONE + b * (G * SEGS) + (G * t + 2 * j + 1)))
                    local(t, 2 * j + 1)
                if t + 1 < SEGS:
                    keys_turned(t + 1)
                if t:
                    out_turned(t - 1)
                if t + 1 < SEGS:
                    for j in range(2):
                        pe.wait_ge(d_dve, ONE + b * DS + (4 * t + 2 * j + 2))
                        pe.wait_ge(d_pool, ONE + b * DS + (4 * t + 2 * j + 2))
                        pe.wait_ge(skt_kept, ONE + b * SEGS + (t + 1))
                        for e in range(2):
                            mm = pe.matmul(s.bank(2 + j)[half(e), 0:G * MW], skt[:, t % 2, P * j + 64 * e:P * j + 64 * e + 64],
                                           D[:, 2 * j + e, :, :].rearrange("p g n -> p (g n)"),
                                           start=False, stop=t == SEGS - 2, skip_group_check=True)
                        mm.then_inc(updated, 1)
            out_turned(SEGS - 1)
            pe.wait_ge(ot_kept, ONE + b * SEGS + SEGS)
            pe.wait_ge(q_out, ONE + b * SEGS + SEGS)
            for c in range(CH):
                mm = pe.matmul(s.bank(7), s.w_out[:, c * P:(c + 1) * P], oT[:, c, :], start=c == 0, stop=c == CH - 1)
            mm.then_inc(out_ready, 1)

    @block.scalar
    def _(act):
        act.activation(beta, s.mem_beta, ACT.Sigmoid).then_inc(beta_ready, 1)
        act.activation(gain, s.mem_beta, ACT.Sigmoid, scale=-1.0).then_inc(beta_ready, 1)
        norm_act(act, s, done)
        norm_act(act, s, done + B)
        with act.Fori(0, B) as b:
            for n in range(NP):
                act.wait_ge(proj_ready, ONE + b * NP + (n + 1))
                act.wait_ge(proj_read, ONE + b * NP + max(0, n - 1))
                act.wait_ge(ot_ready, ONE + b * SEGS)
                act.activation(e_buf[:, n % 2, :], s.bank(n % 4), ACT.Exp).then_inc(exp_ready, 1)
            for n in range(4):
                act.wait_ge(shifted, ONE + b * 4 + (n + 1))
                act.activation(sm[:, n, :], sm[:, n, :], ACT.Exp).then_inc(sm_exp, 1)
            for n in range(SEGS // 2):
                act.wait_ge(v_ready, ONE + b * 8 + (n + 1))
                act.activation(v[:, 2 * n:2 * n + 2, :], s.bank(n % 2).rearrange("p (u m) -> p u m", u=2), ACT.Copy).then_inc(v_kept, 1)

            def keys_kept(t):
                act.wait_ge(skt_ready, ONE + b * SEGS + (t + 1))
                act.wait_ge(updated, ONE + b * (2 * SEGS) + max(0, 2 * t))
                act.activation(skt[:, t % 2, :], s.bank(5)[:, 0:256], ACT.Copy).then_inc(skt_kept, 1)

            def out_kept(t):
                act.wait_ge(ot_ready, ONE + b * SEGS + (t + 1))
                act.activation(oT[:, :, tok(t)], s.bank(6)[:, 0:256].rearrange("p (c t) -> p c t", c=CH), ACT.Copy).then_inc(ot_kept, 1)

            act.wait_ge(sin_ready, ONE + b * NP + NP)
            act.wait_ge(roped, ONE + b * NP + NP)
            act.wait_ge(scores_ready, ONE + b * CH + CH)
            act.wait_ge(turned, ONE + b * 4 + 4)
            for t in range(SEGS):
                for j in range(2):
                    act.wait_ge(updated, ONE + b * (2 * SEGS) + (2 * t + j + 1))
                    if t:
                        act.wait_ge(recall_q, ONE + b * (2 * SEGS) + (2 * t - 1 + j))
                    else:
                        act.wait_ge(recall_q, ONE + b * (2 * SEGS))
                    for e in range(2):
                        act.activation(state[half(e), 4 * j:4 * j + 4, MW * e:MW * e + MW],
                                       s.bank(2 + j)[half(e), 0:G * MW].rearrange("p (g n) -> p g n", g=G),
                                       ACT.Copy).then_inc(state_ready, 1)
                keys_kept(t)
                if t > 1:
                    out_kept(t - 2)
            out_kept(SEGS - 2)
            out_kept(SEGS - 1)

    @block.gpsimd
    def _(pool):
        with pool.Fori(0, B) as b:
            for n in range(NP):
                pool.wait_ge(rot_ready, ONE + b * NP + (n + 1))
                pool.tensor_tensor(rot[:, n % 2, :], rot[:, n % 2, :], s.rope_sin, ALU.mult).then_inc(sin_ready, 1)
            for n in range(4):
                pool.wait_ge(row_max, ONE + b * 4 + (n + 1))
                pool.tensor_tensor(sm[:, n, :].rearrange("p (a k) -> p a k", k=SEG), sm[:, n, :].rearrange("p (a k) -> p a k", k=SEG),
                                   stat[:, 0, 16 * n:16 * n + 16].unsqueeze(2).to_broadcast([P, 16, SEG]), ALU.subtract).then_inc(shifted, 1)
            for n in range(4):
                pool.wait_ge(weight_ready, ONE + b * 8 + (2 * n + 2))
                pool.tensor_tensor(sm[:, n, :].rearrange("p (a k) -> p a k", k=SEG), sm[:, n, :].rearrange("p (a k) -> p a k", k=SEG),
                                   stat[:, 1, 16 * n:16 * n + 16].unsqueeze(2).to_broadcast([P, 16, SEG]), ALU.mult).then_inc(probs, 1)
            for t in range(SEGS - 1):
                for j in range(2):
                    pool.wait_ge(prev_ready, ONE + b * 32 + (2 * t + j + 1))
                    pool.wait_ge(v_kept, ONE + b * 8 + 8)
                    pool.wait_ge(updated, ONE + b * (2 * SEGS) + (2 * t + j + 1))
                    for g in (2, 3):
                        pool.tensor_tensor(D[part(g), 2 * j:2 * j + 2, g, 0:ID],
                                           v[part(g), t, P * j:P * j + P].rearrange("p (e d) -> p e d", e=2),
                                           prev[part(g), 2 * j:2 * j + 2, :], ALU.subtract).then_inc(d_pool, 1)

    @block.vector
    def _(dve):
        dve.memset(z0, 1e-6 / P).then_inc(consts, 1)
        dve.memset(ones_z, 0.0).then_inc(consts, 1)
        dve.memset(D, 0.0).then_inc(consts, 1)
        dve.memset(state, 0.0).then_inc(consts, 1)
        dve.wait_ge(consts, ONE + 4)
        dve.memset(ones_z.rearrange("p (g n) -> p g n", g=G)[:, :, ID:MW], 1.0)
        for g in range(G):
            last = dve.memset(D[part(g), :, g, ID:MW], 1.0)
        last.then_inc(consts, 1)
        norm_dve(dve, s, done)
        norm_dve(dve, s, done + B, again=True)
        dve.wait_ge(beta_ready, ONE + 2)
        with dve.Fori(0, B) as b:
            dve.wait_ge(s.normed, ONE + b + (done + B + 1))
            dve.wait_ge(v_ready, ONE + b * 8)
            dve.tensor_scalar(xa, s.xn[:, batch(b)], s.ln_g, s.ln_b, ALU.mult, ALU.add).then_inc(affine, 1)

            def rope_sum(n):
                dve.wait_ge(sin_ready, ONE + b * NP + (n + 1))
                dve.wait_ge(cos_ready, ONE + b * NP + (n + 1))
                dve.wait_ge(scores_ready, ONE + b * CH + max(0, n // 2 - 1))
                dve.tensor_tensor(zr[:, n % 4, :], tc[:, n % 2, :], rot[:, n % 2, :], ALU.add).then_inc(roped, 1)

            dve.wait_ge(ot_ready, ONE + b * SEGS)
            for n in range(NP):
                c, bank = n // 2, s.bank(n % 4)
                dve.wait_ge(exp_ready, ONE + b * NP + (n + 1))
                dve.wait_ge(roped, ONE + b * NP + max(0, n - 1))
                dve.tensor_tensor(tc[:, n % 2, :], bank, s.rope_cos, ALU.mult).then_inc(cos_ready, 1)
                dve.stream_shuffle(rot[:, n % 2, :], bank, SWAP).then_inc(rot_ready, 1)
                dve.tensor_scalar(e_buf[:, n % 2, :], e_buf[:, n % 2, :], 1.0, None, ALU.min).then_inc(capped, 1)
                if n:
                    rope_sum(n - 1)
                dve.wait_ge(capped, ONE + b * NP + (n + 1))
                dve.scalar_tensor_tensor((sk if n % 2 else sq)[:, c, :], bank, 0.0, e_buf[:, n % 2, :], ALU.max, ALU.add).then_inc(proj_read, 1)
            rope_sum(NP - 1)
            for n in range(4):
                dve.wait_ge(scores_ready, ONE + b * CH + CH)
                dve.wait_ge(out_ready, ONE + b)
                grid = lambda a: a.rearrange("p (a k) -> p a k", k=SEG)
                dve.scalar_tensor_tensor(grid(sm[:, n, :]), grid(s.bank(4 + n)), ID ** -0.5,
                                         s.causal.unsqueeze(1).to_broadcast([P, 16, SEG]), ALU.mult, ALU.add).then_inc(masked, 1)
                dve.wait_ge(masked, ONE + b * 4 + (n + 1))
                dve.tensor_reduce(stat[:, 0, 16 * n:16 * n + 16], grid(sm[:, n, :]), AX.X, ALU.max).then_inc(row_max, 1)
            for n in range(4):
                st = slice(16 * n, 16 * n + 16)
                dve.wait_ge(sm_exp, ONE + b * 4 + (n + 1))
                dve.tensor_reduce(stat[:, 2, st], grid(sm[:, n, :]), AX.X, ALU.add).then_inc(row_sum, 1)
                dve.wait_ge(row_sum, ONE + b * 4 + (n + 1))
                dve.reciprocal(stat[:, 1, st], stat[:, 2, st]).then_inc(weight_ready, 1)
                dve.wait_ge(weight_ready, ONE + b * 8 + (2 * n + 1))
                dve.tensor_tensor(stat[:, 1, st].rearrange("p (t j) -> p t j", j=2), stat[:, 1, st].rearrange("p (t j) -> p t j", j=2),
                                  gain.rearrange("p (j e) -> p e j", e=2)[:, n // 2].unsqueeze(1).to_broadcast([P, 8, 2]), ALU.mult).then_inc(weight_ready, 1)
            for n in range(4):
                dve.wait_ge(probs, ONE + b * 4 + (n + 1))
                dve.transpose(PT[:, n, :], sm[:, n, :]).then_inc(turned, 1)

            den = lambda bank, n: bank[:, 0:n * MW].rearrange("p (a n) -> p a n", a=n)[:, :, ID]
            num = lambda bank, n: bank[:, 0:n * MW].rearrange("p (a n) -> p a n", a=n)[:, :, 0:ID]
            for t in range(SEGS):
                for j in range(2):
                    a = slice(2 * j, 2 * j + 2)
                    dve.wait_ge(recall_k, ONE + b * 32 + (2 * t + j + 1))
                    dve.wait_ge(prev_ready, ONE + b * 32 + 2 * t + j)
                    dve.reciprocal(small[:, a], den(s.bank(j), 2)).then_inc(k_inv, 1)
                    dve.wait_ge(k_inv, ONE + b * 32 + (2 * t + j + 1))
                    dve.wait_ge(d_pool, ONE + b * DS + 4 * t)
                    dve.wait_ge(d_dve, ONE + b * DS + 4 * t)
                    dve.tensor_tensor(prev[:, a, :], num(s.bank(j), 2),
                                      small[:, a].unsqueeze(2).to_broadcast([P, 2, ID]), ALU.mult).then_inc(prev_ready, 1)
                    if t + 1 < SEGS:
                        dve.wait_ge(prev_ready, ONE + b * 32 + (2 * t + j + 1))
                        dve.wait_ge(v_kept, ONE + b * 8 + 8)
                        dve.wait_ge(updated, ONE + b * (2 * SEGS) + (2 * t + j + 1))
                        for g in (0, 1):
                            dve.tensor_tensor(D[part(g), a, g, 0:ID], v[part(g), t, P * j:P * j + P].rearrange("p (e d) -> p e d", e=2),
                                              prev[part(g), a, :], ALU.subtract).then_inc(d_dve, 1)
                dve.wait_ge(recall_q, ONE + b * 32 + (2 * t + 2))
                dve.wait_ge(q_out, ONE + b * SEGS + t)
                dve.tensor_scalar(small[:, 4:8], den(s.bank(7), 4), 1e-6, None, ALU.add).then_inc(q_den, 1)
                dve.wait_ge(q_den, ONE + b * (3 * SEGS) + (3 * t + 1))
                dve.reciprocal(small[:, 8:12], small[:, 4:8]).then_inc(q_den, 1)
                dve.wait_ge(q_den, ONE + b * (3 * SEGS) + (3 * t + 2))
                dve.tensor_tensor(small[:, 12:16], small[:, 8:12], beta, ALU.mult).then_inc(q_den, 1)
                dve.wait_ge(q_den, ONE + b * (3 * SEGS) + (3 * t + 3))
                dve.wait_ge(o_ready, ONE + b * SEGS + t)
                dve.tensor_tensor(mo, num(s.bank(7), 4), small[:, 12:16].unsqueeze(2).to_broadcast([P, 4, ID]), ALU.mult).then_inc(q_out, 1)
                dve.wait_ge(q_out, ONE + b * SEGS + (t + 1))
                dve.wait_ge(pv_ready, ONE + b * (G * SEGS) + (G * t + G))
                dve.wait_ge(ot_ready, ONE + b * SEGS + max(0, t - 1))
                dve.tensor_tensor(o[:, t % 2, :], s.bank(4)[:, 0:256], mo.rearrange("p n d -> p (n d)"), ALU.add).then_inc(o_ready, 1)
            dve.wait_ge(out_ready, ONE + b + 1)
            dve.tensor_tensor(s.x[:, batch(b)], s.x[:, batch(b)], s.bank(7), ALU.add).then_inc(x_added, 1)
        dve.wait_ge(x_added, ONE + B)
    return counters



E, MC = 8, 4
B1, B2 = 2 * MC * P, 2 * MC * P + MC
EXPERT = B2 + 2
TOK = N // P
R = 256
MOST = N // R
TILES_MOE = N // R + E


def moe_layer(nc, s, ctx, done, tag):
    counters = []

    def sem(name):
        counters.append(nc.alloc_semaphore(name=f"{tag}_{name}"))
        return counters[-1]

    weights_in, step, exped, logits_ready = sem("weights_in"), sem("step"), sem("exped"), sem("logits_ready")
    chosen_b_ready, ranked, constants = sem("chosen_b_ready"), sem("ranked"), sem("constants")
    tokens_turned, tokens_scaled, rows_ready = sem("tokens_turned"), sem("tokens_scaled"), sem("rows_ready")
    tiles_known, out_free = sem("tiles_known"), sem("out_free")
    loaded = (sem("loaded0"), sem("loaded1"))
    turned, xt_ready, staged, up_ready = sem("turned"), sem("xt_ready"), sem("staged"), sem("up_ready")
    h_act, h_dve, yt_ready, back_ready, y_ready = sem("h_act"), sem("h_dve"), sem("yt_ready"), sem("back_ready"), sem("y_ready")
    result_turned, x_added = sem("result_turned"), sem("x_added")
    down_ready = sem("down_ready")

    at = [0]

    def f32(n):
        a = at[0]
        at[0] += n
        return s.work[:, a:a + n]

    experts = f32(E * EXPERT)
    own = f32(2 * EXPERT).rearrange("p (n c) -> p n c", n=2)
    tile_in = f32(2 * R).rearrange("p (n r) -> p n r", n=2)
    xt = f32(2 * R).rearrange("p (n r) -> p n r", n=2)
    h = f32(2 * MC * R).rearrange("p (n c r) -> p n c r", n=2, c=MC)
    yt = f32(2 * R).rearrange("p (n r) -> p n r", n=2)
    tile_out = f32(2 * R).rearrange("p (n r) -> p n r", n=2)
    by_token = s.rs
    tile_e = lambda a: a.rearrange("p (i e) -> p i e", e=E)
    score, t0, t1, first, chosen = (tile_e(f32(TOK * E)) for _ in range(5))
    chosen_b = f32(TOK * E // 2).bitcast(BF16)
    before_b, ones_b = f32(P // 2).bitcast(BF16), f32(P // 2).bitcast(BF16)
    restart, total, upto = f32(E * TOK), f32(E * TOK), f32(E * TOK)
    best, weight, row_f, row = f32(TOK), f32(TOK), f32(TOK), f32(TOK).bitcast(I32)
    ones_e, count, tiles, tiles_upto, first_row = f32(E), f32(E), f32(E), f32(E), f32(E)
    filled = f32(E * MOST)
    past = f32(TILES_MOE * E)
    owner_f, owner = f32(TILES_MOE), f32(TILES_MOE).bitcast(I32)
    assert at[0] <= s.work.shape[1]
    wide = lambda a: a.unsqueeze(2).to_broadcast([P, TOK, E])
    each = lambda a: a.unsqueeze(1).to_broadcast([P, TOK, E])
    ei = lambda a: a.rearrange("p (e i) -> p e i", e=E)
    logits = tile_e(s.bank(4)[:, 0:TOK * E])
    rank = tile_e(s.bank(4)[:, 0:TOK * E])
    totals = tile_e(s.bank(4)[:, TOK * E:2 * TOK * E])
    token_bank = lambda b: s.bank((0, 1, 2, 3, 5, 6, 7, 0)[b])
    start_counters(nc, counters + [down_ready])
    scattered, stored = sem("scattered"), (sem("stored0"), sem("stored1"))
    gathered = [sem(f"gathered{b}") for b in range(B)]
    block = ctx.enter_context(nc.Block())

    @block.sync
    def _(sp):
        sp.dma_start(experts, s.expert_w).then_inc(weights_in, 16)
        sp.wait_ge(weights_in, ONE + 16)
        sp.wait_ge(scattered, 16 * TOK)
        with sp.Fori(0, TILES_MOE // 2) as pair:
            t = pair * 2
            for u in range(2):
                sp.wait_ge(turned, ONE + t)
                sp.dma_start(tile_in[:, u, :].rearrange("p (m f) -> p m f", m=2),
                             s.moe_in[bass.ds(t * R + u * R, R), :].rearrange("(m p) f -> p m f", p=P)).then_inc(loaded[u], 16)

    @block.tensor
    def _(pe):
        norm_pe(pe, s, done)
        pe.wait_ge(s.normed, ONE + done + B)
        for i in range(TOK):
            mm = pe.matmul(s.bank(4)[:, i * E:(i + 1) * E], s.xn[:, i * P:(i + 1) * P], s.gate_w, start=True, stop=True)
        mm.then_inc(logits_ready, 1)
        for b in range(B):
            if b == B - 1:
                pe.wait_ge(tokens_scaled, ONE + 1)
            if b == 6:
                pe.wait_ge(constants, ONE + 3)
                pe.wait_ge(chosen_b_ready, ONE + 1)
                pe.matmul(s.bank(4)[:, 0:TOK * E], before_b, chosen_b, start=True, stop=True)
                pe.matmul(s.bank(4)[:, TOK * E:2 * TOK * E], ones_b, chosen_b, start=True, stop=True).then_inc(ranked, 1)
            for n in range(4):
                i = 4 * b + n
                mm = pe.transpose(token_bank(b)[:, n * P:(n + 1) * P], s.xn[:, i * P:(i + 1) * P], s.ident)
            mm.then_inc(tokens_turned, 1)
        pe.wait_ge(tokens_scaled, ONE + B)
        with pe.Fori(0, TILES_MOE // 2) as pair:
            t = pair * 2
            for u in range(2):
                pe.wait_ge(loaded[u], ONE + pair * 16 + 16)
                pe.wait_ge(xt_ready, ONE + t)
                for m in range(2):
                    mm = pe.transpose(s.bank(u)[:, m * P:(m + 1) * P], tile_in[:, u, m * P:(m + 1) * P], s.ident)
                mm.then_inc(turned, 1)
            for u in range(2):
                pe.wait_ge(xt_ready, ONE + t + (u + 1))
                pe.wait_ge(staged, ONE + t + (u + 1))
                pe.wait_ge(h_act, ONE + t * 2)
                pe.wait_ge(h_dve, ONE + t * 2)
                for c in range(MC):
                    pe.matmul(s.bank(2 + 2 * u + c // 2)[:, c % 2 * R:(c % 2 + 1) * R], own[:, u, c * P:(c + 1) * P], xt[:, u, :],
                              start=True, stop=True).then_inc(up_ready, 1)
            for u in range(2):
                pe.wait_ge(y_ready, ONE + t)
                for c in range(MC):
                    pe.wait_ge(h_act if c < 2 else h_dve, ONE + t * 2 + (2 * u + 1 + c % 2))
                    mm = pe.matmul(s.bank(6 + u)[:, 0:R], own[:, u, (MC + c) * P:(MC + c + 1) * P], h[:, u, c, :],
                                   start=c == 0, stop=c == MC - 1)
                mm.then_inc(down_ready, 1)
            for u in range(2):
                pe.wait_ge(yt_ready, ONE + t + (u + 1))
                for m in range(2):
                    mm = pe.transpose(s.bank(6 + u)[:, R + m * P:R + (m + 1) * P], yt[:, u, m * P:(m + 1) * P], s.ident)
                mm.then_inc(back_ready, 1)
        for b in range(B):
            pe.wait_ge(gathered[b], 16 * 4)
            if b >= 6:
                pe.wait_ge(x_added, ONE + b - 5)
            for n in range(4):
                i = 4 * b + n
                mm = pe.transpose(s.bank(b % 6)[:, n * P:(n + 1) * P], by_token[:, i * P:(i + 1) * P], s.ident)
            mm.then_inc(result_turned, 1)

    @block.gpsimd
    def _(pool):
        pool.wait_ge(rows_ready, ONE + 1)
        pool.wait_ge(s.zero_rows, 16)
        for i in range(TOK):
            pool.wait_ge(tokens_scaled, ONE + i // 4 + 1)
            pool.indirect_dma_start(out=s.moe_in[:, :], out_offset=bass.IndirectOffsetOnAxis(ap=row[:, i:i + 1], axis=0),
                                    in_=by_token[:, i * P:(i + 1) * P], in_offset=None).then_inc(scattered, 16)
        with pool.Fori(0, TILES_MOE // 2) as pair:
            t = pair * 2
            for u in range(2):
                pool.wait_ge(y_ready, ONE + t + (u + 1))
                pool.dma_start(s.moe_out[bass.ds(t * R + u * R, R), :].rearrange("(m p) f -> p m f", p=P),
                               tile_out[:, u, :].rearrange("p (m f) -> p m f", m=2)).then_inc(stored[u], 16)
            for u in range(2):
                pool.wait_ge(stored[u], pair * 16 + 16)
                pool.sem_inc(out_free, 1)
        for u in range(2):
            pool.wait_ge(stored[u], TILES_MOE // 2 * 16)
        for i in range(TOK):
            pool.indirect_dma_start(out=by_token[:, i * P:(i + 1) * P], out_offset=None, in_=s.moe_out[:, :],
                                    in_offset=bass.IndirectOffsetOnAxis(ap=row[:, i:i + 1], axis=0)).then_inc(gathered[i // 4], 16)

    @block.scalar
    def _(act):
        norm_act(act, s, done)
        act.wait_ge(step, ONE + 3)
        act.activation(t0, t0, ACT.Exp).then_inc(exped, 1)
        with act.Fori(0, TILES_MOE // 2) as pair:
            t = pair * 2
            for u in range(2):
                act.wait_ge(down_ready, ONE + t + u)
                act.wait_ge(up_ready, ONE + t * MC + (u * MC + 2))
                for c in range(2):
                    act.activation(h[:, u, c, :], s.bank(2 + 2 * u)[:, c * R:(c + 1) * R], ACT.Relu,
                                   bias=own[:, u, B1 + c:B1 + c + 1]).then_inc(h_act, 1)
            for u in range(2):
                act.wait_ge(down_ready, ONE + t + (u + 2))
                act.wait_ge(back_ready, ONE + t)
                act.activation(yt[:, u, :], s.bank(6 + u)[:, 0:R], ACT.Identity, bias=own[:, u, B2:B2 + 1]).then_inc(yt_ready, 1)
            for u in range(2):
                act.wait_ge(back_ready, ONE + t + (u + 1))
                act.wait_ge(out_free, ONE + t)
                act.activation(tile_out[:, u, :], s.bank(6 + u)[:, R:2 * R], ACT.Copy).then_inc(y_ready, 1)

    @block.vector
    def _(dve):
        dve.tensor_copy(before_b, s.before).then_inc(constants, 1)
        dve.memset(ones_b, 1.0).then_inc(constants, 1)
        dve.memset(restart, 1.0).then_inc(constants, 1)
        dve.memset(ones_e, 1.0).then_inc(constants, 1)
        dve.wait_ge(constants, ONE + 4)
        dve.memset(ei(restart)[:, :, 0:1], 0.0).then_inc(constants, 1)
        norm_dve(dve, s, done)

        def after(n):
            dve.wait_ge(step, ONE + n)

        dve.wait_ge(logits_ready, ONE + 1)
        dve.tensor_tensor(score, logits, each(s.gate_b), ALU.add).then_inc(step, 1)
        after(1)
        dve.tensor_reduce(best, score, AX.X, ALU.max).then_inc(step, 1)
        after(2)
        dve.tensor_tensor(t0, score, wide(best), ALU.subtract).then_inc(step, 1)
        dve.wait_ge(exped, ONE + 1)
        after(3)
        dve.tensor_reduce(best, t0, AX.X, ALU.add).then_inc(step, 1)
        after(4)
        dve.reciprocal(best, best).then_inc(step, 1)
        after(5)
        dve.tensor_tensor(score, t0, wide(best), ALU.mult).then_inc(step, 1)
        n = 6
        for is_best, pool in ((first, score), (t1, t0)):
            if is_best is t1:
                after(n)
                dve.scalar_tensor_tensor(t0, first, -2.0, score, ALU.mult, ALU.add).then_inc(step, 1)
                n += 1
            after(n)
            dve.tensor_reduce(best, pool, AX.X, ALU.max).then_inc(step, 1)
            after(n + 1)
            dve.tensor_tensor(is_best, pool, wide(best), ALU.is_equal).then_inc(step, 1)
            after(n + 2)
            dve.tensor_tensor(is_best, is_best, each(s.low_first), ALU.mult).then_inc(step, 1)
            after(n + 3)
            dve.tensor_reduce(best, is_best, AX.X, ALU.max).then_inc(step, 1)
            after(n + 4)
            dve.tensor_tensor(is_best, is_best, wide(best), ALU.is_equal).then_inc(step, 1)
            n += 5
        after(n)
        dve.tensor_tensor(t1, t1, first, ALU.add).then_inc(step, 1)
        after(n + 1)
        dve.scalar_tensor_tensor(t1, score, 0.0, t1, ALU.is_gt, ALU.mult).then_inc(step, 1)
        after(n + 2)
        dve.tensor_tensor(t1, t1, each(s.high_first), ALU.mult).then_inc(step, 1)
        after(n + 3)
        dve.tensor_reduce(best, t1, AX.X, ALU.max).then_inc(step, 1)
        after(n + 4)
        dve.tensor_tensor(chosen, t1, wide(best), ALU.is_equal).then_inc(step, 1)

        after(n + 5)
        dve.tensor_copy(chosen_b, chosen.rearrange("p i e -> p (i e)")).then_inc(chosen_b_ready, 1)
        dve.tensor_tensor(t0, chosen, score, ALU.mult).then_inc(step, 1)
        after(n + 6)
        dve.tensor_reduce(weight, t0, AX.X, ALU.add).then_inc(step, 1)
        after(n + 7)
        for b in range(B):
            if b == 4:
                dve.wait_ge(ranked, ONE + 1)
                dve.wait_ge(constants, ONE + 5)
                dve.tensor_copy(ei(total).rearrange("p e i -> p i e"), totals).then_inc(step, 1)
                after(n + 8)
                dve.tensor_tensor_scan(upto, restart, total, 0.0, ALU.mult, ALU.add).then_inc(step, 1)
                after(n + 9)
                dve.tensor_scalar(count, ei(upto)[:, :, TOK - 1], 1.0 / R, None, ALU.mult).then_inc(step, 1)
                after(n + 10)
                dve.tensor_tensor(filled.rearrange("p (e m) -> p e m", e=E), count.unsqueeze(2).to_broadcast([P, E, MOST]),
                                  s.ramp[:, 0:MOST].unsqueeze(1).to_broadcast([P, E, MOST]), ALU.is_gt).then_inc(step, 1)
                after(n + 11)
                dve.tensor_reduce(tiles, filled.rearrange("p (e m) -> p e m", e=E), AX.X, ALU.add).then_inc(step, 1)
                after(n + 12)
                dve.tensor_tensor_scan(tiles_upto, ones_e, tiles, 0.0, ALU.mult, ALU.add).then_inc(step, 1)
                after(n + 13)
                dve.tensor_tensor(first_row, tiles_upto, tiles, ALU.subtract).then_inc(step, 1)
                dve.tensor_tensor(upto, upto, total, ALU.subtract).then_inc(step, 1)
                after(n + 15)
                dve.scalar_tensor_tensor(ei(upto), first_row.unsqueeze(2).to_broadcast([P, E, TOK]), float(R), ei(upto),
                                         ALU.mult, ALU.add).then_inc(step, 1)
                after(n + 16)
                dve.tensor_tensor(t0, rank, ei(upto).rearrange("p e i -> p i e"), ALU.add).then_inc(step, 1)
                after(n + 17)
                dve.tensor_tensor(t0, t0, chosen, ALU.mult).then_inc(step, 1)
                after(n + 18)
                dve.tensor_reduce(row_f, t0, AX.X, ALU.add).then_inc(step, 1)
                after(n + 19)
                dve.tensor_copy(row, row_f).then_inc(rows_ready, 1)
            dve.wait_ge(tokens_turned, ONE + b + 1)
            dve.tensor_tensor(by_token[:, batch(b)].rearrange("p (n f) -> p n f", n=4),
                              token_bank(b).rearrange("p (n f) -> p n f", n=4),
                              weight[:, 4 * b:4 * b + 4].unsqueeze(2).to_broadcast([P, 4, P]), ALU.mult).then_inc(tokens_scaled, 1)
        dve.tensor_tensor(past.rearrange("p (t e) -> p t e", e=E), s.ramp.unsqueeze(2).to_broadcast([P, TILES_MOE, E]),
                          tiles_upto.unsqueeze(1).to_broadcast([P, TILES_MOE, E]), ALU.is_ge).then_inc(step, 1)
        after(n + 20)
        dve.tensor_reduce(owner_f, past.rearrange("p (t e) -> p t e", e=E), AX.X, ALU.add).then_inc(step, 1)
        after(n + 21)
        dve.tensor_scalar(owner, owner_f, E - 1.0, float(EXPERT), ALU.min, ALU.mult).then_inc(tiles_known, 1)
        dve.wait_ge(tiles_known, ONE + 1)
        dve.wait_ge(weights_in, ONE + 16)
        with dve.Fori(0, TILES_MOE // 2) as pair:
            t = pair * 2
            for u in range(2):
                expert = dve.value_load(owner[0:1, bass.ds(t + u, 1)], min_val=0, max_val=(E - 1) * EXPERT)
                dve.wait_ge(down_ready, ONE + t + u)
                dve.wait_ge(yt_ready, ONE + t)
                dve.tensor_copy(own[:, u, :], experts[:, bass.ds(expert, EXPERT)]).then_inc(staged, 1)
            for u in range(2):
                dve.wait_ge(turned, ONE + t + (u + 1))
                dve.wait_ge(up_ready, ONE + t * MC)
                dve.tensor_copy(xt[:, u, :], s.bank(u)[:, 0:R]).then_inc(xt_ready, 1)
            for u in range(2):
                dve.wait_ge(staged, ONE + t + (u + 1))
                dve.wait_ge(up_ready, ONE + t * MC + (u * MC + 4))
                for c in range(2, MC):
                    dve.tensor_scalar(h[:, u, c, :], s.bank(3 + 2 * u)[:, c % 2 * R:(c % 2 + 1) * R],
                                      own[:, u, B1 + c:B1 + c + 1], 0.0, ALU.add, ALU.max).then_inc(h_dve, 1)
        for b in range(B):
            dve.wait_ge(result_turned, ONE + b + 1)
            dve.tensor_tensor(s.x[:, batch(b)], s.x[:, batch(b)], s.bank(b % 6), ALU.add).then_inc(x_added, 1)
        dve.wait_ge(x_added, ONE + B)
    return counters



def _columns(sizes):
    at, out = 0, {}
    for name, n in sizes:
        out[name] = (at, at + n)
        at += n
    return out, at


WEIGHTS, WEIGHT_COLS = _columns(
    [("avg", P), ("ident", P), ("slopes", 16), ("key_rows", T)]
    + [("w_qkv", 3 * CH * P), ("w_out", CH * P), ("ln_g", 1), ("ln_b", 1), ("mem_beta", 4)]
    + [("rope_cos", T), ("rope_sin", T), ("causal", SEG)]
    + [("Wq", P), ("Wk", P), ("Wv", 32), ("Wo", P)]
    + [(name, P) for name in ("W_in", "W_B", "W_D", "W_out", "C_mat")] + [(name, 16) for name in ("W_ig", "W_fg", "B_mat")]
    + [(name, 1) for name in ("b_in", "b_B", "b_D", "b_out", "b_ig", "b_fg", "gamma", "beta")]
    + [(name, P) for name in ("W_key", "W_value", "W_receptance", "W_output")]
    + [(name, 1) for name in ("time_decay", "time_first", "mix_k", "mix_v", "mix_r")]
    + [("gate_w", E), ("gate_b", E), ("low_first", E), ("high_first", E), ("before", P), ("ramp", TILES_MOE)]
)
INTS, INT_COLS = _columns([("wgate", HID), ("wup", HID), ("wdown", HID)])


class Shared:
    pass


GQA_BF16_COLS = (HEADS + KV) * 3 * P + P


def build(nc, x_in, weights, ints, gqa_tables, expert_w, out, layers):
    with ExitStack() as ctx:
        def sb(name, shape, dt=F32):
            return ctx.enter_context(nc.sbuf_tensor(name, shape, dt))

        def sem(name):
            return ctx.enter_context(nc.semaphore("norm_" + name))

        w = sb("w", [P, WEIGHT_COLS])
        wf = sb("wf", [P, INT_COLS])
        weight = lambda name: w[:, WEIGHTS[name][0]:WEIGHTS[name][1]]
        integer = lambda name: wf[:, INTS[name][0]:INTS[name][1]]
        s = Shared()
        s.avg, s.ident, s.slopes, s.key_rows = weight("avg"), weight("ident"), weight("slopes"), weight("key_rows")
        s.w_qkv, s.w_out, s.ln_g, s.ln_b = weight("w_qkv"), weight("w_out"), weight("ln_g"), weight("ln_b")
        s.mem_beta, s.rope_cos, s.rope_sin, s.causal = weight("mem_beta"), weight("rope_cos"), weight("rope_sin"), weight("causal")
        s.Wq, s.Wk, s.Wv, s.Wo = weight("Wq"), weight("Wk"), weight("Wv"), weight("Wo")
        s.W_in, s.W_B, s.W_D, s.W_out = weight("W_in"), weight("W_B"), weight("W_D"), weight("W_out")
        s.C_mat, s.W_ig, s.W_fg, s.B_mat = weight("C_mat"), weight("W_ig"), weight("W_fg"), weight("B_mat")
        s.b_in, s.b_B, s.b_D, s.b_out = weight("b_in"), weight("b_B"), weight("b_D"), weight("b_out")
        s.b_ig, s.b_fg, s.gamma, s.beta = weight("b_ig"), weight("b_fg"), weight("gamma"), weight("beta")
        s.W_key, s.W_value, s.W_receptance, s.W_output = weight("W_key"), weight("W_value"), weight("W_receptance"), weight("W_output")
        s.time_decay, s.time_first, s.mix_k, s.mix_v = weight("time_decay"), weight("time_first"), weight("mix_k"), weight("mix_v")
        s.mix_r, s.gate_w, s.gate_b = weight("mix_r"), weight("gate_w"), weight("gate_b")
        s.low_first, s.high_first, s.before, s.ramp = weight("low_first"), weight("high_first"), weight("before"), weight("ramp")
        s.wgate, s.wup, s.wdown = integer("wgate"), integer("wup"), integer("wdown")
        s.b_ig, s.b_fg = s.b_ig[0:16, :], s.b_fg[0:16, :]

        s.gqa_tables, s.expert_w = gqa_tables, expert_w
        s.x = sb("x", [P, N])
        s.xn = sb("xn", [P, N])
        s.rs = sb("rs", [P, N])
        s.sq = sb("sq", [P, 2, T])
        s.eps = sb("eps", [P, 1])
        s.scrap = sb("scrap", [P, 1])
        s.work = sb("work", [P, 23 * 1024])
        wi = s.work[:, 0:INT_COLS].bitcast(I32)
        s.psum = ctx.enter_context(nc.psum_tensor("psum", [P, 8, T], F32))
        s.bank = lambda i: s.psum[:, i, :]
        s.centered, s.squared, s.mean_ready = sem("centered"), sem("squared"), sem("mean_ready")
        s.var_ready, s.logged, s.rstd_ready = sem("var_ready"), sem("logged"), sem("rstd_ready")
        s.normed, s.warmed = sem("normed"), sem("warmed")
        norm_counters = (s.centered, s.squared, s.mean_ready, s.var_ready, s.logged, s.rstd_ready, s.normed, s.warmed)
        s.moe_in = nc.dram_tensor("moe_in", (TILES_MOE * R, P), F32, kind="Internal").ap()
        s.moe_out = nc.dram_tensor("moe_out", (TILES_MOE * R, P), F32, kind="Internal").ap()
        s.zero_rows = ctx.enter_context(nc.semaphore("zero_rows"))
        loaded = ctx.enter_context(nc.semaphore("loaded"))
        cleared = ctx.enter_context(nc.semaphore("cleared"))
        consts = ctx.enter_context(nc.semaphore("consts"))
        stored = ctx.enter_context(nc.semaphore("stored"))

        start_counters(nc, norm_counters)
        with nc.Block() as block:
            @block.sync
            def _(sp):
                sp.dma_start(s.x[:, :], x_in).then_inc(loaded, 16)
                sp.dma_start(w[:, :], weights).then_inc(loaded, 16)
                sp.dma_start(wi, ints).then_inc(loaded, 16)
                sp.wait_ge(loaded, 48)

            @block.gpsimd
            def _(pool):
                pool.memset(s.xn[:, :], 0.0).then_inc(cleared, 1)
                pool.wait_ge(cleared, 1)
                for a in range(0, TILES_MOE * R // P, N // P):
                    n = min(N // P, TILES_MOE * R // P - a)
                    pool.dma_start(s.moe_in[a * P:(a + n) * P, :].rearrange("(m p) f -> p m f", p=P),
                                   s.xn[:, 0:n * P].rearrange("p (m f) -> p m f", f=P)).then_inc(s.zero_rows, 16)
                pool.wait_ge(s.zero_rows, 32)

            @block.vector
            def _(dve):
                dve.memset(s.eps[:, :], 1e-5).then_inc(consts, 1)
                dve.wait_ge(loaded, 48)
                dve.tensor_scalar(wf[:, :], wi, float(np.float32(1.0 / 127.0)), None, ALU.mult).then_inc(consts, 1)
                dve.wait_ge(consts, 2)

        done = 0
        for n, kind in enumerate(layers):
            with ExitStack() as own:
                counters = LAYERS[kind](nc, s, own, done, f"l{n}")
            nc.all_engine_barrier()
            nc.clear_and_free_semaphores(counters)
            nc.all_engine_barrier()
            done += 2 * B if kind == "infini" else B

        with nc.Block() as block:
            @block.sync
            def _(sp):
                sp.dma_start(out, s.x[:, :]).then_inc(stored, 16)
                sp.wait_ge(stored, 16)


LAYERS = {"swiglu": swiglu_layer, "ssm": ssm_layer, "rwkv": rwkv_layer, "gqa": gqa_layer, "infini": infini_layer,
          "moe": moe_layer}



def gqa_constants():
    bf = np.dtype("bfloat16")
    start = 2.0 ** (-2.0 ** (-(math.log2(HEADS) - 3)))
    slope = np.array([start * start ** i for i in range(HEADS)], dtype=np.float32)
    slopes, rows = np.zeros((P, HEADS), np.float32), np.zeros((P, T), np.float32)
    position = np.arange(T)
    left = slope
    for i in range(3):
        part = left.astype(bf).astype(np.float32)
        left = left - part
        for j, pos in enumerate((position // 256 * 256, position % 256)):
            slopes[BIAS_ROW + 2 * i + j] = part
            rows[BIAS_ROW + 2 * i + j] = pos
    rows[MAX_ROW:MAX_ROW + 3] = 1
    tables = np.zeros((P, GQA_BF16_COLS), bf)
    for side, heads, at in ((0, HEADS, 0), (1, KV, HEADS * 3 * P)):
        for h in range(heads):
            for n, pair in enumerate(SLOTS):
                for d in range(HD):
                    tables[h * HD + d, at + (h * 3 + pair[side]) * P + n * HD + d] = 1
    tables[:, (HEADS + KV) * 3 * P:] = np.eye(P)
    return slopes, rows, tables


def infini_constants():
    freqs = np.float32(10000.0) ** (-np.arange(0, ID, 2, dtype=np.float32) / np.float32(ID))
    angle = (np.arange(T, dtype=np.float32)[:, None] * freqs).astype(np.float32)
    feature = np.arange(P) % ID
    cos = np.cos(angle)[:, feature // 2].T
    sin = np.sin(angle)[:, feature // 2].T * np.where(feature % 2, 1.0, -1.0).astype(np.float32)[:, None]
    row, column = np.arange(P) % SEG, np.arange(SEG)
    causal = np.where(column[None, :] <= row[:, None], np.float32(0), np.float32(-1e30))
    return cos.astype(np.float32), sin.astype(np.float32), causal.astype(np.float32)


def lay_out(i):
    f = lambda name: np.asarray(i[name])
    x = np.ascontiguousarray(f("L0_attn_a_x").reshape(N, P).T)
    avg = np.full((P, P), 1.0 / P, np.float32)
    col = lambda a: np.concatenate([a.reshape(-1, 1), np.zeros((P - a.size, 1), a.dtype)])
    rows = lambda a: np.concatenate([a, np.zeros((P - a.shape[0], a.shape[1]), a.dtype)])
    parts = {"avg": avg, "ident": np.eye(P, dtype=np.float32)}
    parts["slopes"], parts["key_rows"], gqa_tables = gqa_constants()
    parts["w_qkv"] = f("L0_attn_b_w_qkv")
    parts["w_out"] = f("L0_attn_b_w_out").reshape(CH, P, P).transpose(1, 0, 2).reshape(P, CH * P)
    parts["ln_g"], parts["ln_b"] = col(f("L0_attn_b_ln_g")), col(f("L0_attn_b_ln_b"))
    gate = f("L0_attn_b_mem_beta").reshape(2, G, 2).transpose(1, 0, 2).reshape(G, 1, 4)
    parts["mem_beta"] = np.broadcast_to(gate, (G, 32, 4)).reshape(P, 4)
    parts["rope_cos"], parts["rope_sin"], parts["causal"] = infini_constants()
    for name in ("Wq", "Wv", "Wo"):
        parts[name] = f("L0_attn_a_" + name)
    parts["Wk"] = np.concatenate([f("L0_attn_a_Wk"), np.zeros((P, P - KV * HD), np.float32)], axis=1)
    for name in ("W_in", "W_B", "W_D", "W_out", "W_ig", "W_fg", "B_mat"):
        parts[name] = f("L1_attn_a_" + name)
    parts["C_mat"] = rows(f("L1_attn_a_C_mat"))
    for name in ("b_in", "b_B", "b_D", "b_out", "b_ig", "b_fg", "gamma", "beta"):
        parts[name] = col(f("L1_attn_a_" + name))
    for name in ("W_key", "W_value", "W_receptance", "W_output"):
        parts[name] = f("L1_attn_b_" + name).T
    for name in ("time_decay", "time_first"):
        parts[name] = col(f("L1_attn_b_" + name))
    for name in "kvr":
        parts["mix_" + name] = col(f("L1_attn_b_time_mix_" + name))
    everywhere = lambda a: np.broadcast_to(a.reshape(1, -1), (P, a.size))
    parts["gate_w"], parts["gate_b"] = f("L0_ffn_gate_w"), everywhere(f("L0_ffn_gate_b"))
    index = np.arange(E, dtype=np.float32)
    parts["low_first"], parts["high_first"] = everywhere(E - index), everywhere(index + 1)
    parts["before"] = np.triu(np.ones((P, P), np.float32), 1)
    parts["ramp"] = everywhere(np.arange(TILES_MOE, dtype=np.float32))
    weights = np.concatenate([parts[name] for name in WEIGHTS], axis=1)
    wd = f("L1_ffn_w_down")
    ints = np.concatenate([
        f("L1_ffn_w_gate").T, f("L1_ffn_w_up").T,
        wd.T.reshape(HC, P, P).transpose(1, 0, 2).reshape(P, HID)], axis=1)
    up = f("L0_ffn_w1").transpose(1, 0, 2)
    down = f("L0_ffn_w2").reshape(E, MC, P, P).transpose(2, 0, 1, 3).reshape(P, E, MC * P)
    b1, b2 = f("L0_ffn_b1").reshape(E, MC, P).transpose(2, 0, 1), f("L0_ffn_b2").T.reshape(P, E, 1)
    pad = np.zeros((P, E, EXPERT - B2 - 1), np.float32)
    expert_w = np.ascontiguousarray(np.concatenate([up, down, b1, b2, pad], axis=2).reshape(P, E * EXPERT))
    return {"x_in": x, "weights": np.ascontiguousarray(weights), "ints": np.ascontiguousarray(ints),
            "gqa_tables": gqa_tables, "expert_w": expert_w}


MODEL = ["gqa", "moe", "infini", "moe", "ssm", "swiglu", "rwkv", "swiglu"]


def kernel(**inputs):
    import concourse.bacc as bacc
    from concourse.bass_utils import run_bass_kernel_spmd

    arrays = lay_out(inputs)
    nc = bacc.Bacc("TRN2", target_bir_lowering=False, num_devices=1)
    args = [nc.dram_tensor(name, a.shape, mybir.dt.from_np(a.dtype), kind="ExternalInput").ap()
            for name, a in arrays.items()]
    out = nc.dram_tensor("out", (P, N), F32, kind="ExternalOutput").ap()
    build(nc, *args, out, MODEL)
    results = run_bass_kernel_spmd(nc, [arrays], core_ids=[0]).results
    return np.ascontiguousarray(results[0]["out"].T).reshape(B, T, P)
```

```python
from contextlib import ExitStack
import math

import numpy as np

import concourse.bass as bass
from concourse import mybir

P = 128
B, T = 8, 512
N = B * T
F32, BF16 = mybir.dt.float32, mybir.dt.bfloat16
I32 = mybir.dt.int32
ALU, ACT, AX = mybir.AluOpType, mybir.ActivationFunctionType, mybir.AxisListType

HID = 384
HC = HID // P
FREE = 2
ONE = 1


def start_counters(nc, counters):
    with nc.Block() as block:
        @block.sync
        def _(sp):
            for counter in counters:
                sp.sem_inc(counter, ONE)


def batch(b):
    return bass.ds(b * T, T) if not isinstance(b, int) else slice(b * T, b * T + T)



def norm_pairs(eng, first, second):
    first(0)
    with eng.Fori(1, B // 2) as pair:
        b = pair * 2
        first(b)
        second(b - 2)
    second(B - 2)


def norm_pe(pe, s, done, again=False):
    src = s.xn if again else s.x

    def means(b):
        for u in range(2):
            pe.wait_ge(s.centered, ONE + b + done)
            if again:
                pe.wait_ge(s.normed, ONE + b + (done - B + u + 1))
            pe.matmul(s.bank(u), s.avg[:, :], src[:, batch(b + u)], start=True, stop=True).then_inc(s.mean_ready, 1)

    def variances(b):
        for u in range(2):
            pe.wait_ge(s.squared, ONE + b + (done + u + 1))
            pe.wait_ge(s.logged, ONE + b + done)
            pe.matmul(s.bank(2 + u), s.avg[:, :], s.rs[:, batch(b + u)], start=True, stop=True).then_inc(s.var_ready, 1)

    norm_pairs(pe, means, variances)


def norm_act(act, s, done):
    if done:
        act.wait_ge(s.warmed, ONE + done // B * 2)
    act.activation(s.scrap[:, 0:1], s.eps[:, 0:1], ACT.Ln).then_inc(s.warmed, 1)

    def squares(b):
        for u in range(2):
            act.wait_ge(s.centered, ONE + b + (done + u + 1))
            act.activation(s.rs[:, batch(b + u)], s.xn[:, batch(b + u)], ACT.Square).then_inc(s.squared, 1)

    def logarithms(b):
        for u in range(2):
            act.wait_ge(s.var_ready, ONE + b + (done + u + 1))
            act.activation(s.rs[:, batch(b + u)], s.bank(2 + u), ACT.Ln, bias=s.eps[:, 0:1]).then_inc(s.logged, 1)

    norm_pairs(act, squares, logarithms)
    act.wait_ge(s.warmed, ONE + done // B * 2 + 1)
    act.activation(s.scrap[:, 0:1], s.eps[:, 0:1], ACT.Exp).then_inc(s.warmed, 1)
    act.wait_ge(s.logged, ONE + done + B)
    with act.Fori(0, B) as b:
        act.activation(s.rs[:, batch(b)], s.rs[:, batch(b)], ACT.Exp, scale=-0.5).then_inc(s.rstd_ready, 1)


def norm_dve(dve, s, done, again=False):
    src = s.xn if again else s.x
    with dve.Fori(0, B // 2) as pair:
        b = pair * 2
        for u in range(2):
            dve.wait_ge(s.mean_ready, ONE + b + (done + u + 1))
            dve.tensor_tensor(s.xn[:, batch(b + u)], src[:, batch(b + u)], s.bank(u), ALU.subtract).then_inc(s.centered, 1)
    dve.wait_ge(s.centered, ONE + done + B)
    with dve.Fori(0, B) as b:
        dve.wait_ge(s.rstd_ready, ONE + b + (done + 1))
        dve.tensor_tensor(s.xn[:, batch(b)], s.xn[:, batch(b)], s.rs[:, batch(b)], ALU.mult).then_inc(s.normed, 1)



def swiglu_layer(nc, s, ctx, done, tag):
    counters = []

    def sem(name):
        counters.append(nc.alloc_semaphore(name=f"{tag}_{name}"))
        return counters[-1]

    gate_ready, up_ready = sem("gate_ready"), sem("up_ready")
    silu_ready, h_ready = sem("silu_ready"), sem("h_ready")
    down_ready, x_added = sem("down_ready"), sem("x_added")
    sg = s.work[:, 0:2 * T].rearrange("p (n t) -> p n t", n=2)
    h = s.work[:, 2 * T:(2 + 2 * HC) * T].rearrange("p (n t) -> p n t", n=2 * HC)
    start_counters(nc, counters + FREE * [h_ready])
    block = ctx.enter_context(nc.Block())

    if s.last:
        @block.sync
        def _(sp):
            for b in range(B):
                sp.wait_ge(x_added, ONE + b + 1)
                sp.dma_start(s.out[:, batch(b)], s.x[:, batch(b)]).then_inc(s.stored, 16)
            sp.wait_ge(s.stored, 16 * B)

    @block.tensor
    def _(pe):
        norm_pe(pe, s, done)
        with pe.Fori(0, B // 2) as pair:
            b = pair * 2
            for u in range(2):
                pe.wait_ge(s.normed, ONE + b + (done + u + 1))
                for c in range(HC):
                    k = HC * u + c
                    pe.wait_ge(h_ready, ONE + b * HC + (k + 1))
                    pe.matmul(s.bank(k % 2), s.wgate[:, P * c:P * c + P], s.xn[:, batch(b + u)],
                              start=True, stop=True).then_inc(gate_ready, 1)
                    pe.matmul(s.bank(2 + k % 2), s.wup[:, P * c:P * c + P], s.xn[:, batch(b + u)],
                              start=True, stop=True).then_inc(up_ready, 1)
            for u in range(2):
                pe.wait_ge(x_added, ONE + b)
                for c in range(HC):
                    pe.wait_ge(h_ready, ONE + b * HC + (HC * u + c + 1 + FREE))
                    mm = pe.matmul(s.bank(4 + u), s.wdown[:, P * c:P * c + P], h[:, HC * u + c, :],
                                   start=c == 0, stop=c == HC - 1)
                mm.then_inc(down_ready, 1)

    @block.scalar
    def _(act):
        norm_act(act, s, done)
        with act.Fori(0, B // 2) as pair:
            b = pair * 2
            for k in range(2 * HC):
                act.wait_ge(gate_ready, ONE + b * HC + (k + 1))
                act.wait_ge(h_ready, ONE + b * HC + (k + 1))
                act.activation(sg[:, k % 2, :], s.bank(k % 2), ACT.Silu).then_inc(silu_ready, 1)

    @block.vector
    def _(dve):
        norm_dve(dve, s, done)
        with dve.Fori(0, B // 2) as pair:
            b = pair * 2
            dve.wait_ge(down_ready, ONE + b)
            for k in range(2 * HC):
                dve.wait_ge(silu_ready, ONE + b * HC + (k + 1))
                dve.wait_ge(up_ready, ONE + b * HC + (k + 1))
                dve.tensor_tensor(h[:, k, :], s.bank(2 + k % 2), sg[:, k % 2, :], ALU.mult).then_inc(h_ready, 1)
            for u in range(2):
                dve.wait_ge(down_ready, ONE + b + (u + 1))
                dve.tensor_tensor(s.x[:, batch(b + u)], s.x[:, batch(b + u)], s.bank(4 + u), ALU.add).then_inc(x_added, 1)
        dve.wait_ge(x_added, ONE + B)
    return counters



def ssm_layer(nc, s, ctx, done, tag):
    counters = []

    def sem(name):
        counters.append(nc.alloc_semaphore(name=f"{tag}_{name}"))
        return counters[-1]

    xp_ready, t_ready, gates_ready, tb_ready = sem("xp_ready"), sem("t_ready"), sem("gates_ready"), sem("tb_ready")
    xp_mm, bx_ready, gated, drive_ready = sem("xp_mm"), sem("bx_ready"), sem("gated"), sem("drive_ready")
    states_ready, pre_ready, tanh_ready, y_ready = sem("states"), sem("pre_ready"), sem("tanh_ready"), sem("y_ready")
    res_ready, mean_ready, centered, squared = sem("res_ready"), sem("mean_ready"), sem("centered"), sem("squared")
    var_ready, var_kept, ln_done, rstd, scaled, x_added = (
        sem("var_ready"), sem("var_kept"), sem("ln_done"), sem("rstd"), sem("scaled"), sem("x_added"))
    zeroed = sem("zeroed")
    S = s.W_ig.shape[1]
    w = s.work
    xp = w[:, 0:2 * T].rearrange("p (u t) -> p u t", u=2)
    tb = w[:, 2 * T:4 * T].rearrange("p (u t) -> p u t", u=2)
    hs = w[:, 4 * T:6 * T].rearrange("p (u t) -> p u t", u=2)
    y = w[:, 6 * T:8 * T].rearrange("p (u t) -> p u t", u=2)
    ig = w[0:S, 8 * T:10 * T].rearrange("p (u t) -> p u t", u=2)
    fg = w[0:S, 10 * T:12 * T].rearrange("p (u t) -> p u t", u=2)
    drive = w[0:S, 12 * T:14 * T].rearrange("p (u t) -> p u t", u=2)
    bank = lambda u, i: s.bank(4 * u + i)
    start_counters(nc, counters)
    block = ctx.enter_context(nc.Block())

    @block.tensor
    def _(pe):
        norm_pe(pe, s, done)
        pe.wait_ge(zeroed, ONE + 1)
        with pe.Fori(0, B // 2) as pair:
            b = pair * 2
            for u in range(2):
                pe.wait_ge(s.normed, ONE + b + (done + u + 1))
                pe.wait_ge(gated, ONE + b * 2)
                pe.matmul(bank(u, 0), s.W_in, s.xn[:, batch(b + u)], start=True, stop=True).then_inc(xp_mm, 1)
            for u in range(2):
                pe.wait_ge(xp_ready, ONE + b + (u + 1))
                pe.wait_ge(drive_ready, ONE + b)
                pe.matmul(bank(u, 1), s.W_B, xp[:, u, :], start=True, stop=True).then_inc(t_ready, 1)
                pe.wait_ge(centered, ONE + b)
                pe.matmul(bank(u, 2)[0:S, :], s.W_ig, xp[:, u, :], start=True, stop=True)
                pe.matmul(bank(u, 0)[0:S, :], s.W_fg, xp[:, u, :], start=True, stop=True).then_inc(gates_ready, 1)
                pe.wait_ge(var_kept, ONE + b)
                pe.matmul(bank(u, 3), s.W_D, xp[:, u, :], start=True, stop=False)
            for u in range(2):
                pe.wait_ge(tb_ready, ONE + b + (u + 1))
                pe.matmul(bank(u, 1)[0:S, :], s.B_mat, tb[:, u, :], start=True, stop=True).then_inc(bx_ready, 1)
            for u in range(2):
                pe.wait_ge(states_ready, ONE + b + (u + 1))
                pe.matmul(bank(u, 3), s.C_mat, hs[:, u, :], start=False, stop=True).then_inc(pre_ready, 1)
            for u in range(2):
                pe.wait_ge(tanh_ready, ONE + b + (u + 1))
                pe.matmul(bank(u, 3), s.W_out, y[:, u, :], start=True, stop=True).then_inc(y_ready, 1)
            for u in range(2):
                pe.wait_ge(res_ready, ONE + b + (u + 1))
                pe.wait_ge(gated, ONE + b * 2 + (2 * u + 2))
                pe.matmul(bank(u, 2), s.avg, s.xn[:, batch(b + u)], start=True, stop=True).then_inc(mean_ready, 1)
            for u in range(2):
                pe.wait_ge(squared, ONE + b + (u + 1))
                pe.matmul(bank(u, 3), s.avg, s.sq[:, u, :], start=True, stop=True).then_inc(var_ready, 1)

    @block.scalar
    def _(act):
        norm_act(act, s, done)
        with act.Fori(0, B // 2) as pair:
            b = pair * 2
            for u in range(2):
                act.wait_ge(xp_mm, ONE + b + (u + 1))
                act.wait_ge(res_ready, ONE + b)
                act.activation(xp[:, u, :], bank(u, 0), ACT.Identity, bias=s.b_in).then_inc(xp_ready, 1)
            for u in range(2):
                act.wait_ge(t_ready, ONE + b + (u + 1))
                act.wait_ge(bx_ready, ONE + b)
                act.activation(tb[:, u, :], bank(u, 1), ACT.Identity, bias=s.b_B).then_inc(tb_ready, 1)
            for u in range(2):
                act.wait_ge(gates_ready, ONE + b + (u + 1))
                act.wait_ge(states_ready, ONE + b)
                act.activation(ig[:, u, :], bank(u, 2)[0:S, :], ACT.Sigmoid, bias=s.b_ig).then_inc(gated, 1)
                act.activation(fg[:, u, :], bank(u, 0)[0:S, :], ACT.Sigmoid, bias=s.b_fg).then_inc(gated, 1)
            for u in range(2):
                act.wait_ge(pre_ready, ONE + b + (u + 1))
                act.wait_ge(y_ready, ONE + b)
                act.activation(y[:, u, :], bank(u, 3), ACT.Tanh, bias=s.b_D).then_inc(tanh_ready, 1)
            for u in range(2):
                act.wait_ge(centered, ONE + b + (u + 1))
                act.wait_ge(var_ready, ONE + b)
                act.activation(s.sq[:, u, :], s.xn[:, batch(b + u)], ACT.Square).then_inc(squared, 1)
            for u in range(2):
                act.wait_ge(var_ready, ONE + b + (u + 1))
                act.wait_ge(s.normed, ONE + b + (done + u + 1))
                act.activation(s.rs[:, batch(b + u)], bank(u, 3), ACT.Identity).then_inc(var_kept, 1)
        act.wait_ge(var_kept, ONE + B)
        act.activation(s.rs[:, :], s.rs[:, :], ACT.Ln, bias=s.eps[:, 0:1]).then_inc(ln_done, 1)
        act.wait_ge(ln_done, ONE + 1)
        for b in range(B):
            act.activation(s.rs[:, batch(b)], s.rs[:, batch(b)], ACT.Exp, scale=-0.5).then_inc(rstd, 1)

    @block.vector
    def _(dve):
        dve.memset(hs, 0.0).then_inc(zeroed, 1)
        norm_dve(dve, s, done)
        with dve.Fori(0, B // 2) as pair:
            b = pair * 2
            for u in range(2):
                dve.wait_ge(bx_ready, ONE + b + (u + 1))
                dve.wait_ge(gated, ONE + b * 2 + (2 * u + 2))
                dve.wait_ge(states_ready, ONE + b + u)
                dve.tensor_tensor(drive[:, u, :], bank(u, 1)[0:S, :], ig[:, u, :], ALU.mult).then_inc(drive_ready, 1)
                dve.wait_ge(drive_ready, ONE + b + (u + 1))
                dve.wait_ge(pre_ready, ONE + b)
                dve.tensor_tensor_scan(hs[0:S, u, :], fg[:, u, :], drive[:, u, :], 0.0, ALU.mult, ALU.add).then_inc(states_ready, 1)
            for u in range(2):
                dve.wait_ge(y_ready, ONE + b + (u + 1))
                dve.scalar_tensor_tensor(s.xn[:, batch(b + u)], bank(u, 3), s.b_out, xp[:, u, :], ALU.add, ALU.add).then_inc(res_ready, 1)
            for u in range(2):
                dve.wait_ge(mean_ready, ONE + b + (u + 1))
                dve.wait_ge(res_ready, ONE + b + (u + 1))
                dve.tensor_tensor(s.xn[:, batch(b + u)], s.xn[:, batch(b + u)], bank(u, 2), ALU.subtract).then_inc(centered, 1)
        for b in range(B):
            dve.wait_ge(rstd, ONE + b + 1)
            dve.wait_ge(centered, ONE + b + 1)
            dve.scalar_tensor_tensor(s.xn[:, batch(b)], s.xn[:, batch(b)], s.gamma, s.rs[:, batch(b)], ALU.mult, ALU.mult).then_inc(scaled, 1)
            dve.wait_ge(scaled, ONE + b + 1)
            dve.scalar_tensor_tensor(s.x[:, batch(b)], s.xn[:, batch(b)], s.beta, s.x[:, batch(b)], ALU.add, ALU.add).then_inc(x_added, 1)
        dve.wait_ge(x_added, ONE + B)
    return counters



def rwkv_layer(nc, s, ctx, done, tag):
    counters = []

    def sem(name):
        counters.append(nc.alloc_semaphore(name=f"{tag}_{name}"))
        return counters[-1]

    NEG = -1e38
    shifted, delta_ready, mixed, krv_ready = sem("shifted"), sem("delta"), sem("mixed"), sem("krv_ready")
    max_ready, peak_ready, exponents, exps = sem("max_ready"), sem("peak_ready"), sem("exponents"), sem("exps")
    kv_ready, sums_ready, r_ready = sem("kv_ready"), sem("sums_ready"), sem("r_ready")
    parts, num_ready, den_ready, gated = sem("parts"), sem("num_ready"), sem("den_ready"), sem("gated")
    consts, den_log, inv_ready, wkv_ready, out_ready, x_added = (
        sem("consts"), sem("den_log"), sem("inv_ready"), sem("wkv_ready"), sem("out_ready"), sem("x_added"))
    before_ready, den_part = sem("before_ready"), sem("den_part")
    at = [0]

    def buf(n):
        a = at[0]
        at[0] += n
        return s.work[:, a:a + n]

    def two(n):
        return buf(2 * n).rearrange("p (u t) -> p u t", u=2)

    last, delta = two(T), two(T)
    xk, xv, xr = two(T), two(T), two(T)
    m, A, Z = two(T + 1), two(T + 1), two(T + 1)
    E = buf(2 * 4 * T).rearrange("p (u n t) -> p u n t", u=2, n=4)
    kv, peak, th = two(T), two(T), two(T)
    negw_row = buf(T)
    c = buf(2)
    neg_w, w_pos = c[:, 0:1], c[:, 1:2]
    bank = lambda u, i: s.bank(4 * u + i)
    start_counters(nc, counters)
    block = ctx.enter_context(nc.Block())

    @block.tensor
    def _(pe):
        norm_pe(pe, s, done)
        with pe.Fori(0, B // 2) as pair:
            b = pair * 2
            for u in range(2):
                pe.wait_ge(mixed, ONE + b * 3 + (3 * u + 3))
                pe.wait_ge(num_ready, ONE + b)
                pe.matmul(bank(u, 0), s.W_key, xk[:, u, :], start=True, stop=True)
                pe.matmul(bank(u, 1), s.W_value, xv[:, u, :], start=True, stop=True)
                pe.matmul(bank(u, 2), s.W_receptance, xr[:, u, :], start=True, stop=True).then_inc(krv_ready, 1)
        with pe.Fori(0, B // 2) as pair:
            b = pair * 2
            for u in range(2):
                pe.wait_ge(wkv_ready, ONE + b + (u + 1))
                pe.wait_ge(x_added, ONE + b)
                pe.matmul(bank(u, 3), s.W_output, s.xn[:, batch(b + u)], start=True, stop=True).then_inc(out_ready, 1)

    @block.gpsimd
    def _(pool):
        with pool.Fori(0, B // 2) as pair:
            b = pair * 2
            for u in range(2):
                pool.wait_ge(peak_ready, ONE + b + (u + 1))
                pool.wait_ge(max_ready, ONE + b + (u + 1))
                pool.tensor_tensor(E[:, u, 3, :], m[:, u, 0:T], peak[:, u, :], ALU.subtract).then_inc(before_ready, 1)
            for u in range(2):
                pool.wait_ge(exps, ONE + b + (u + 1))
                pool.wait_ge(sums_ready, ONE + b * 2 + (2 * u + 2))
                pool.tensor_tensor(kv[:, u, :], E[:, u, 3, :], Z[:, u, 0:T], ALU.mult).then_inc(den_part, 1)
                pool.wait_ge(den_part, ONE + b + (u + 1))
                pool.tensor_tensor(s.rs[:, batch(b + u)], E[:, u, 2, :], kv[:, u, :], ALU.add).then_inc(den_ready, 1)

    @block.scalar
    def _(act):
        norm_act(act, s, done)
        act.activation(w_pos, s.time_decay, ACT.Exp).then_inc(consts, 1)
        with act.Fori(0, B // 2) as pair:
            b = pair * 2
            for u in range(2):
                act.wait_ge(s.normed, ONE + b + (done + u + 1))
                act.wait_ge(mixed, ONE + b * 3)
                act.wait_ge(consts, ONE + 3)
                act.activation(last[:, u, 1:T], s.xn[:, bass.ds((b + u) * T, T - 1)], ACT.Copy).then_inc(shifted, 1)
            for u in range(2):
                act.wait_ge(exponents, ONE + b * 3 + (3 * u + 3))
                act.wait_ge(before_ready, ONE + b + (u + 1))
                act.activation(E[:, u, :, :], E[:, u, :, :], ACT.Exp).then_inc(exps, 1)
            for u in range(2):
                act.wait_ge(krv_ready, ONE + b + (u + 1))
                act.wait_ge(num_ready, ONE + b)
                act.activation(th[:, u, :], bank(u, 2), ACT.Tanh, scale=0.5).then_inc(r_ready, 1)
        act.wait_ge(den_ready, ONE + B)
        act.activation(s.rs[:, :], s.rs[:, :], ACT.Ln).then_inc(den_log, 1)
        act.wait_ge(den_log, ONE + 1)
        for b in range(B):
            act.activation(s.rs[:, batch(b)], s.rs[:, batch(b)], ACT.Exp, scale=-1.0).then_inc(inv_ready, 1)

    @block.vector
    def _(dve):
        dve.memset(last[:, :, 0:1], 0.0)
        dve.memset(A[:, :, 0:1], 0.0)
        dve.memset(Z[:, :, 0:1], 0.0)
        dve.memset(m[:, :, 0:1], NEG).then_inc(consts, 1)
        dve.memset(negw_row, 0.0).then_inc(consts, 1)
        norm_dve(dve, s, done)
        dve.wait_ge(consts, ONE + 3)
        dve.tensor_scalar(negw_row, negw_row, w_pos, None, ALU.subtract).then_inc(consts, 1)
        dve.tensor_scalar(neg_w, w_pos, -1.0, None, ALU.mult).then_inc(consts, 1)
        with dve.Fori(0, B // 2) as pair:
            b = pair * 2
            for u in range(2):
                xb = s.xn[:, batch(b + u)]
                dve.wait_ge(shifted, ONE + b + (u + 1))
                dve.wait_ge(mixed, ONE + b * 3)
                dve.tensor_tensor(delta[:, u, :], xb, last[:, u, :], ALU.subtract).then_inc(delta_ready, 1)
                dve.wait_ge(delta_ready, ONE + b + (u + 1))
                dve.wait_ge(krv_ready, ONE + b)
                for out, mix in ((xk, s.mix_k), (xv, s.mix_v), (xr, s.mix_r)):
                    dve.scalar_tensor_tensor(out[:, u, :], delta[:, u, :], mix, last[:, u, :], ALU.mult, ALU.add).then_inc(mixed, 1)
            for u in range(2):
                k, before, now = bank(u, 0), m[:, u, 0:T], m[:, u, 1:T + 1]
                dve.wait_ge(consts, ONE + 5)
                dve.wait_ge(krv_ready, ONE + b + (u + 1))
                dve.wait_ge(num_ready, ONE + b)
                dve.wait_ge(den_ready, ONE + b)
                dve.tensor_tensor_scan(now, negw_row, k, NEG, ALU.add, ALU.max).then_inc(max_ready, 1)
                dve.wait_ge(max_ready, ONE + b + (u + 1))
                dve.scalar_tensor_tensor(peak[:, u, :], k, s.time_first, before, ALU.add, ALU.max).then_inc(peak_ready, 1)
                dve.tensor_tensor(E[:, u, 0, :], k, now, ALU.subtract).then_inc(exponents, 1)
                dve.scalar_tensor_tensor(E[:, u, 1, :], before, neg_w, now, ALU.add, ALU.subtract).then_inc(exponents, 1)
                dve.wait_ge(peak_ready, ONE + b + (u + 1))
                dve.scalar_tensor_tensor(E[:, u, 2, :], k, s.time_first, peak[:, u, :], ALU.add, ALU.subtract).then_inc(exponents, 1)
            for u in range(2):
                v = bank(u, 1)
                ek, decay, own, past = (E[:, u, n, :] for n in range(4))
                dve.wait_ge(exps, ONE + b + (u + 1))
                dve.tensor_tensor(kv[:, u, :], ek, v, ALU.mult).then_inc(kv_ready, 1)
                dve.tensor_tensor_scan(Z[:, u, 1:T + 1], decay, ek, 0.0, ALU.mult, ALU.add).then_inc(sums_ready, 1)
                dve.wait_ge(kv_ready, ONE + b + (u + 1))
                dve.tensor_tensor_scan(A[:, u, 1:T + 1], decay, kv[:, u, :], 0.0, ALU.mult, ALU.add).then_inc(sums_ready, 1)
                dve.wait_ge(sums_ready, ONE + b * 2 + (2 * u + 2))
                dve.wait_ge(before_ready, ONE + b + (u + 1))
                dve.tensor_tensor(peak[:, u, :], past, A[:, u, 0:T], ALU.mult).then_inc(parts, 1)
                dve.tensor_tensor(ek, own, v, ALU.mult).then_inc(parts, 1)
                dve.wait_ge(parts, ONE + b * 3 + (3 * u + 2))
                dve.tensor_tensor(peak[:, u, :], peak[:, u, :], ek, ALU.add).then_inc(parts, 1)
                dve.wait_ge(r_ready, ONE + b + (u + 1))
                dve.wait_ge(parts, ONE + b * 3 + (3 * u + 3))
                dve.wait_ge(mixed, ONE + b * 3 + (3 * u + 3))
                dve.scalar_tensor_tensor(s.xn[:, batch(b + u)], th[:, u, :], 1.0, peak[:, u, :], ALU.add, ALU.mult).then_inc(num_ready, 1)
        dve.wait_ge(num_ready, ONE + B)
        for b in range(B):
            dve.wait_ge(inv_ready, ONE + b + 1)
            dve.scalar_tensor_tensor(s.xn[:, batch(b)], s.xn[:, batch(b)], 0.5, s.rs[:, batch(b)], ALU.mult, ALU.mult).then_inc(wkv_ready, 1)
        for b in range(B):
            dve.wait_ge(out_ready, ONE + b + 1)
            dve.tensor_tensor(s.x[:, batch(b)], s.x[:, batch(b)], bank(b % 2, 3), ALU.add).then_inc(x_added, 1)
        dve.wait_ge(x_added, ONE + B)
    return counters



HEADS, KV, HD = 16, 4, 8
QUAD = HEADS // KV
TILES = T // P
SLOTS = [(i, j) for i in range(3) for j in range(3)]
BIAS_ROW = len(SLOTS) * HD
MAX_ROW = 96


def gqa_layer(nc, s, ctx, done, tag):
    counters = []

    def sem(name):
        counters.append(nc.alloc_semaphore(name=f"{tag}_{name}"))
        return counters[-1]

    misc_ready, misc_read = sem("misc_ready"), sem("misc_read")
    tables = sem("tables")
    split = sem("split")
    scores_ready, scores_read = sem("scores_ready"), sem("scores_read")
    cut, max_cut = sem("cut"), sem("max_cut")
    keyed_ready, exp_ready, pv_ready = sem("keyed_ready"), sem("exp_ready"), sem("pv_ready")
    raw_ready, inv_ready, xv_ready = sem("raw_ready"), sem("inv_ready"), sem("xv_ready")
    zeroed = sem("zeroed")
    v_ready, v_read = sem("v_ready"), sem("v_read")
    ksel_ready, ksel_read = sem("ksel_ready"), sem("ksel_read")

    at = [0]

    def f32(n):
        a = at[0]
        at[0] += n
        return s.work[:, a:a + n]

    def bf16(n):
        return f32(n // 2).bitcast(BF16)

    sel = bf16(GQA_BF16_COLS)
    sel_q = sel[:, 0:HEADS * 3 * P].rearrange("p (h i r) -> p h i r", h=HEADS, i=3)
    sel_k = sel[:, HEADS * 3 * P:(HEADS + KV) * 3 * P].rearrange("p (h i r) -> p h i r", h=KV, i=3)
    ident_b = sel[:, (HEADS + KV) * 3 * P:(HEADS + KV) * 3 * P + P]
    parts = bf16(6 * T).rearrange("p (a i t) -> p a i t", a=2, i=3)
    rest = f32(2 * T).rearrange("p (a t) -> p a t", a=2)
    qop = bf16(HEADS * T).rearrange("p (q i t) -> p q i t", q=KV, i=QUAD)
    kop = bf16(KV * T).rearrange("p (g t) -> p g t", g=KV)
    vaug = f32(TILES * KV * 32).rearrange("p (n g c) -> p n g c", n=TILES, g=KV)
    mx = f32(2 * 16).rearrange("p (a n) -> p a n", a=2)
    mrest = f32(2 * 16).rearrange("p (a n) -> p a n", a=2)
    mrow = bf16(2 * 16 * 32).rearrange("p (a n c) -> p a n c", a=2, n=16)
    E = f32(2 * QUAD * T).rearrange("p (a i t) -> p a i t", a=2, i=QUAD)
    raw = f32(T)
    inv = f32(16)
    on = f32(T).rearrange("p (n h d) -> p n h d", n=TILES, h=HEADS)
    oT = f32(T)
    xv = f32(T)
    assert at[0] <= s.work.shape[1]
    misc, pv = s.bank(7), s.bank(6)

    opening_2 = ["k", "q"]
    opening_3 = [("ksel", 0)] + [("qsel", q, i) for q in range(2) for i in range(QUAD)]

    def numbered(opens):
        uses = []
        for q in range(KV):
            if q + 2 < KV:
                uses += [("qsel", q + 2, i) for i in range(QUAD)]
            elif opens:
                uses += opening_2 if q == 2 else opening_3
            uses.append(("turn", q))
        return {name: n for n, name in enumerate(uses + ["back", "out"])}

    pre, full, short = {name: n for n, name in enumerate(opening_2 + opening_3)}, numbered(True), numbered(False)
    U0, U = len(pre), len(full)
    before_loop = lambda name: pre[name]
    in_loop = lambda b: lambda name: U0 + b * U + full[name]
    in_last = lambda name: U0 + (B - 1) * U + short[name]
    ALL_MISC = U0 + (B - 1) * U + len(short)
    RING = 16 + QUAD
    SPLITS = 6
    start_counters(nc, counters)
    block = ctx.enter_context(nc.Block())

    @block.sync
    def _(sp):
        s.load_rest(sp)
        sp.dma_start(sel, s.gqa_tables).then_inc(tables, 16)
        sp.wait_ge(tables, ONE + 16)

    @block.gpsimd
    def _(pool):
        pool.wait_ge(tables, ONE + 16)
        s.clear_rows(pool)

    @block.tensor
    def _(pe):
        norm_pe(pe, s, done)
        s.rest_there(pe)
        pe.wait_ge(tables, ONE + 16)
        pe.wait_ge(zeroed, ONE + 3)

        def misc_free(at, name):
            pe.wait_ge(misc_read, ONE + at(name))

        def project(at, b, name, weight):
            misc_free(at, name)
            pe.matmul(misc, weight, s.xn[:, batch(b)], start=True, stop=True).then_inc(misc_ready, 1)

        def place(bank, selector, source, ready):
            for n in range(3):
                mm = pe.matmul(bank, selector[:, n, :], parts[:, source, n, :], start=n == 0, stop=n == 2)
            mm.then_inc(ready, 1)

        def first_keys(at, b):
            misc_free(at, ("ksel", 0))
            pe.wait_ge(split, ONE + b * SPLITS + SPLITS // 2)
            place(misc, sel_k[:, 0], 1, misc_ready)

        def qsel(at, b, q, i):
            misc_free(at, ("qsel", q, i))
            pe.wait_ge(split, ONE + b * SPLITS + SPLITS)
            place(misc, sel_q[:, q * QUAD + i], 0, misc_ready)

        def scores(at, b, q, n):
            r = q * RING + n
            i, qt = n // TILES, n % TILES
            if qt == 0 and q != 1:
                pe.wait_ge(misc_read, ONE + at(("qsel", q, i)) + 1)
            if q and n == 0:
                pe.wait_ge(ksel_read, ONE + b * (KV - 1) + q)
            pe.wait_ge(scores_read, ONE + b * (KV * RING) + max(0, r - 1))
            pe.matmul(s.bank(r % 2), qop[:, q, i, qt * P:(qt + 1) * P], kop[:, q, :],
                      start=True, stop=True).then_inc(scores_ready, 1)

        def max_rows(b, q):
            pe.wait_ge(max_cut, ONE + b * KV + (q + 1))
            for i in range(QUAD):
                r = q * RING + 16 + i
                pe.wait_ge(scores_read, ONE + b * (KV * RING) + (r - 1))
                for qt in range(TILES):
                    mm = pe.matmul(s.bank(r % 2)[MAX_ROW:P, qt * P:(qt + 1) * P], mrow[:, q % 2, 4 * i + qt, :],
                                   ident_b, start=True, stop=True)
                mm.then_inc(scores_ready, 1)

        def keyed(b, q, kt, half):
            g = q * 8 + kt * 2 + half
            if g < 2:
                pe.wait_ge(ksel_read, ONE + b * (KV - 1) + (KV - 1))
            pe.wait_ge(scores_read, ONE + b * (KV * RING) + (q * RING + 16 + 2 * half + 2))
            pe.wait_ge(exp_ready, ONE + b * 32 + max(0, g - 1))
            for j in range(2):
                mm = pe.matmul(s.bank(2 + 2 * half + j), kop[:, q, kt * P:(kt + 1) * P],
                               qop[:, q, 2 * half + j, :], start=True, stop=True)
            mm.then_inc(keyed_ready, 1)

        def values(b, q, kt):
            pe.wait_ge(exp_ready, ONE + b * 32 + (q * 8 + kt * 2 + 2))
            if kt == 0:
                pe.wait_ge(raw_ready, ONE + b * KV + q)
                pe.wait_ge(v_read, ONE + b + 1)
            for i in range(QUAD):
                mm = pe.matmul(pv[32 * i:32 * i + 32, :], vaug[:, kt, q, :], E[:, kt % 2, i, :],
                               start=kt == 0, stop=kt == TILES - 1)
            mm.then_inc(pv_ready, 1)

        def other_keys(b):
            for g in range(1, KV):
                pe.wait_ge(exp_ready, ONE + b * 32)
                place(s.bank(1 + g), sel_k[:, g], 1, ksel_ready)

        def own_values(b):
            pe.wait_ge(xv_ready, ONE + b + 1)
            pe.wait_ge(raw_ready, ONE + b * KV)
            for n in range(TILES):
                mm = pe.matmul(pv[:, 32 * n:32 * n + 32], xv[:, n * P:(n + 1) * P], s.Wv, start=True, stop=True)
            mm.then_inc(v_ready, 1)

        def turn(at, b, q):
            pe.wait_ge(raw_ready, ONE + b * KV + (q + 1))
            misc_free(at, ("turn", q))
            for n in range(TILES):
                mm = pe.transpose(misc[:, n * P:(n + 1) * P], raw[:, n * P:(n + 1) * P], s.ident)
            mm.then_inc(misc_ready, 1)

        def batch_of_quads(at, b, opens):
            for q in range(KV):
                for n in range(16):
                    if q + 1 < KV:
                        scores(at, b, q + 1, n)
                    if n % 2 == 0:
                        keyed(b, q, n // 4, n // 2 % 2)
                    if n % 4 == 1 and q + 2 < KV:
                        qsel(at, b, q + 2, n // 4)
                    if opens and q == 2 and n == 1:
                        project(at, b + 1, "k", s.Wk)
                    if opens and q == 2 and n == 7:
                        project(at, b + 1, "q", s.Wq)
                    if opens and q == 3:
                        if n == 0:
                            first_keys(at, b + 1)
                        if n == 1:
                            qsel(at, b + 1, 0, 0)
                        elif n % 2 == 0 and n:
                            qsel(at, b + 1, n // 8, n // 2 % 4)
                        if n > 2:
                            scores(at, b + 1, 0, n - 3)
                    if n % 4 == 3 and n > 4:
                        values(b, q, n // 4 - 1)
                values(b, q, TILES - 1)
                if q + 1 < KV:
                    max_rows(b, q + 1)
                    turn(at, b, q)
            if opens:
                for n in range(13, 16):
                    scores(at, b + 1, 0, n)
                other_keys(b + 1)
            turn(at, b, KV - 1)
            if opens:
                own_values(b + 1)
                max_rows(b + 1, 0)
            misc_free(at, "back")
            for n in range(TILES):
                mm = pe.transpose(misc[:, n * P:(n + 1) * P], on[:, n, :, :].rearrange("p h d -> p (h d)"), s.ident)
            mm.then_inc(misc_ready, 1)
            misc_free(at, "out")
            pe.matmul(misc, s.Wo, oT, start=True, stop=True).then_inc(misc_ready, 1)

        pe.wait_ge(s.normed, ONE + done + B)
        project(before_loop, 0, "k", s.Wk)
        project(before_loop, 0, "q", s.Wq)
        first_keys(before_loop, 0)
        for i in range(QUAD):
            qsel(before_loop, 0, 0, i)
        for n in range(16):
            scores(before_loop, 0, 0, n)
            if n % 4 == 3:
                qsel(before_loop, 0, 1, n // 4)
        other_keys(0)
        own_values(0)
        max_rows(0, 0)
        pe.wait_ge(misc_read, ONE + U0)
        with pe.Fori(0, B - 1) as b:
            batch_of_quads(in_loop(b), b, True)
        batch_of_quads(in_last, B - 1, False)

    @block.scalar
    def _(act):
        norm_act(act, s, done)
        s.rest_there(act)

        def qsel(at, q, i):
            act.wait_ge(misc_ready, ONE + at(("qsel", q, i)) + 1)
            act.activation(qop[:, q, i, :], misc, ACT.Identity,
                           bias=s.slopes[:, q * QUAD + i:q * QUAD + i + 1]).then_inc(misc_read, 1)

        def keep_tokens(b):
            act.wait_ge(s.normed, ONE + b + (done + 1))
            act.wait_ge(v_ready, ONE + b)
            act.activation(xv, s.xn[:, batch(b)], ACT.Copy).then_inc(xv_ready, 1)

        def batch_of_quads(at, b, opens):
            for q in range(KV):
                if opens and q == 3:
                    keep_tokens(b + 1)
                for n in range(0, 16, 2):
                    kt, half, g = n // 4, n // 2 % 2, q * 8 + n // 2
                    act.wait_ge(keyed_ready, ONE + b * 32 + (g + 1))
                    act.wait_ge(pv_ready, ONE + b * 16 + max(0, 4 * q + kt - 1))
                    act.activation(E[:, kt % 2, 2 * half:2 * half + 2, :], s.psum[:, 2 + 2 * half:4 + 2 * half, :],
                                   ACT.Exp).then_inc(exp_ready, 1)
                    if n % 4 == 2 and q + 2 < KV:
                        qsel(at, q + 2, n // 4)
                    if opens and q == 3:
                        qsel(at, n // 8, n // 2 % 4)
                act.wait_ge(pv_ready, ONE + b * 16 + 4 * q + 4)
                if q:
                    act.wait_ge(misc_ready, ONE + at(("turn", q - 1)) + 1)
                act.activation(raw, pv, ACT.Copy).then_inc(raw_ready, 1)

        keep_tokens(0)
        for q in range(2):
            for i in range(QUAD):
                qsel(before_loop, q, i)
        with act.Fori(0, B - 1) as b:
            batch_of_quads(in_loop(b), b, True)
        batch_of_quads(in_last, B - 1, False)

    @block.vector
    def _(dve):
        dve.memset(mrow, 0.0).then_inc(zeroed, 1)
        dve.memset(vaug, 0.0).then_inc(zeroed, 1)
        dve.wait_ge(zeroed, ONE + 2)
        dve.memset(vaug[:, :, :, HD:HD + 1], 1.0).then_inc(zeroed, 1)
        norm_dve(dve, s, done)
        s.rest_there(dve)
        s.dequantise(dve)
        dve.wait_ge(zeroed, ONE + 3)

        def misc_there(at, name):
            dve.wait_ge(misc_ready, ONE + at(name) + 1)

        def cut_in_parts(at, b, name, steps=range(4)):
            first, a, scale = (0, 1, 1.0) if name == "k" else (3, 0, HD ** -0.5)
            done_before = ONE + b * SPLITS + first
            for step in steps:
                if step == 0:
                    misc_there(at, name)
                    dve.wait_ge(split, done_before)
                    dve.tensor_scalar(parts[:, a, 0, :], misc, scale, None, ALU.mult).then_inc(split, 1)
                elif step == 1:
                    dve.wait_ge(split, done_before + 1)
                    dve.scalar_tensor_tensor(rest[:, a, :], misc, scale, parts[:, a, 0, :], ALU.mult, ALU.subtract).then_inc(misc_read, 1)
                elif step == 2:
                    dve.wait_ge(misc_read, ONE + at(name) + 1)
                    dve.tensor_copy(parts[:, a, 1, :], rest[:, a, :]).then_inc(split, 1)
                else:
                    dve.wait_ge(split, done_before + 2)
                    dve.tensor_tensor(parts[:, a, 2, :], rest[:, a, :], parts[:, a, 1, :], ALU.subtract).then_inc(split, 1)

        def first_keys(at):
            misc_there(at, ("ksel", 0))
            dve.tensor_tensor(kop[:, 0, :], misc, s.key_rows, ALU.add).then_inc(misc_read, 1)

        def maxima(b, q, n):
            dve.wait_ge(scores_ready, ONE + b * (KV * RING) + (q * RING + n + 1))
            dve.tensor_reduce(mx[:, q % 2, n:n + 1], s.bank((q * RING + n) % 2), AX.X, ALU.max).then_inc(scores_read, 1)

        def max_parts(b, q):
            m, r, c = mx[:, q % 2, :], mrest[:, q % 2, :], b * (3 * KV) + 3 * q
            dve.wait_ge(scores_read, ONE + b * (KV * RING) + (q * RING + 16))
            dve.tensor_scalar(mrow[:, q % 2, :, 0], m, -1.0, None, ALU.mult).then_inc(cut, 1)
            dve.wait_ge(cut, ONE + c + 1)
            dve.scalar_tensor_tensor(r, m, -1.0, mrow[:, q % 2, :, 0], ALU.mult, ALU.subtract).then_inc(cut, 1)
            dve.wait_ge(cut, ONE + c + 2)
            dve.tensor_copy(mrow[:, q % 2, :, 1], r).then_inc(cut, 1)
            dve.wait_ge(cut, ONE + c + 3)
            dve.tensor_tensor(mrow[:, q % 2, :, 2], r, mrow[:, q % 2, :, 1], ALU.subtract).then_inc(max_cut, 1)

        def max_rows(b, q):
            for i in range(QUAD):
                r = q * RING + 16 + i
                dve.wait_ge(scores_ready, ONE + b * (KV * RING) + (r + 1))
                dve.tensor_copy(qop[MAX_ROW:P, q, i, :], s.bank(r % 2)[MAX_ROW:P, :]).then_inc(scores_read, 1)

        def divide(at, b, q):
            misc_there(at, ("turn", q))
            turned = misc.rearrange("p (n i c) -> p n i c", n=TILES, i=QUAD)
            dve.wait_ge(misc_read, ONE + at(("turn", q)))
            dve.reciprocal(inv.rearrange("p (n i) -> p n i", n=TILES), turned[:, :, :, HD]).then_inc(inv_ready, 1)
            dve.wait_ge(inv_ready, ONE + b * KV + (q + 1))
            for n in range(TILES):
                last = dve.tensor_tensor(on[:, n, q * QUAD:(q + 1) * QUAD, :], turned[:, n, :, 0:HD],
                                         inv[:, 4 * n:4 * n + 4].unsqueeze(2).to_broadcast([P, QUAD, HD]), ALU.mult)
            last.then_inc(misc_read, 1)

        def other_keys_and_values(b):
            for g in range(1, KV):
                dve.wait_ge(ksel_ready, ONE + b * (KV - 1) + g)
                dve.tensor_tensor(kop[:, g, :], s.bank(1 + g), s.key_rows, ALU.add).then_inc(ksel_read, 1)
            dve.wait_ge(v_ready, ONE + b + 1)
            dve.wait_ge(pv_ready, ONE + b * 16)
            dve.tensor_copy(vaug[:, :, :, 0:HD], pv[:, 0:TILES * 32].rearrange("p (n g d) -> p n g d", n=TILES, g=KV)).then_inc(v_read, 1)

        def batch_of_quads(at, b, opens):
            for q in range(KV):
                if q + 1 < KV:
                    for n in range(16):
                        maxima(b, q + 1, n)
                        if opens and q == 2 and 3 <= n < 7:
                            cut_in_parts(at, b + 1, "k", [n - 3])
                        if opens and q == 2 and 9 <= n < 13:
                            cut_in_parts(at, b + 1, "q", [n - 9])
                    max_parts(b, q + 1)
                    max_rows(b, q + 1)
                elif opens:
                    first_keys(at)
                    for n in range(16):
                        maxima(b + 1, 0, n)
                    max_parts(b + 1, 0)
                divide(at, b, q)
            if opens:
                other_keys_and_values(b + 1)
                max_rows(b + 1, 0)
            misc_there(at, "back")
            dve.tensor_copy(oT, misc).then_inc(misc_read, 1)
            misc_there(at, "out")
            dve.tensor_tensor(s.x[:, batch(b)], s.x[:, batch(b)], misc, ALU.add).then_inc(misc_read, 1)

        cut_in_parts(before_loop, 0, "k")
        cut_in_parts(before_loop, 0, "q")
        first_keys(before_loop)
        for n in range(16):
            maxima(0, 0, n)
        max_parts(0, 0)
        other_keys_and_values(0)
        max_rows(0, 0)
        with dve.Fori(0, B - 1) as b:
            batch_of_quads(in_loop(b), b, True)
        batch_of_quads(in_last, B - 1, False)
        dve.wait_ge(misc_read, ONE + ALL_MISC)
    return counters



IH, ID = 16, 64
SEG = 32
SEGS = T // SEG
CH = IH * ID // P
G = 4
MW = ID + 1
SWAP = [i ^ 1 for i in range(32)]


def infini_layer(nc, s, ctx, done, tag):
    counters = []

    def sem(name):
        counters.append(nc.alloc_semaphore(name=f"{tag}_{name}"))
        return counters[-1]

    affine = sem("affine")
    proj_ready, exp_ready, elu_ready = sem("proj_ready"), sem("exp_ready"), sem("elu_ready")
    rot_ready, cos_ready, sin_ready, roped = (
        sem("rot_ready"), sem("cos_ready"), sem("sin_ready"), (sem("roped_q"), sem("roped_k")))
    scores_ready, masked, row_max, shifted = sem("scores_ready"), sem("masked"), sem("row_max"), sem("shifted")
    sm_exp, row_sum, weight_ready, probs, turned = (
        sem("sm_exp"), sem("row_sum"), sem("weight"), sem("probs"), sem("turned"))
    v_ready, v_kept = sem("v_ready"), sem("v_kept")
    skt_ready, skt_kept = sem("skt_ready"), sem("skt_kept")
    recall_k, recall_q, k_inv, prev_ready, d_dve, d_pool = (
        sem("recall_k"), sem("recall_q"), sem("k_inv"), sem("prev"), sem("d_dve"), sem("d_pool"))
    updated, state_ready = sem("updated"), sem("state_ready")
    q_den, q_out, pv_ready, o_ready, ot_ready, ot_kept = (
        sem("q_den"), sem("q_out"), sem("pv_ready"), sem("o_ready"), sem("ot_ready"), sem("ot_kept"))
    out_ready, x_added, consts, beta_ready = sem("out_ready"), sem("x_added"), sem("consts"), sem("beta_ready")

    at = [0]

    def f32(n):
        a = at[0]
        at[0] += n
        return s.work[:, a:a + n]

    sq = f32(CH * T).rearrange("p (c t) -> p c t", c=CH)
    sk = f32(CH * T).rearrange("p (c t) -> p c t", c=CH)
    v = f32(SEGS * 256).rearrange("p (t n) -> p t n", t=SEGS)
    state = f32(CH * 2 * MW).rearrange("p (c n) -> p c n", c=CH)
    PT = f32(SEGS * 4 * SEG).rearrange("p (n m) -> p n m", n=4)
    D = f32(16 * MW).rearrange("p (a g n) -> p a g n", a=4, g=G)
    ones_z = f32(G * MW)
    z0 = f32(ID)
    xa = f32(T)
    betas = f32(8)
    beta, gain = betas[:, 0:4], betas[:, 4:8]
    e_buf = f32(2 * T).rearrange("p (a t) -> p a t", a=2)
    rot = f32(2 * T).rearrange("p (a t) -> p a t", a=2)
    tc = f32(2 * T).rearrange("p (a t) -> p a t", a=2)
    zr = f32(4 * T).rearrange("p (a t) -> p a t", a=4)
    stat = f32(3 * 64).rearrange("p (a n) -> p a n", a=3)
    relu = f32(2 * T).rearrange("p (a t) -> p a t", a=2)
    skt = f32(2 * 256).rearrange("p (a n) -> p a n", a=2)
    prev = f32(256).rearrange("p (n d) -> p n d", n=4)
    mo = f32(256).rearrange("p (n d) -> p n d", n=4)
    o = f32(2 * 256).rearrange("p (a n) -> p a n", a=2)
    small = f32(16)
    assert at[0] <= s.work.shape[1]
    sm = s.rs[:, 0:4 * T].rearrange("p (n m) -> p n m", n=4)
    oT = s.rs[:, 0:CH * T].rearrange("p (c t) -> p c t", c=CH)
    wq = lambda c: s.w_qkv[:, c * P:(c + 1) * P]
    wk = lambda c: s.w_qkv[:, (CH + c) * P:(CH + c + 1) * P]
    wv = s.w_qkv[:, 2 * CH * P:3 * CH * P].rearrange("p (j g n) -> p g j n", j=2, g=G)
    tok = lambda t: slice(t * SEG, (t + 1) * SEG)
    part = lambda g: slice(32 * g, 32 * g + 32)
    half = lambda e: slice(64 * e, 64 * e + 64)
    tile_of = lambda j, e: 2 * e + j
    TILE_ORDER = [(0, 0), (0, 1), (1, 0), (1, 1)]
    DS = 4 * (SEGS - 1)
    NP = 2 * CH
    start_counters(nc, counters)
    block = ctx.enter_context(nc.Block())

    @block.tensor
    def _(pe):
        norm_pe(pe, s, done)
        norm_pe(pe, s, done + B, again=True)
        pe.wait_ge(consts, ONE + 5)
        def project(b, n):
            pe.wait_ge(rot_ready, ONE + b * NP + max(0, n - 2))
            pe.matmul(s.bank(n % 3), (wk if n % 2 else wq)(n // 2), xa, start=True, stop=True).then_inc(proj_ready, 1)

        def open_batch(b):
            pe.wait_ge(affine, ONE + b + 1)
            pe.wait_ge(prev_ready, ONE + b * (2 * SEGS))
            project(b, 0)
            project(b, 1)

        def batch_of_segments(b, opens):
            def scores(c):
                j, g = c // G, c % G
                for t in range(SEGS):
                    for e in range(2):
                        mm = pe.matmul(s.psum[part(g), 4 + tile_of(j, e), tok(t)],
                                       zr[half(e), (2 * c) % 4, tok(t)], zr[half(e), (2 * c + 1) % 4, tok(t)],
                                       start=True, stop=True)
                mm.then_inc(scores_ready, 1)

            def roped_both(c):
                for z in range(2):
                    pe.wait_ge(roped[z], ONE + b * CH + (c + 1))

            def keep_clock(bank, n):
                for _ in range(n):
                    pe.matmul(bank, s.avg, xa, start=True, stop=True)

            def values(n, warm=0):
                pe.wait_ge(v_kept, ONE + b * 8 + n)
                keep_clock(s.bank(3), warm)
                for u in range(2):
                    for g in range(G):
                        mm = pe.matmul(s.bank(3)[part(g), 256 * u:256 * u + 256], xa[:, tok(2 * n + u)], wv[:, g],
                                       start=True, stop=True)
                mm.then_inc(v_ready, 1)

            for c in range(CH):
                if c > 1:
                    roped_both(c - 2)
                if c == G + 2:
                    pe.wait_ge(x_added, ONE + b)
                if c:
                    project(b, 2 * c)
                if c > 1:
                    scores(c - 2)
                if c:
                    project(b, 2 * c + 1)
                if c < CH - 2:
                    values(c)
            for c in (CH - 2, CH - 1):
                roped_both(c)
                values(c, 0 if c == CH - 1 else 0)
                scores(c)

            def keys_turned(t):
                pe.wait_ge(skt_kept, ONE + b * SEGS + t)
                for j in range(2):
                    for g in range(G):
                        mm = pe.matmul(s.bank(5)[part(g), P * j:P * j + P], sk[:, 4 * j + g, tok(t)], s.ident,
                                       start=True, stop=True)
                mm.then_inc(skt_ready, 1)

            def out_turned(t):
                pe.wait_ge(o_ready, ONE + b * SEGS + (t + 1))
                pe.wait_ge(ot_kept, ONE + b * SEGS + t)
                for j in range(2):
                    mm = pe.transpose(s.bank(6)[:, P * j:P * j + P], o[:, t % 2, P * j:P * j + P], s.ident)
                mm.then_inc(ot_ready, 1)

            pe.wait_ge(elu_ready, ONE + b * NP + NP)
            keep_clock(s.bank(0), 7)
            pe.wait_ge(v_kept, ONE + b * 8 + 8)
            pe.wait_ge(elu_ready, ONE + b * NP + NP)
            pe.wait_ge(masked, ONE + b * 4 + 4)
            for j in range(2):
                for e in range(2):
                    mm = pe.matmul(s.bank(2 + j)[half(e), 0:G * MW], z0, ones_z, start=True, stop=False, skip_group_check=True)
                mm.then_inc(updated, 1)
            keys_turned(0)
            pe.wait_ge(turned, ONE + b * 4 + 4)

            def recall(bank, at, operand, t, j, done_sem, before):
                for g in range(G):
                    if g == G - 1:
                        pe.wait_ge(*before)
                    mm = pe.matmul(bank[part(g), at:at + 2 * MW], operand[:, 4 * j + g, tok(t)],
                                   state[:, 4 * j + g, :], start=True, stop=True)
                mm.then_inc(done_sem, 1)

            def local(t, g):
                for j in range(2):
                    for e in range(2):
                        a = 2 * j + e
                        mm = pe.matmul(s.bank(4)[part(g), ID * a:ID * a + ID], PT[part(g), tile_of(j, e), tok(t)],
                                       v[part(g), t, ID * a:ID * a + ID], start=True, stop=True,
                                       tile_position=(32 * g, 32 * g))
                mm.then_inc(pv_ready, 1)

            for t in range(SEGS):
                for j in range(2):
                    pe.wait_ge(state_ready, ONE + b * (4 * SEGS) + (4 * t + 2 * j + 2))
                    pe.wait_ge(prev_ready, ONE + b * 32 + max(0, 2 * t + j - 1))
                    recall(s.bank(j), 0, sk, t, j, recall_k,
                           (pv_ready, ONE + b * (G * SEGS) + (G * t + 2)) if j
                           else (o_ready, ONE + b * SEGS + t))
                    local(t, 2 * j)
                    pe.wait_ge(q_out, ONE + b * SEGS + t)
                    recall(s.bank(7), j * 2 * MW, sq, t, j, recall_q,
                           (pv_ready, ONE + b * (G * SEGS) + (G * t + 2 * j + 1)))
                    local(t, 2 * j + 1)
                if t + 1 < SEGS:
                    keys_turned(t + 1)
                if t:
                    out_turned(t - 1)
                if t + 1 < SEGS:
                    for j in range(2):
                        pe.wait_ge(d_dve, ONE + b * DS + (4 * t + 2 * j + 2))
                        pe.wait_ge(d_pool, ONE + b * DS + (4 * t + 2 * j + 2))
                        pe.wait_ge(skt_kept, ONE + b * SEGS + (t + 1))
                        for e in range(2):
                            mm = pe.matmul(s.bank(2 + j)[half(e), 0:G * MW], skt[:, t % 2, P * j + 64 * e:P * j + 64 * e + 64],
                                           D[:, 2 * j + e, :, :].rearrange("p g n -> p (g n)"),
                                           start=False, stop=t == SEGS - 2, skip_group_check=True)
                        mm.then_inc(updated, 1)
            out_turned(SEGS - 1)
            pe.wait_ge(ot_kept, ONE + b * SEGS + SEGS)
            pe.wait_ge(q_out, ONE + b * SEGS + SEGS)
            if opens:
                open_batch(b + 1)
            for c in range(CH):
                mm = pe.matmul(s.bank(7), s.w_out[:, c * P:(c + 1) * P], oT[:, c, :], start=c == 0, stop=c == CH - 1)
            mm.then_inc(out_ready, 1)

        open_batch(0)
        with pe.Fori(0, B - 1) as b:
            batch_of_segments(b, True)
        batch_of_segments(B - 1, False)

    @block.scalar
    def _(act):
        act.activation(beta, s.mem_beta, ACT.Sigmoid).then_inc(beta_ready, 1)
        act.activation(gain, s.mem_beta, ACT.Sigmoid, scale=-1.0).then_inc(beta_ready, 1)
        norm_act(act, s, done)
        norm_act(act, s, done + B)
        with act.Fori(0, B) as b:
            def softmax_exp(n):
                j, e = TILE_ORDER[n]
                act.wait_ge(shifted, ONE + b * 4 + (n + 1))
                act.activation(sm[:, tile_of(j, e), :], sm[:, tile_of(j, e), :], ACT.Exp).then_inc(sm_exp, 1)

            def values_kept(n):
                act.wait_ge(v_ready, ONE + b * 8 + (n + 1))
                act.activation(v[:, 2 * n:2 * n + 2, :], s.bank(3).rearrange("p (u m) -> p u m", u=2), ACT.Copy).then_inc(v_kept, 1)

            act.wait_ge(ot_ready, ONE + b * SEGS)
            for n in range(NP):
                act.wait_ge(proj_ready, ONE + b * NP + (n + 1))
                act.wait_ge(elu_ready, ONE + b * NP + max(0, n - 1))
                act.activation(e_buf[:, n % 2, :], s.bank(n % 3), ACT.Exp)
                act.activation(relu[:, n % 2, :], s.bank(n % 3), ACT.Relu).then_inc(exp_ready, 1)
                if n % 2 and n // 2 < CH - 2:
                    values_kept(n // 2)
            values_kept(CH - 2)
            softmax_exp(0)
            softmax_exp(1)
            values_kept(CH - 1)
            softmax_exp(2)
            softmax_exp(3)

            def keys_kept(t):
                act.wait_ge(skt_ready, ONE + b * SEGS + (t + 1))
                act.wait_ge(updated, ONE + b * (2 * SEGS) + max(0, 2 * t))
                act.activation(skt[:, t % 2, :], s.bank(5)[:, 0:256], ACT.Copy).then_inc(skt_kept, 1)

            def out_kept(t):
                act.wait_ge(ot_ready, ONE + b * SEGS + (t + 1))
                act.activation(oT[:, :, tok(t)], s.bank(6)[:, 0:256].rearrange("p (c t) -> p c t", c=CH), ACT.Copy).then_inc(ot_kept, 1)

            act.wait_ge(turned, ONE + b * 4 + 4)
            for t in range(SEGS):
                for j in range(2):
                    act.wait_ge(updated, ONE + b * (2 * SEGS) + (2 * t + j + 1))
                    if t:
                        act.wait_ge(recall_q, ONE + b * (2 * SEGS) + (2 * t - 1 + j))
                    else:
                        act.wait_ge(recall_q, ONE + b * (2 * SEGS))
                    for e in range(2):
                        act.activation(state[half(e), 4 * j:4 * j + 4, MW * e:MW * e + MW],
                                       s.bank(2 + j)[half(e), 0:G * MW].rearrange("p (g n) -> p g n", g=G),
                                       ACT.Copy).then_inc(state_ready, 1)
                keys_kept(t)
                if t > 1:
                    out_kept(t - 2)
            out_kept(SEGS - 2)
            out_kept(SEGS - 1)

    @block.gpsimd
    def _(pool):
        with pool.Fori(0, B) as b:
            grid = lambda a: a.rearrange("p (a k) -> p a k", k=SEG)

            def shift(n):
                j, e = TILE_ORDER[n]
                tile = grid(sm[:, tile_of(j, e), :])
                pool.wait_ge(row_max, ONE + b * 4 + (n + 1))
                pool.tensor_tensor(tile, tile, stat[:, 0, 16 * n:16 * n + 16].unsqueeze(2).to_broadcast([P, 16, SEG]),
                                   ALU.subtract).then_inc(shifted, 1)

            def weigh(n):
                j, e = TILE_ORDER[n]
                tile = grid(sm[:, tile_of(j, e), :])
                pool.wait_ge(weight_ready, ONE + b * 8 + (2 * n + 2))
                pool.tensor_tensor(tile, tile, stat[:, 1, 16 * n:16 * n + 16].unsqueeze(2).to_broadcast([P, 16, SEG]),
                                   ALU.mult).then_inc(probs, 1)

            for n in range(NP):
                pool.wait_ge(rot_ready, ONE + b * NP + (n + 1))
                pool.tensor_tensor(rot[:, n % 2, :], rot[:, n % 2, :], s.rope_sin, ALU.mult).then_inc(sin_ready, 1)
                if n % 2:
                    pool.wait_ge(sin_ready, ONE + b * NP + (n + 1))
                    pool.wait_ge(scores_ready, ONE + b * CH + max(0, n // 2 - 1))
                    pool.tensor_tensor(zr[:, n % 4, :], tc[:, n % 2, :], rot[:, n % 2, :], ALU.add).then_inc(roped[1], 1)
            shift(0)
            shift(1)
            weigh(0)
            weigh(1)
            for n in (2, 3):
                shift(n)
            for n in (2, 3):
                weigh(n)
            for t in range(SEGS - 1):
                for j in range(2):
                    pool.wait_ge(prev_ready, ONE + b * 32 + (2 * t + j + 1))
                    pool.wait_ge(v_kept, ONE + b * 8 + 8)
                    pool.wait_ge(updated, ONE + b * (2 * SEGS) + (2 * t + j + 1))
                    for g in (2, 3):
                        pool.tensor_tensor(D[part(g), 2 * j:2 * j + 2, g, 0:ID],
                                           v[part(g), t, P * j:P * j + P].rearrange("p (e d) -> p e d", e=2),
                                           prev[part(g), 2 * j:2 * j + 2, :], ALU.subtract).then_inc(d_pool, 1)

    @block.vector
    def _(dve):
        dve.memset(z0, 1e-6 / P).then_inc(consts, 1)
        dve.memset(ones_z, 0.0).then_inc(consts, 1)
        dve.memset(D, 0.0).then_inc(consts, 1)
        dve.memset(state, 0.0).then_inc(consts, 1)
        dve.wait_ge(consts, ONE + 4)
        dve.memset(ones_z.rearrange("p (g n) -> p g n", g=G)[:, :, ID:MW], 1.0)
        for g in range(G):
            last = dve.memset(D[part(g), :, g, ID:MW], 1.0)
        last.then_inc(consts, 1)
        norm_dve(dve, s, done)
        norm_dve(dve, s, done + B, again=True)
        dve.wait_ge(beta_ready, ONE + 2)

        def open_batch(b):
            dve.wait_ge(s.normed, ONE + b + (done + B + 1))
            dve.wait_ge(v_ready, ONE + b * 8)
            dve.tensor_scalar(xa, s.xn[:, batch(b)], s.ln_g, s.ln_b, ALU.mult, ALU.add).then_inc(affine, 1)

        def rope_sum(b, n):
            dve.wait_ge(sin_ready, ONE + b * NP + (n + 1))
            dve.wait_ge(cos_ready, ONE + b * NP + (n + 1))
            dve.wait_ge(scores_ready, ONE + b * CH + max(0, n // 2 - 1))
            dve.tensor_tensor(zr[:, n % 4, :], tc[:, n % 2, :], rot[:, n % 2, :], ALU.add).then_inc(roped[0], 1)

        def take_projection(b, n):
            c, bank = n // 2, s.bank(n % 3)
            dve.wait_ge(exp_ready, ONE + b * NP + (n + 1))
            dve.wait_ge(roped[n % 2], ONE + b * CH + c)
            dve.tensor_tensor(tc[:, n % 2, :], bank, s.rope_cos, ALU.mult).then_inc(cos_ready, 1)
            dve.stream_shuffle(rot[:, n % 2, :], bank, SWAP).then_inc(rot_ready, 1)
            dve.scalar_tensor_tensor((sk if n % 2 else sq)[:, c, :], e_buf[:, n % 2, :], 1.0, relu[:, n % 2, :],
                                     ALU.min, ALU.add).then_inc(elu_ready, 1)
            if n % 2:
                rope_sum(b, n - 1)

        def batch_of_segments(b, opens):
            grid = lambda a: a.rearrange("p (a k) -> p a k", k=SEG)

            def row_maxima(n):
                j, e = TILE_ORDER[n]
                tile = sm[:, tile_of(j, e), :]
                dve.wait_ge(scores_ready, ONE + b * CH + (4 * j + 4))
                dve.wait_ge(out_ready, ONE + b)
                dve.scalar_tensor_tensor(grid(tile), grid(s.bank(4 + tile_of(j, e))), ID ** -0.5,
                                         s.causal.unsqueeze(1).to_broadcast([P, 16, SEG]), ALU.mult, ALU.add).then_inc(masked, 1)
                dve.wait_ge(masked, ONE + b * 4 + (n + 1))
                dve.tensor_reduce(stat[:, 0, 16 * n:16 * n + 16], grid(tile), AX.X, ALU.max).then_inc(row_max, 1)

            def row_weights(n):
                j, e = TILE_ORDER[n]
                st = slice(16 * n, 16 * n + 16)
                dve.wait_ge(sm_exp, ONE + b * 4 + (n + 1))
                dve.tensor_reduce(stat[:, 2, st], grid(sm[:, tile_of(j, e), :]), AX.X, ALU.add).then_inc(row_sum, 1)
                dve.wait_ge(row_sum, ONE + b * 4 + (n + 1))
                dve.reciprocal(stat[:, 1, st], stat[:, 2, st]).then_inc(weight_ready, 1)
                dve.wait_ge(weight_ready, ONE + b * 8 + (2 * n + 1))
                dve.tensor_scalar(stat[:, 1, st], stat[:, 1, st], gain[:, 2 * j + e:2 * j + e + 1], None, ALU.mult).then_inc(weight_ready, 1)

            def turn(n):
                j, e = TILE_ORDER[n]
                dve.wait_ge(probs, ONE + b * 4 + (n + 1))
                dve.transpose(PT[:, tile_of(j, e), :], sm[:, tile_of(j, e), :]).then_inc(turned, 1)

            for n in range(2, NP):
                take_projection(b, n)
                if n == 13:
                    row_maxima(0)
                if n == 15:
                    row_maxima(1)
            row_weights(0)
            row_weights(1)
            row_maxima(2)
            row_maxima(3)
            turn(0)
            turn(1)
            row_weights(2)
            row_weights(3)
            turn(2)
            turn(3)

            den = lambda bank, n: bank[:, 0:n * MW].rearrange("p (a n) -> p a n", a=n)[:, :, ID]
            num = lambda bank, n: bank[:, 0:n * MW].rearrange("p (a n) -> p a n", a=n)[:, :, 0:ID]
            for t in range(SEGS):
                for j in range(2):
                    a = slice(2 * j, 2 * j + 2)
                    dve.wait_ge(recall_k, ONE + b * 32 + (2 * t + j + 1))
                    dve.wait_ge(prev_ready, ONE + b * 32 + 2 * t + j)
                    dve.reciprocal(small[:, a], den(s.bank(j), 2)).then_inc(k_inv, 1)
                    dve.wait_ge(k_inv, ONE + b * 32 + (2 * t + j + 1))
                    dve.wait_ge(d_pool, ONE + b * DS + 4 * t)
                    dve.wait_ge(d_dve, ONE + b * DS + 4 * t)
                    dve.tensor_tensor(prev[:, a, :], num(s.bank(j), 2),
                                      small[:, a].unsqueeze(2).to_broadcast([P, 2, ID]), ALU.mult).then_inc(prev_ready, 1)
                    if t + 1 < SEGS:
                        dve.wait_ge(prev_ready, ONE + b * 32 + (2 * t + j + 1))
                        dve.wait_ge(v_kept, ONE + b * 8 + 8)
                        dve.wait_ge(updated, ONE + b * (2 * SEGS) + (2 * t + j + 1))
                        for g in (0, 1):
                            dve.tensor_tensor(D[part(g), a, g, 0:ID], v[part(g), t, P * j:P * j + P].rearrange("p (e d) -> p e d", e=2),
                                              prev[part(g), a, :], ALU.subtract).then_inc(d_dve, 1)
                if opens and t == SEGS - 1:
                    open_batch(b + 1)
                dve.wait_ge(recall_q, ONE + b * 32 + (2 * t + 2))
                dve.wait_ge(q_out, ONE + b * SEGS + t)
                dve.tensor_scalar(small[:, 4:8], den(s.bank(7), 4), 1e-6, None, ALU.add).then_inc(q_den, 1)
                dve.wait_ge(q_den, ONE + b * (3 * SEGS) + (3 * t + 1))
                dve.reciprocal(small[:, 8:12], small[:, 4:8]).then_inc(q_den, 1)
                dve.wait_ge(q_den, ONE + b * (3 * SEGS) + (3 * t + 2))
                dve.tensor_tensor(small[:, 12:16], small[:, 8:12], beta, ALU.mult).then_inc(q_den, 1)
                dve.wait_ge(q_den, ONE + b * (3 * SEGS) + (3 * t + 3))
                dve.wait_ge(o_ready, ONE + b * SEGS + t)
                dve.tensor_tensor(mo, num(s.bank(7), 4), small[:, 12:16].unsqueeze(2).to_broadcast([P, 4, ID]), ALU.mult).then_inc(q_out, 1)
                dve.wait_ge(q_out, ONE + b * SEGS + (t + 1))
                dve.wait_ge(pv_ready, ONE + b * (G * SEGS) + (G * t + G))
                dve.wait_ge(ot_ready, ONE + b * SEGS + max(0, t - 1))
                dve.tensor_tensor(o[:, t % 2, :], s.bank(4)[:, 0:256], mo.rearrange("p n d -> p (n d)"), ALU.add).then_inc(o_ready, 1)
            if opens:
                take_projection(b + 1, 0)
                take_projection(b + 1, 1)
            dve.wait_ge(out_ready, ONE + b + 1)
            dve.tensor_tensor(s.x[:, batch(b)], s.x[:, batch(b)], s.bank(7), ALU.add).then_inc(x_added, 1)

        open_batch(0)
        take_projection(0, 0)
        take_projection(0, 1)
        with dve.Fori(0, B - 1) as b:
            batch_of_segments(b, True)
        batch_of_segments(B - 1, False)
        dve.wait_ge(x_added, ONE + B)
    return counters



E, MC = 8, 4
B1, B2 = 2 * MC * P, 2 * MC * P + MC
EXPERT = B2 + 2
TOK = N // P
R = 256
MOST = N // R
TILES_MOE = N // R + E


def moe_layer(nc, s, ctx, done, tag):
    counters = []

    def sem(name):
        counters.append(nc.alloc_semaphore(name=f"{tag}_{name}"))
        return counters[-1]

    weights_in, step, exped, logits_ready = sem("weights_in"), sem("step"), sem("exped"), sem("logits_ready")
    chosen_b_ready, ranked, constants = sem("chosen_b_ready"), sem("ranked"), sem("constants")
    tokens_turned, tokens_scaled, rows_ready = sem("tokens_turned"), sem("tokens_scaled"), sem("rows_ready")
    tiles_known, out_free = sem("tiles_known"), sem("out_free")
    loaded = (sem("loaded0"), sem("loaded1"))
    turned, xt_ready, staged, up_ready = sem("turned"), sem("xt_ready"), sem("staged"), sem("up_ready")
    h_act, h_dve, yt_ready, back_ready, y_ready = sem("h_act"), sem("h_dve"), sem("yt_ready"), sem("back_ready"), sem("y_ready")
    result_turned, x_added = sem("result_turned"), sem("x_added")
    down_ready = sem("down_ready")

    at = [0]

    def f32(n):
        a = at[0]
        at[0] += n
        return s.work[:, a:a + n]

    experts = f32(E * EXPERT)
    own = f32(2 * EXPERT).rearrange("p (n c) -> p n c", n=2)
    tile_in = f32(2 * R).rearrange("p (n r) -> p n r", n=2)
    xt = f32(2 * R).rearrange("p (n r) -> p n r", n=2)
    h = f32(2 * MC * R).rearrange("p (n c r) -> p n c r", n=2, c=MC)
    yt = f32(2 * R).rearrange("p (n r) -> p n r", n=2)
    tile_out = f32(2 * R).rearrange("p (n r) -> p n r", n=2)
    by_token = s.rs
    tile_e = lambda a: a.rearrange("p (i e) -> p i e", e=E)
    score, t0, t1, first, chosen = (tile_e(f32(TOK * E)) for _ in range(5))
    chosen_b = f32(TOK * E // 2).bitcast(BF16)
    before_b, ones_b = f32(P // 2).bitcast(BF16), f32(P // 2).bitcast(BF16)
    restart, total, upto = f32(E * TOK), f32(E * TOK), f32(E * TOK)
    best, weight, row_f, row = f32(TOK), f32(TOK), f32(TOK), f32(TOK).bitcast(I32)
    ones_e, count, tiles, tiles_upto, first_row = f32(E), f32(E), f32(E), f32(E), f32(E)
    filled = f32(E * MOST)
    past = f32(TILES_MOE * E)
    owner_f, owner = f32(TILES_MOE), f32(TILES_MOE).bitcast(I32)
    assert at[0] <= s.work.shape[1]
    wide = lambda a: a.unsqueeze(2).to_broadcast([P, TOK, E])
    each = lambda a: a.unsqueeze(1).to_broadcast([P, TOK, E])
    ei = lambda a: a.rearrange("p (e i) -> p e i", e=E)
    logits = tile_e(s.bank(4)[:, 0:TOK * E])
    rank = tile_e(s.bank(4)[:, 0:TOK * E])
    totals = tile_e(s.bank(4)[:, TOK * E:2 * TOK * E])
    token_bank = lambda b: s.bank((0, 1, 2, 3, 5, 6, 7, 0)[b])
    start_counters(nc, counters + [down_ready, yt_ready])
    scattered, stored = sem("scattered"), (sem("stored0"), sem("stored1"))
    gathered = [sem(f"gathered{b}") for b in range(B)]
    block = ctx.enter_context(nc.Block())

    @block.sync
    def _(sp):
        sp.dma_start(experts, s.expert_w).then_inc(weights_in, 16)
        sp.wait_ge(weights_in, ONE + 16)
        sp.wait_ge(scattered, 16 * TOK)
        with sp.Fori(0, TILES_MOE // 2) as pair:
            t = pair * 2
            for u in range(2):
                sp.wait_ge(turned, ONE + t)
                sp.dma_start(tile_in[:, u, :].rearrange("p (m f) -> p m f", m=2),
                             s.moe_in[bass.ds(t * R + u * R, R), :].rearrange("(m p) f -> p m f", p=P)).then_inc(loaded[u], 16)

    @block.tensor
    def _(pe):
        norm_pe(pe, s, done)
        for i in range(TOK):
            if i % 4 == 0:
                pe.wait_ge(s.normed, ONE + done + i // 4 + 1)
            mm = pe.matmul(s.bank(4)[:, i * E:(i + 1) * E], s.xn[:, i * P:(i + 1) * P], s.gate_w, start=True, stop=True)
        mm.then_inc(logits_ready, 1)
        for b in range(B):
            if b == B - 1:
                pe.wait_ge(tokens_scaled, ONE + 1)
            if b == 6:
                pe.wait_ge(constants, ONE + 3)
                pe.wait_ge(chosen_b_ready, ONE + 1)
                pe.matmul(s.bank(4)[:, 0:TOK * E], before_b, chosen_b, start=True, stop=True)
                pe.matmul(s.bank(4)[:, TOK * E:2 * TOK * E], ones_b, chosen_b, start=True, stop=True).then_inc(ranked, 1)
            for n in range(4):
                i = 4 * b + n
                mm = pe.transpose(token_bank(b)[:, n * P:(n + 1) * P], s.xn[:, i * P:(i + 1) * P], s.ident)
            mm.then_inc(tokens_turned, 1)
        pe.wait_ge(tokens_scaled, ONE + B)
        with pe.Fori(0, TILES_MOE // 2) as pair:
            t = pair * 2
            for u in range(2):
                pe.wait_ge(loaded[u], ONE + pair * 16 + 16)
                pe.wait_ge(xt_ready, ONE + t)
                for m in range(2):
                    mm = pe.transpose(s.bank(u)[:, m * P:(m + 1) * P], tile_in[:, u, m * P:(m + 1) * P], s.ident)
                mm.then_inc(turned, 1)
            for u in range(2):
                pe.wait_ge(xt_ready, ONE + t + (u + 1))
                pe.wait_ge(staged, ONE + t + (u + 1))
                pe.wait_ge(h_act, ONE + t * 2)
                pe.wait_ge(h_dve, ONE + t * 2)
                for c in range(MC):
                    pe.matmul(s.bank(2 + 2 * u + c // 2)[:, c % 2 * R:(c % 2 + 1) * R], own[:, u, c * P:(c + 1) * P], xt[:, u, :],
                              start=True, stop=True).then_inc(up_ready, 1)
            for u in range(2):
                pe.wait_ge(y_ready, ONE + t)
                for c in range(MC):
                    pe.wait_ge(h_act if c < 2 else h_dve, ONE + t * 2 + (2 * u + 1 + c % 2))
                    mm = pe.matmul(s.bank(6 + u)[:, 0:R], own[:, u, (MC + c) * P:(MC + c + 1) * P], h[:, u, c, :],
                                   start=c == 0, stop=c == MC - 1)
                mm.then_inc(down_ready, 1)
            for u in range(2):
                pe.wait_ge(yt_ready, ONE + t + (u + 2))
                for m in range(2):
                    mm = pe.transpose(s.bank(6 + u)[:, R + m * P:R + (m + 1) * P], yt[:, u, m * P:(m + 1) * P], s.ident)
                mm.then_inc(back_ready, 1)
        for b in range(B):
            pe.wait_ge(gathered[b], 16 * 4)
            if b >= 6:
                pe.wait_ge(x_added, ONE + b - 5)
            for n in range(4):
                i = 4 * b + n
                mm = pe.transpose(s.bank(b % 6)[:, n * P:(n + 1) * P], by_token[:, i * P:(i + 1) * P], s.ident)
            mm.then_inc(result_turned, 1)

    @block.gpsimd
    def _(pool):
        pool.wait_ge(rows_ready, ONE + 1)
        pool.wait_ge(s.zero_rows, 16)
        for i in range(TOK):
            pool.wait_ge(tokens_scaled, ONE + i // 4 + 1)
            pool.indirect_dma_start(out=s.moe_in[:, :], out_offset=bass.IndirectOffsetOnAxis(ap=row[:, i:i + 1], axis=0),
                                    in_=by_token[:, i * P:(i + 1) * P], in_offset=None).then_inc(scattered, 16)
        with pool.Fori(0, TILES_MOE // 2) as pair:
            t = pair * 2
            for u in range(2):
                pool.wait_ge(y_ready, ONE + t + (u + 1))
                pool.dma_start(s.moe_out[bass.ds(t * R + u * R, R), :].rearrange("(m p) f -> p m f", p=P),
                               tile_out[:, u, :].rearrange("p (m f) -> p m f", m=2)).then_inc(stored[u], 16)
            for u in range(2):
                pool.wait_ge(stored[u], pair * 16 + 16)
                pool.sem_inc(out_free, 1)
        for u in range(2):
            pool.wait_ge(stored[u], TILES_MOE // 2 * 16)
        for i in range(TOK):
            pool.indirect_dma_start(out=by_token[:, i * P:(i + 1) * P], out_offset=None, in_=s.moe_out[:, :],
                                    in_offset=bass.IndirectOffsetOnAxis(ap=row[:, i:i + 1], axis=0)).then_inc(gathered[i // 4], 16)

    @block.scalar
    def _(act):
        norm_act(act, s, done)
        act.wait_ge(step, ONE + 3)
        act.activation(t0, t0, ACT.Exp).then_inc(exped, 1)
        with act.Fori(0, TILES_MOE // 2) as pair:
            t = pair * 2
            for u in range(2):
                act.wait_ge(down_ready, ONE + t + u)
                act.wait_ge(up_ready, ONE + t * MC + (u * MC + 2))
                for c in range(2):
                    act.activation(h[:, u, c, :], s.bank(2 + 2 * u)[:, c * R:(c + 1) * R], ACT.Relu,
                                   bias=own[:, u, B1 + c:B1 + c + 1]).then_inc(h_act, 1)
            for u in range(2):
                act.wait_ge(down_ready, ONE + t + (u + 2))
                act.wait_ge(back_ready, ONE + t)
                act.activation(yt[:, u, :], s.bank(6 + u)[:, 0:R], ACT.Identity, bias=own[:, u, B2:B2 + 1]).then_inc(yt_ready, 1)
            for u in range(2):
                act.wait_ge(back_ready, ONE + t + (u + 1))
                act.wait_ge(out_free, ONE + t)
                act.activation(tile_out[:, u, :], s.bank(6 + u)[:, R:2 * R], ACT.Copy).then_inc(y_ready, 1)

    @block.vector
    def _(dve):
        dve.tensor_copy(before_b, s.before).then_inc(constants, 1)
        dve.memset(ones_b, 1.0).then_inc(constants, 1)
        dve.memset(restart, 1.0).then_inc(constants, 1)
        dve.memset(ones_e, 1.0).then_inc(constants, 1)
        dve.wait_ge(constants, ONE + 4)
        dve.memset(ei(restart)[:, :, 0:1], 0.0).then_inc(constants, 1)
        norm_dve(dve, s, done)

        def after(n):
            dve.wait_ge(step, ONE + n)

        dve.wait_ge(logits_ready, ONE + 1)
        dve.tensor_tensor(score, logits, each(s.gate_b), ALU.add).then_inc(step, 1)
        after(1)
        dve.tensor_reduce(best, score, AX.X, ALU.max).then_inc(step, 1)
        after(2)
        dve.tensor_tensor(t0, score, wide(best), ALU.subtract).then_inc(step, 1)
        dve.wait_ge(exped, ONE + 1)
        after(3)
        dve.tensor_reduce(best, t0, AX.X, ALU.add).then_inc(step, 1)
        after(4)
        dve.reciprocal(best, best).then_inc(step, 1)
        after(5)
        dve.tensor_tensor(score, t0, wide(best), ALU.mult).then_inc(step, 1)
        n = 6
        for is_best, pool in ((first, score), (t1, t0)):
            if is_best is t1:
                after(n)
                dve.scalar_tensor_tensor(t0, first, -2.0, score, ALU.mult, ALU.add).then_inc(step, 1)
                n += 1
            after(n)
            dve.tensor_reduce(best, pool, AX.X, ALU.max).then_inc(step, 1)
            after(n + 1)
            dve.tensor_tensor(is_best, pool, wide(best), ALU.is_equal).then_inc(step, 1)
            after(n + 2)
            dve.tensor_tensor(is_best, is_best, each(s.low_first), ALU.mult).then_inc(step, 1)
            after(n + 3)
            dve.tensor_reduce(best, is_best, AX.X, ALU.max).then_inc(step, 1)
            after(n + 4)
            dve.tensor_tensor(is_best, is_best, wide(best), ALU.is_equal).then_inc(step, 1)
            n += 5
        after(n)
        dve.tensor_tensor(t1, t1, first, ALU.add).then_inc(step, 1)
        after(n + 1)
        dve.scalar_tensor_tensor(t1, score, 0.0, t1, ALU.is_gt, ALU.mult).then_inc(step, 1)
        after(n + 2)
        dve.tensor_tensor(t1, t1, each(s.high_first), ALU.mult).then_inc(step, 1)
        after(n + 3)
        dve.tensor_reduce(best, t1, AX.X, ALU.max).then_inc(step, 1)
        after(n + 4)
        dve.tensor_tensor(chosen, t1, wide(best), ALU.is_equal).then_inc(step, 1)

        after(n + 5)
        dve.tensor_copy(chosen_b, chosen.rearrange("p i e -> p (i e)")).then_inc(chosen_b_ready, 1)
        dve.tensor_tensor(t0, chosen, score, ALU.mult).then_inc(step, 1)
        after(n + 6)
        dve.tensor_reduce(weight, t0, AX.X, ALU.add).then_inc(step, 1)
        after(n + 7)
        for b in range(B):
            if b == 4:
                dve.wait_ge(ranked, ONE + 1)
                dve.wait_ge(constants, ONE + 5)
                dve.tensor_copy(ei(total).rearrange("p e i -> p i e"), totals).then_inc(step, 1)
                after(n + 8)
                dve.tensor_tensor_scan(upto, restart, total, 0.0, ALU.mult, ALU.add).then_inc(step, 1)
                after(n + 9)
                dve.tensor_scalar(count, ei(upto)[:, :, TOK - 1], 1.0 / R, None, ALU.mult).then_inc(step, 1)
                after(n + 10)
                dve.tensor_tensor(filled.rearrange("p (e m) -> p e m", e=E), count.unsqueeze(2).to_broadcast([P, E, MOST]),
                                  s.ramp[:, 0:MOST].unsqueeze(1).to_broadcast([P, E, MOST]), ALU.is_gt).then_inc(step, 1)
                after(n + 11)
                dve.tensor_reduce(tiles, filled.rearrange("p (e m) -> p e m", e=E), AX.X, ALU.add).then_inc(step, 1)
                after(n + 12)
                dve.tensor_tensor_scan(tiles_upto, ones_e, tiles, 0.0, ALU.mult, ALU.add).then_inc(step, 1)
                after(n + 13)
                dve.tensor_tensor(first_row, tiles_upto, tiles, ALU.subtract).then_inc(step, 1)
                dve.tensor_tensor(upto, upto, total, ALU.subtract).then_inc(step, 1)
                after(n + 15)
                dve.scalar_tensor_tensor(ei(upto), first_row.unsqueeze(2).to_broadcast([P, E, TOK]), float(R), ei(upto),
                                         ALU.mult, ALU.add).then_inc(step, 1)
                after(n + 16)
                dve.tensor_tensor(t0, rank, ei(upto).rearrange("p e i -> p i e"), ALU.add).then_inc(step, 1)
                after(n + 17)
                dve.tensor_tensor(t0, t0, chosen, ALU.mult).then_inc(step, 1)
                after(n + 18)
                dve.tensor_reduce(row_f, t0, AX.X, ALU.add).then_inc(step, 1)
                after(n + 19)
                dve.tensor_copy(row, row_f).then_inc(rows_ready, 1)
            dve.wait_ge(tokens_turned, ONE + b + 1)
            dve.tensor_tensor(by_token[:, batch(b)].rearrange("p (n f) -> p n f", n=4),
                              token_bank(b).rearrange("p (n f) -> p n f", n=4),
                              weight[:, 4 * b:4 * b + 4].unsqueeze(2).to_broadcast([P, 4, P]), ALU.mult).then_inc(tokens_scaled, 1)
        dve.tensor_tensor(past.rearrange("p (t e) -> p t e", e=E), s.ramp.unsqueeze(2).to_broadcast([P, TILES_MOE, E]),
                          tiles_upto.unsqueeze(1).to_broadcast([P, TILES_MOE, E]), ALU.is_ge).then_inc(step, 1)
        after(n + 20)
        dve.tensor_reduce(owner_f, past.rearrange("p (t e) -> p t e", e=E), AX.X, ALU.add).then_inc(step, 1)
        after(n + 21)
        dve.tensor_scalar(owner, owner_f, E - 1.0, float(EXPERT), ALU.min, ALU.mult).then_inc(tiles_known, 1)
        dve.wait_ge(tiles_known, ONE + 1)
        dve.wait_ge(weights_in, ONE + 16)
        with dve.Fori(0, TILES_MOE // 2) as pair:
            t = pair * 2
            for u in range(2):
                expert = dve.value_load(owner[0:1, bass.ds(t + u, 1)], min_val=0, max_val=(E - 1) * EXPERT)
                dve.wait_ge(down_ready, ONE + t + u)
                dve.wait_ge(yt_ready, ONE + t + u)
                dve.tensor_copy(own[:, u, :], experts[:, bass.ds(expert, EXPERT)]).then_inc(staged, 1)
            for u in range(2):
                dve.wait_ge(turned, ONE + t + (u + 1))
                dve.wait_ge(up_ready, ONE + t * MC)
                dve.tensor_copy(xt[:, u, :], s.bank(u)[:, 0:R]).then_inc(xt_ready, 1)
            for u in range(2):
                dve.wait_ge(staged, ONE + t + (u + 1))
                dve.wait_ge(up_ready, ONE + t * MC + (u * MC + 4))
                for c in range(2, MC):
                    dve.tensor_scalar(h[:, u, c, :], s.bank(3 + 2 * u)[:, c % 2 * R:(c % 2 + 1) * R],
                                      own[:, u, B1 + c:B1 + c + 1], 0.0, ALU.add, ALU.max).then_inc(h_dve, 1)
        for b in range(B):
            dve.wait_ge(result_turned, ONE + b + 1)
            dve.tensor_tensor(s.x[:, batch(b)], s.x[:, batch(b)], s.bank(b % 6), ALU.add).then_inc(x_added, 1)
        dve.wait_ge(x_added, ONE + B)
    return counters



def _columns(sizes):
    at, out = 0, {}
    for name, n in sizes:
        out[name] = (at, at + n)
        at += n
    return out, at


WEIGHTS, WEIGHT_COLS = _columns(
    [("avg", P), ("ident", P), ("slopes", 16), ("key_rows", T)]
    + [("w_qkv", 3 * CH * P), ("w_out", CH * P), ("ln_g", 1), ("ln_b", 1), ("mem_beta", 4)]
    + [("rope_cos", T), ("rope_sin", T), ("causal", SEG)]
    + [("Wq", P), ("Wk", P), ("Wv", 32), ("Wo", P)]
    + [(name, P) for name in ("W_in", "W_B", "W_D", "W_out", "C_mat")] + [(name, 16) for name in ("W_ig", "W_fg", "B_mat")]
    + [(name, 1) for name in ("b_in", "b_B", "b_D", "b_out", "b_ig", "b_fg", "gamma", "beta")]
    + [(name, P) for name in ("W_key", "W_value", "W_receptance", "W_output")]
    + [(name, 1) for name in ("time_decay", "time_first", "mix_k", "mix_v", "mix_r")]
    + [("gate_w", E), ("gate_b", E), ("low_first", E), ("high_first", E), ("before", P), ("ramp", TILES_MOE)]
)
INTS, INT_COLS = _columns([("wgate", HID), ("wup", HID), ("wdown", HID)])


class Shared:
    pass


GQA_BF16_COLS = (HEADS + KV) * 3 * P + P


def build(nc, x_in, weights, ints, gqa_tables, expert_w, out, layers):
    with ExitStack() as ctx:
        def sb(name, shape, dt=F32):
            return ctx.enter_context(nc.sbuf_tensor(name, shape, dt))

        def sem(name):
            return ctx.enter_context(nc.semaphore("norm_" + name))

        w = sb("w", [P, WEIGHT_COLS])
        wf = sb("wf", [P, INT_COLS])
        weight = lambda name: w[:, WEIGHTS[name][0]:WEIGHTS[name][1]]
        integer = lambda name: wf[:, INTS[name][0]:INTS[name][1]]
        s = Shared()
        s.avg, s.ident, s.slopes, s.key_rows = weight("avg"), weight("ident"), weight("slopes"), weight("key_rows")
        s.w_qkv, s.w_out, s.ln_g, s.ln_b = weight("w_qkv"), weight("w_out"), weight("ln_g"), weight("ln_b")
        s.mem_beta, s.rope_cos, s.rope_sin, s.causal = weight("mem_beta"), weight("rope_cos"), weight("rope_sin"), weight("causal")
        s.Wq, s.Wk, s.Wv, s.Wo = weight("Wq"), weight("Wk"), weight("Wv"), weight("Wo")
        s.W_in, s.W_B, s.W_D, s.W_out = weight("W_in"), weight("W_B"), weight("W_D"), weight("W_out")
        s.C_mat, s.W_ig, s.W_fg, s.B_mat = weight("C_mat"), weight("W_ig"), weight("W_fg"), weight("B_mat")
        s.b_in, s.b_B, s.b_D, s.b_out = weight("b_in"), weight("b_B"), weight("b_D"), weight("b_out")
        s.b_ig, s.b_fg, s.gamma, s.beta = weight("b_ig"), weight("b_fg"), weight("gamma"), weight("beta")
        s.W_key, s.W_value, s.W_receptance, s.W_output = weight("W_key"), weight("W_value"), weight("W_receptance"), weight("W_output")
        s.time_decay, s.time_first, s.mix_k, s.mix_v = weight("time_decay"), weight("time_first"), weight("mix_k"), weight("mix_v")
        s.mix_r, s.gate_w, s.gate_b = weight("mix_r"), weight("gate_w"), weight("gate_b")
        s.low_first, s.high_first, s.before, s.ramp = weight("low_first"), weight("high_first"), weight("before"), weight("ramp")
        s.wgate, s.wup, s.wdown = integer("wgate"), integer("wup"), integer("wdown")
        s.b_ig, s.b_fg = s.b_ig[0:16, :], s.b_fg[0:16, :]

        s.gqa_tables, s.expert_w = gqa_tables, expert_w
        s.x = sb("x", [P, N])
        s.xn = sb("xn", [P, N])
        s.rs = sb("rs", [P, N])
        s.sq = sb("sq", [P, 2, T])
        s.eps = sb("eps", [P, 1])
        s.scrap = sb("scrap", [P, 1])
        s.work = sb("work", [P, 25 * 1024])
        wi = s.work[:, s.work.shape[1] - INT_COLS:].bitcast(I32)
        s.psum = ctx.enter_context(nc.psum_tensor("psum", [P, 8, T], F32))
        s.bank = lambda i: s.psum[:, i, :]
        s.centered, s.squared, s.mean_ready = sem("centered"), sem("squared"), sem("mean_ready")
        s.var_ready, s.logged, s.rstd_ready = sem("var_ready"), sem("logged"), sem("rstd_ready")
        s.normed, s.warmed = sem("normed"), sem("warmed")
        norm_counters = (s.centered, s.squared, s.mean_ready, s.var_ready, s.logged, s.rstd_ready, s.normed, s.warmed)
        s.moe_in = nc.dram_tensor("moe_in", (TILES_MOE * R, P), F32, kind="Internal").ap()
        s.moe_out = nc.dram_tensor("moe_out", (TILES_MOE * R, P), F32, kind="Internal").ap()
        s.zero_rows = ctx.enter_context(nc.semaphore("zero_rows"))
        s.loaded = ctx.enter_context(nc.semaphore("loaded"))
        s.rest_loaded = ctx.enter_context(nc.semaphore("rest_loaded"))
        cleared = ctx.enter_context(nc.semaphore("cleared"))
        consts = ctx.enter_context(nc.semaphore("consts"))
        s.stored = ctx.enter_context(nc.semaphore("stored"))

        start_counters(nc, norm_counters)
        with nc.Block() as block:
            @block.sync
            def _(sp):
                sp.dma_start(w[:, 0:P], weights[:, 0:P]).then_inc(s.loaded, 16)
                sp.dma_start(s.x[:, :], x_in).then_inc(s.loaded, 16)
                sp.wait_ge(s.loaded, 32)

            @block.vector
            def _(dve):
                dve.memset(s.eps[:, :], 1e-5).then_inc(consts, 1)
                dve.wait_ge(consts, 1)

        def load_rest(sp):
            sp.dma_start(w[:, P:], weights[:, P:]).then_inc(s.rest_loaded, 16)
            sp.dma_start(wi, ints).then_inc(s.rest_loaded, 16)

        def clear_rows(pool):
            pool.memset(s.sq[:, :, :], 0.0).then_inc(cleared, 1)
            pool.wait_ge(cleared, 1)
            zeros = s.sq[:, :, :].rearrange("p n (m f) -> p (n m) f", f=P)
            for a in range(0, TILES_MOE * R // P, zeros.shape[1]):
                pool.dma_start(s.moe_in[a * P:(a + zeros.shape[1]) * P, :].rearrange("(m p) f -> p m f", p=P),
                               zeros).then_inc(s.zero_rows, 16)

        def rest_there(eng):
            eng.wait_ge(s.rest_loaded, 32)

        def dequantise(dve):
            dve.tensor_scalar(wf[:, :], wi, float(np.float32(1.0 / 127.0)), None, ALU.mult).then_inc(consts, 1)
            dve.wait_ge(consts, 2)

        s.load_rest, s.clear_rows, s.rest_there, s.dequantise = load_rest, clear_rows, rest_there, dequantise
        s.out = out
        done = 0
        for n, kind in enumerate(layers):
            s.last = n == len(layers) - 1
            with ExitStack() as own:
                counters = LAYERS[kind](nc, s, own, done, f"l{n}")
            nc.all_engine_barrier()
            nc.clear_and_free_semaphores(counters)
            nc.all_engine_barrier()
            done += 2 * B if kind == "infini" else B


LAYERS = {"swiglu": swiglu_layer, "ssm": ssm_layer, "rwkv": rwkv_layer, "gqa": gqa_layer, "infini": infini_layer,
          "moe": moe_layer}



def gqa_constants():
    bf = np.dtype("bfloat16")
    start = 2.0 ** (-2.0 ** (-(math.log2(HEADS) - 3)))
    slope = np.array([start * start ** i for i in range(HEADS)], dtype=np.float32)
    slopes, rows = np.zeros((P, HEADS), np.float32), np.zeros((P, T), np.float32)
    position = np.arange(T)
    left = slope
    for i in range(3):
        part = left.astype(bf).astype(np.float32)
        left = left - part
        for j, pos in enumerate((position // 256 * 256, position % 256)):
            slopes[BIAS_ROW + 2 * i + j] = part
            rows[BIAS_ROW + 2 * i + j] = pos
    rows[MAX_ROW:MAX_ROW + 3] = 1
    tables = np.zeros((P, GQA_BF16_COLS), bf)
    for side, heads, at in ((0, HEADS, 0), (1, KV, HEADS * 3 * P)):
        for h in range(heads):
            for n, pair in enumerate(SLOTS):
                for d in range(HD):
                    tables[h * HD + d, at + (h * 3 + pair[side]) * P + n * HD + d] = 1
    tables[:, (HEADS + KV) * 3 * P:] = np.eye(P)
    return slopes, rows, tables


def infini_constants():
    freqs = np.float32(10000.0) ** (-np.arange(0, ID, 2, dtype=np.float32) / np.float32(ID))
    angle = (np.arange(T, dtype=np.float32)[:, None] * freqs).astype(np.float32)
    feature = np.arange(P) % ID
    cos = np.cos(angle)[:, feature // 2].T
    sin = np.sin(angle)[:, feature // 2].T * np.where(feature % 2, 1.0, -1.0).astype(np.float32)[:, None]
    row, column = np.arange(P) % SEG, np.arange(SEG)
    causal = np.where(column[None, :] <= row[:, None], np.float32(0), np.float32(-1e30))
    return cos.astype(np.float32), sin.astype(np.float32), causal.astype(np.float32)


def lay_out(i):
    f = lambda name: np.asarray(i[name])
    x = np.ascontiguousarray(f("L0_attn_a_x").reshape(N, P).T)
    avg = np.full((P, P), 1.0 / P, np.float32)
    col = lambda a: np.concatenate([a.reshape(-1, 1), np.zeros((P - a.size, 1), a.dtype)])
    rows = lambda a: np.concatenate([a, np.zeros((P - a.shape[0], a.shape[1]), a.dtype)])
    parts = {"avg": avg, "ident": np.eye(P, dtype=np.float32)}
    parts["slopes"], parts["key_rows"], gqa_tables = gqa_constants()
    parts["w_qkv"] = f("L0_attn_b_w_qkv")
    parts["w_out"] = f("L0_attn_b_w_out").reshape(CH, P, P).transpose(1, 0, 2).reshape(P, CH * P)
    parts["ln_g"], parts["ln_b"] = col(f("L0_attn_b_ln_g")), col(f("L0_attn_b_ln_b"))
    gate = f("L0_attn_b_mem_beta").reshape(2, G, 2).transpose(1, 0, 2).reshape(G, 1, 4)
    parts["mem_beta"] = np.broadcast_to(gate, (G, 32, 4)).reshape(P, 4)
    parts["rope_cos"], parts["rope_sin"], parts["causal"] = infini_constants()
    for name in ("Wq", "Wv", "Wo"):
        parts[name] = f("L0_attn_a_" + name)
    parts["Wk"] = np.concatenate([f("L0_attn_a_Wk"), np.zeros((P, P - KV * HD), np.float32)], axis=1)
    for name in ("W_in", "W_B", "W_D", "W_out", "W_ig", "W_fg", "B_mat"):
        parts[name] = f("L1_attn_a_" + name)
    parts["C_mat"] = rows(f("L1_attn_a_C_mat"))
    for name in ("b_in", "b_B", "b_D", "b_out", "b_ig", "b_fg", "gamma", "beta"):
        parts[name] = col(f("L1_attn_a_" + name))
    for name in ("W_key", "W_value", "W_receptance", "W_output"):
        parts[name] = f("L1_attn_b_" + name).T
    for name in ("time_decay", "time_first"):
        parts[name] = col(f("L1_attn_b_" + name))
    for name in "kvr":
        parts["mix_" + name] = col(f("L1_attn_b_time_mix_" + name))
    everywhere = lambda a: np.broadcast_to(a.reshape(1, -1), (P, a.size))
    parts["gate_w"], parts["gate_b"] = f("L0_ffn_gate_w"), everywhere(f("L0_ffn_gate_b"))
    index = np.arange(E, dtype=np.float32)
    parts["low_first"], parts["high_first"] = everywhere(E - index), everywhere(index + 1)
    parts["before"] = np.triu(np.ones((P, P), np.float32), 1)
    parts["ramp"] = everywhere(np.arange(TILES_MOE, dtype=np.float32))
    weights = np.concatenate([parts[name] for name in WEIGHTS], axis=1)
    wd = f("L1_ffn_w_down")
    ints = np.concatenate([
        f("L1_ffn_w_gate").T, f("L1_ffn_w_up").T,
        wd.T.reshape(HC, P, P).transpose(1, 0, 2).reshape(P, HID)], axis=1)
    up = f("L0_ffn_w1").transpose(1, 0, 2)
    down = f("L0_ffn_w2").reshape(E, MC, P, P).transpose(2, 0, 1, 3).reshape(P, E, MC * P)
    b1, b2 = f("L0_ffn_b1").reshape(E, MC, P).transpose(2, 0, 1), f("L0_ffn_b2").T.reshape(P, E, 1)
    pad = np.zeros((P, E, EXPERT - B2 - 1), np.float32)
    expert_w = np.ascontiguousarray(np.concatenate([up, down, b1, b2, pad], axis=2).reshape(P, E * EXPERT))
    return {"x_in": x, "weights": np.ascontiguousarray(weights), "ints": np.ascontiguousarray(ints),
            "gqa_tables": gqa_tables, "expert_w": expert_w}


MODEL = ["gqa", "moe", "infini", "moe", "ssm", "swiglu", "rwkv", "swiglu"]


def kernel(**inputs):
    import concourse.bacc as bacc
    from concourse.bass_utils import run_bass_kernel_spmd

    arrays = lay_out(inputs)
    nc = bacc.Bacc("TRN2", target_bir_lowering=False, num_devices=1)
    args = [nc.dram_tensor(name, a.shape, mybir.dt.from_np(a.dtype), kind="ExternalInput").ap()
            for name, a in arrays.items()]
    out = nc.dram_tensor("out", (P, N), F32, kind="ExternalOutput").ap()
    build(nc, *args, out, MODEL)
    results = run_bass_kernel_spmd(nc, [arrays], core_ids=[0]).results
    return np.ascontiguousarray(results[0]["out"].T).reshape(B, T, P)
```
